# Optimizing a Trainium2 kernel written in Bass

```python
import numpy as np
import jax
import jax.numpy as jnp

def _softmax(x, axis=-1):
    return jax.nn.softmax(x, axis=axis)

def _gelu(x):
    return jax.nn.gelu(x, approximate=True)

def _silu(x):
    return jax.nn.silu(x)

def _sigmoid(x):
    return jax.nn.sigmoid(x)

def _layernorm(x, axis=-1, eps=1e-05):
    m = jnp.mean(x, axis=axis, keepdims=True)
    v = jnp.var(x, axis=axis, keepdims=True)
    return (x - m) / jnp.sqrt(v + eps)

def _scatter_add(tgt, idx, src, axis=0):
    return tgt.at[idx].add(src)

def _segment_sum(src, seg, n):
    return jax.ops.segment_sum(src, seg, n)
kernel_name = 'mk_gnn_resnorm_d4_gnn_r32_648a57'

def setup_inputs(seed: int=0):
    np.random.seed(seed)
    _w = jnp.asarray

    def _rec_inputs():
        import jax
        import jax.numpy as jnp
        _gk = jax.random.key(seed)
        x = -0.000202 + 1 * jax.random.normal(jax.random.fold_in(_gk, 1), (3125, 128), jnp.float32)
        src = jax.random.randint(jax.random.fold_in(_gk, 2), (50000,), 0, 3125, jnp.int32)
        dst = jax.random.randint(jax.random.fold_in(_gk, 3), (50000,), 0, 3125, jnp.int32)
        _o = jnp.argsort(dst, stable=True)
        src = src[_o]
        dst = dst[_o]
        edge_attr_128 = -2.25437e-05 + 0.999858 * jax.random.normal(jax.random.fold_in(_gk, 12), (50000, 128), jnp.float32)
        return (x, src, dst, edge_attr_128)
    x, src, dst, edge_attr_128 = _rec_inputs()

    def _L0_gnn_setup():
        import jax, jax.numpy as jnp
        import numpy as np
        LN_EPS = 1e-05
        key = jax.random.key(seed)
        k = jax.random.split(key, 6)
        n_nodes, n_edges, d = (50000, 25000, 128)
        x = jax.random.normal(k[0], (n_nodes, d), dtype=jnp.float32)
        src = jax.random.randint(k[1], (n_edges,), 0, n_nodes, dtype=jnp.int32)
        dst = jax.random.randint(k[2], (n_edges,), 0, n_nodes, dtype=jnp.int32)
        W = jax.random.normal(k[3], (d, d), dtype=jnp.float32) * (1.0 / np.sqrt(d))
        b = jnp.zeros((d,), dtype=jnp.float32)
        gamma = jnp.ones((d,), dtype=jnp.float32)
        beta = jnp.zeros((d,), dtype=jnp.float32)
        return {'x': x, 'src': src, 'dst': dst, 'W': W, 'b': b, 'gamma': gamma, 'beta': beta}
    _L0_gnn_all = _L0_gnn_setup()
    _L0_gnn_in = {k: v for k, v in _L0_gnn_all.items() if k in ('W', 'b', 'gamma', 'beta')}
    del _L0_gnn_all

    def _L1_gnn_setup():
        import jax, jax.numpy as jnp
        import numpy as np
        N_NODES = 50000
        N_EDGES = 15625
        D = 128
        RRELU_SLOPE = (1.0 / 8.0 + 1.0 / 3.0) / 2.0

        def _leaky(x):
            return jnp.where(x >= 0, x, x * RRELU_SLOPE)

        def _layer(h, e, src, dst, W1, W2, W3):
            n = h.shape[0]
            msg = (h[src] + e) @ W1.T
            deg = jax.ops.segment_sum(jnp.ones(src.shape[0], h.dtype), dst, num_segments=n)
            agg = jax.ops.segment_sum(msg, dst, num_segments=n)
            neigh = agg / jnp.maximum(deg, 1.0)[:, None]
            iso = (deg == 0)[:, None]
            self_msg = jnp.where(iso, h @ W3.T, h @ W2.T)
            return _leaky(neigh + self_msg)
        key = jax.random.key(seed)
        ks = jax.random.split(key, 10)
        inp = {'node_feats': jax.random.normal(ks[0], (N_NODES, D), dtype=jnp.float32), 'edge_feats': jax.random.normal(ks[1], (N_EDGES, D), dtype=jnp.float32), 'src': jax.random.randint(ks[2], (N_EDGES,), 0, N_NODES, dtype=jnp.int32), 'dst': jax.random.randint(ks[3], (N_EDGES,), 0, N_NODES, dtype=jnp.int32)}
        scale = 1.0 / np.sqrt(D)
        for i, name in enumerate(['W1_0', 'W2_0', 'W3_0', 'W1_1', 'W2_1', 'W3_1']):
            inp[name] = jax.random.uniform(ks[4 + i], (D, D), dtype=jnp.float32, minval=-scale, maxval=scale)
        return inp
    _L1_gnn_all = _L1_gnn_setup()
    _L1_gnn_in = {k: v for k, v in _L1_gnn_all.items() if k in ('W1_0', 'W2_0', 'W3_0', 'W1_1', 'W2_1', 'W3_1')}
    del _L1_gnn_all

    def _L2_gnn_setup():
        import jax, jax.numpy as jnp
        import numpy as np
        N_NODES = 50000
        N_EDGES = 25000
        D_IN = 128
        D_OUT = 128
        key = jax.random.key(seed)
        k1, k2, k3, k4, k5, k6 = jax.random.split(key, 6)
        feat = jax.random.normal(k1, (N_NODES, D_IN), dtype=jnp.float32)
        src = jax.random.randint(k2, (N_EDGES,), 0, N_NODES, dtype=jnp.int64)
        dst = jax.random.randint(k3, (N_EDGES,), 0, N_NODES, dtype=jnp.int64)
        scale = 1.0 / np.sqrt(D_IN)
        W_neigh = jax.random.normal(k4, (D_OUT, D_IN), dtype=jnp.float32) * scale
        W_self = jax.random.normal(k5, (D_OUT, D_IN), dtype=jnp.float32) * scale
        b_self = jax.random.normal(k6, (D_OUT,), dtype=jnp.float32) * scale
        return {'feat': feat, 'src': src, 'dst': dst, 'W_neigh': W_neigh, 'W_self': W_self, 'b_self': b_self}
    _L2_gnn_all = _L2_gnn_setup()
    _L2_gnn_in = {k: v for k, v in _L2_gnn_all.items() if k in ('W_neigh', 'W_self', 'b_self')}
    del _L2_gnn_all

    def _L3_gnn_setup():
        import jax, jax.numpy as jnp
        import numpy as np
        N, E, F, H, L = (50000, 18750, 128, 128, 5)
        key = jax.random.key(seed)
        ks = jax.random.split(key, 16)
        s = 1.0 / np.sqrt(H)
        u = lambda k, shape: jax.random.uniform(k, shape, jnp.float32, -s, s)
        return {'x': jax.random.normal(ks[0], (N, F), jnp.float32), 'edge_index': jax.random.randint(ks[1], (2, E), 0, N, jnp.int64), 'enc_w1': u(ks[2], (H, F)), 'enc_b1': u(ks[3], (H,)), 'enc_w2': u(ks[4], (H, H)), 'enc_b2': u(ks[5], (H,)), 'conv_w': u(ks[6], (L, H, H)), 'gru_wih': u(ks[7], (3 * H, H)), 'gru_whh': u(ks[8], (3 * H, H)), 'gru_bih': u(ks[9], (3 * H,)), 'gru_bhh': u(ks[10], (3 * H,)), 'dec_w1': u(ks[11], (H, H)), 'dec_b1': u(ks[12], (H,)), 'dec_w2': u(ks[13], (F, H)), 'dec_b2': u(ks[14], (F,))}
    _L3_gnn_all = _L3_gnn_setup()
    _L3_gnn_in = {k: v for k, v in _L3_gnn_all.items() if k in ('enc_w1', 'enc_b1', 'enc_w2', 'enc_b2', 'conv_w', 'gru_wih', 'gru_whh', 'gru_bih', 'gru_bhh', 'dec_w1', 'dec_b1', 'dec_w2', 'dec_b2')}
    del _L3_gnn_all
    return {'x': x, 'src': src, 'dst': dst, 'edge_attr_128': edge_attr_128, 'L0_gnn_W': _L0_gnn_in['W'], 'L0_gnn_b': _L0_gnn_in['b'], 'L0_gnn_gamma': _L0_gnn_in['gamma'], 'L0_gnn_beta': _L0_gnn_in['beta'], 'L1_gnn_W1_0': _L1_gnn_in['W1_0'], 'L1_gnn_W2_0': _L1_gnn_in['W2_0'], 'L1_gnn_W3_0': _L1_gnn_in['W3_0'], 'L1_gnn_W1_1': _L1_gnn_in['W1_1'], 'L1_gnn_W2_1': _L1_gnn_in['W2_1'], 'L1_gnn_W3_1': _L1_gnn_in['W3_1'], 'L2_gnn_W_neigh': _L2_gnn_in['W_neigh'], 'L2_gnn_W_self': _L2_gnn_in['W_self'], 'L2_gnn_b_self': _L2_gnn_in['b_self'], 'L3_gnn_enc_w1': _L3_gnn_in['enc_w1'], 'L3_gnn_enc_b1': _L3_gnn_in['enc_b1'], 'L3_gnn_enc_w2': _L3_gnn_in['enc_w2'], 'L3_gnn_enc_b2': _L3_gnn_in['enc_b2'], 'L3_gnn_conv_w': _L3_gnn_in['conv_w'], 'L3_gnn_gru_wih': _L3_gnn_in['gru_wih'], 'L3_gnn_gru_whh': _L3_gnn_in['gru_whh'], 'L3_gnn_gru_bih': _L3_gnn_in['gru_bih'], 'L3_gnn_gru_bhh': _L3_gnn_in['gru_bhh'], 'L3_gnn_dec_w1': _L3_gnn_in['dec_w1'], 'L3_gnn_dec_b1': _L3_gnn_in['dec_b1'], 'L3_gnn_dec_w2': _L3_gnn_in['dec_w2'], 'L3_gnn_dec_b2': _L3_gnn_in['dec_b2']}

def reference(x, src, dst, edge_attr_128, L0_gnn_W, L0_gnn_b, L0_gnn_gamma, L0_gnn_beta, L1_gnn_W1_0, L1_gnn_W2_0, L1_gnn_W3_0, L1_gnn_W1_1, L1_gnn_W2_1, L1_gnn_W3_1, L2_gnn_W_neigh, L2_gnn_W_self, L2_gnn_b_self, L3_gnn_enc_w1, L3_gnn_enc_b1, L3_gnn_enc_w2, L3_gnn_enc_b2, L3_gnn_conv_w, L3_gnn_gru_wih, L3_gnn_gru_whh, L3_gnn_gru_bih, L3_gnn_gru_bhh, L3_gnn_dec_w1, L3_gnn_dec_b1, L3_gnn_dec_w2, L3_gnn_dec_b2):
    import jax
    import jax.numpy as jnp

    def _L0_gnn_ref(x, src, dst, W, b, gamma, beta):
        import jax, jax.numpy as jnp
        import numpy as np
        LN_EPS = 1e-05
        n_nodes = x.shape[0]
        h = x @ W
        agg = jax.ops.segment_sum(h[src], dst, num_segments=n_nodes)
        deg = jax.ops.segment_sum(jnp.ones_like(src, dtype=x.dtype), dst, num_segments=n_nodes)
        deg = jnp.clip(deg, 1.0)
        out = agg / deg[:, None] + b
        out = out + x
        mean = jnp.mean(out, axis=-1, keepdims=True)
        var = jnp.var(out, axis=-1, keepdims=True)
        ln = (out - mean) * jax.lax.rsqrt(var + LN_EPS) * gamma + beta
        return jax.nn.gelu(ln, approximate=False)

    def _L1_gnn_ref(node_feats, edge_feats, src, dst, W1_0, W2_0, W3_0, W1_1, W2_1, W3_1):
        import jax, jax.numpy as jnp
        import numpy as np
        N_NODES = 50000
        N_EDGES = 15625
        D = 128
        RRELU_SLOPE = (1.0 / 8.0 + 1.0 / 3.0) / 2.0

        def _leaky(x):
            return jnp.where(x >= 0, x, x * RRELU_SLOPE)

        def _layer(h, e, src, dst, W1, W2, W3):
            n = h.shape[0]
            msg = (h[src] + e) @ W1.T
            deg = jax.ops.segment_sum(jnp.ones(src.shape[0], h.dtype), dst, num_segments=n)
            agg = jax.ops.segment_sum(msg, dst, num_segments=n)
            neigh = agg / jnp.maximum(deg, 1.0)[:, None]
            iso = (deg == 0)[:, None]
            self_msg = jnp.where(iso, h @ W3.T, h @ W2.T)
            return _leaky(neigh + self_msg)
        h = _layer(node_feats, edge_feats, src, dst, W1_0, W2_0, W3_0)
        h = _layer(h, edge_feats, src, dst, W1_1, W2_1, W3_1)
        return h

    def _L2_gnn_ref(feat, src, dst, W_neigh, W_self, b_self):
        import jax, jax.numpy as jnp
        import numpy as np
        N_NODES = 50000
        N_EDGES = 25000
        D_IN = 128
        D_OUT = 128
        "SAGEConv with aggregator_type='mean', feat_drop=0, bias=True.\n\n            in_feats == out_feats (128) -> lin_before_mp is False:\n              h_neigh = fc_neigh(mean over incoming neighbors of feat)\n              out     = fc_self(feat) + h_neigh\n            "
        n = feat.shape[0]
        msgs = feat[src]
        summed = jax.ops.segment_sum(msgs, dst, num_segments=n)
        deg = jax.ops.segment_sum(jnp.ones((src.shape[0],), feat.dtype), dst, num_segments=n)
        h_neigh = summed / jnp.maximum(deg, 1.0)[:, None]
        h_neigh = h_neigh @ W_neigh.T
        h_self = feat @ W_self.T + b_self
        return h_self + h_neigh

    def _L3_gnn_ref(x, edge_index, enc_w1, enc_b1, enc_w2, enc_b2, conv_w, gru_wih, gru_whh, gru_bih, gru_bhh, dec_w1, dec_b1, dec_w2, dec_b2):
        import jax, jax.numpy as jnp
        import numpy as np
        N, E, F, H, L = (50000, 18750, 128, 128, 5)
        src, dst = (edge_index[0], edge_index[1])
        n_nodes = x.shape[0]
        h = jnp.maximum(x @ enc_w1.T + enc_b1, 0.0) @ enc_w2.T + enc_b2

        def step(h, w):
            m = h @ w
            agg = jax.ops.segment_sum(m[src], dst, num_segments=n_nodes)
            gi = agg @ gru_wih.T + gru_bih
            gh = h @ gru_whh.T + gru_bhh
            ir, iz, i_n = jnp.split(gi, 3, axis=1)
            hr, hz, h_n = jnp.split(gh, 3, axis=1)
            r = jax.nn.sigmoid(ir + hr)
            z = jax.nn.sigmoid(iz + hz)
            n = jnp.tanh(i_n + r * h_n)
            return ((1.0 - z) * n + z * h, None)
        h, _ = jax.lax.scan(step, h, conv_w)
        h = jnp.maximum(h, 0.0)
        out = jnp.maximum(h @ dec_w1.T + dec_b1, 0.0) @ dec_w2.T + dec_b2
        return jax.nn.sigmoid(out)
    edge_index = jnp.stack([src, dst])
    x = _layernorm(x + _L0_gnn_ref(x, src, dst, L0_gnn_W, L0_gnn_b, L0_gnn_gamma, L0_gnn_beta), axis=-1)
    x = _layernorm(x + _L1_gnn_ref(x, edge_attr_128, src, dst, L1_gnn_W1_0, L1_gnn_W2_0, L1_gnn_W3_0, L1_gnn_W1_1, L1_gnn_W2_1, L1_gnn_W3_1), axis=-1)
    x = _layernorm(x + _L2_gnn_ref(x, src, dst, L2_gnn_W_neigh, L2_gnn_W_self, L2_gnn_b_self), axis=-1)
    x = _layernorm(x + _L3_gnn_ref(x, edge_index, L3_gnn_enc_w1, L3_gnn_enc_b1, L3_gnn_enc_w2, L3_gnn_enc_b2, L3_gnn_conv_w, L3_gnn_gru_wih, L3_gnn_gru_whh, L3_gnn_gru_bih, L3_gnn_gru_bhh, L3_gnn_dec_w1, L3_gnn_dec_b1, L3_gnn_dec_w2, L3_gnn_dec_b2), axis=-1)
    return x

_drawn_inputs = setup_inputs


def setup_inputs(seed=0):
    import zlib

    import numpy as np

    out = dict(_drawn_inputs(seed))
    spreads = {'L0_gnn_b': (0.0, 0.1), 'L0_gnn_gamma': (1.0, 0.2), 'L0_gnn_beta': (0.0, 0.1)}
    factors = {'L3_gnn_enc_w1': 4.225,
     'L3_gnn_enc_b1': 17.017,
     'L3_gnn_enc_w2': 2.965,
     'L3_gnn_enc_b2': 3.686,
     'L3_gnn_conv_w': 2.715,
     'L3_gnn_gru_wih': 3.102,
     'L3_gnn_gru_whh': 23.663,
     'L3_gnn_gru_bih': 151.017,
     'L3_gnn_gru_bhh': 179.867,
     'L3_gnn_dec_b1': 8.0,
     'L3_gnn_dec_b2': 4.462}
    for name, (base, spread) in spreads.items():
        noise = np.random.default_rng([zlib.crc32(name.encode()), seed]).standard_normal(out[name].shape)
        drawn = base * np.exp(spread * noise) if base else spread * noise
        out[name] = jnp.asarray(drawn.astype(out[name].dtype))
    for name, factor in factors.items():
        out[name] = (out[name] * factor).astype(out[name].dtype)
    return out
```

```python
from contextlib import ExitStack

import concourse.bass as bass
from concourse import mybir

F32 = mybir.dt.float32
F16 = mybir.dt.float16
BF16 = mybir.dt.bfloat16
I32 = mybir.dt.int32
ALU = mybir.AluOpType
ACT = mybir.ActivationFunctionType
AX_X = mybir.AxisListType.X

N, D, E = 3125, 128, 50000
B = 125
T = N // B
ET = E // B
TQ = 4
TP = ET // TQ
W = 25
NW = N // W
WPJ = B // W
KA = 5
KE = 20
EQ = KE // 5
MW = T * W
C0 = 13
NC = 8
CW = 391
NPAD = NC * CW
NPAIR = NC // 2
MG = (T + 3) // 4
BIG = 512.0
MAGIC = 12582912.0
LEAK = (1.0 / 8.0 + 1.0 / 3.0) / 2.0
EPS = 1e-5
STEPS = 5

WT = ["L1_gnn_W1_0", "L1_gnn_W2_0", "L1_gnn_W3_0", "L1_gnn_W1_1", "L1_gnn_W2_1", "L1_gnn_W3_1",
      "L2_gnn_W_neigh", "L2_gnn_W_self", "L3_gnn_enc_w1", "L3_gnn_enc_w2",
      "L3_gnn_gru_wih", "L3_gnn_gru_whh", "L3_gnn_dec_w1", "L3_gnn_dec_w2"]
WROWS = {"L3_gnn_gru_wih": 3, "L3_gnn_gru_whh": 3}
VECS = ["L0_gnn_b", "L0_gnn_gamma", "L0_gnn_beta", "L2_gnn_b_self", "L3_gnn_enc_b1", "L3_gnn_enc_b2",
        "L3_gnn_gru_bih", "L3_gnn_gru_bhh", "L3_gnn_dec_b1", "L3_gnn_dec_b2"]


def gnn_kernel(nc, ins, out):
    a = ins
    ctx = ExitStack()
    with ctx:
        def sb(name, shape, dt, stack=ctx):
            return stack.enter_context(nc.sbuf_tensor(name, shape, dt))

        def sem(name):
            return ctx.enter_context(nc.semaphore(name))

        adj = sb("adj", [B, T, NPAD], F16)
        nW = sum(WROWS.get(n, 1) for n in WT)
        wT = sb("wT", [128, nW, 128], F32)
        slot, at = {}, 0
        for n in WT:
            slot[n] = at
            at += WROWS.get(n, 1)
        w0 = sb("w0", [128, 128], F32)
        conv = sb("conv", [128, STEPS * 128], F32)
        vec = sb("vec", [128, 14], F32)
        vcol, at = {}, 0
        for n in VECS:
            vcol[n] = at
            at += 3 if "gru" in n else 1
        gbias = sb("gbias", [128, 2], F32)
        ident = sb("ident", [128, 128], F32)
        center = sb("center", [128, 128], F32)
        mean = sb("mean", [128, 128], F32)
        epsc = sb("epsc", [128, 1], F32)
        rows_i = sb("rows_i", [1, NW + T + 1], I32)
        flag_at = NW + T

        PS = [ctx.enter_context(nc.psum_tensor(n, [128, 512], F32))
              for n in ("acc0", "acc1", "g0", "g1", "g2", "g3", "m0", "m1")]
        acc, gate, mps = PS[0:2], PS[2:6], PS[6:8]

        sums = nc.dram_tensor("edge_sums_and_degree", (128, 2, NPAD), F32).ap()
        x1s = nc.dram_tensor("x1_transposed", (128, NPAD), F32).ap()
        x3s = nc.dram_tensor("x3_transposed", (128, NPAD), F32).ap()

        build = ExitStack()
        tab = sb("tab", [B, ET, 2], F32, build)
        dstc = sb("dstc", [B, ET], F32, build)
        wkey = sb("wkey", [B, NW, 2], F32, build)
        jkey = sb("jkey", [B, T], F32, build)
        iota_m = sb("iota_m", [B, MW], F16, build)
        iota_b = sb("iota_b", [B, B], F32, build)
        ones_bf = sb("ones_bf", [B, 128], BF16, build)
        zpad = sb("zpad", [128, 2, NPAD - N], F32, build)
        prep = ExitStack()
        wraw = sb("wraw", [128, nW, 128], F32, prep)
        vraw = sb("vraw", [14, 128], F32, prep)
        ei = sb("ei", [TP, 2, TQ * B], I32, prep)
        ef = sb("ef", [TP, 2, TQ * B], F32, prep)
        src_tile = ei[:, 0, :].bitcast(F32)
        window = ei[:, 1, :].bitcast(F32)
        keys = sb("keys", [TP, 2, TQ * B], F32, prep)
        mm = sb("mm", [TP, 2, TQ], F32, prep)
        ones = sb("ones", [128, 128], F32, prep)
        mmb = sb("mmb", [TP, 2, TQ, B], F32, prep)
        tnum = sb("tnum", [B, TQ, TP], F32, prep)
        first = sb("first", [B, 2], F32, prep)
        cover = sb("cover", [B, 3, TQ * TP], F32, prep)
        ends = sb("ends", [B, 2, 4], F32, prep)
        flag_f = sb("flag_f", [1, 1], F32, prep)

        weights_in, edges_in, vecs_in = sem("weights_in"), sem("edges_in"), sem("vecs_in")
        consts, ident_zero, consts2 = sem("consts"), sem("ident_zero"), sem("consts2")
        prep_step, turned, taken = sem("prep_step"), sem("turned"), sem("taken")
        wturned, wtaken = sem("wturned"), sem("wtaken")
        pads_out = sem("pads_out")

        wgroups = [(g, min(4, nW - g)) for g in range(0, nW, 4)]

        with nc.Block() as block:
            @block.sync
            def _(sp):
                sp.dma_start(ei[:, 0, :], a["src"].rearrange("(p e) -> p e", p=TP)).then_inc(edges_in, 16)
                sp.dma_start(ei[:, 1, :], a["dst"].rearrange("(p e) -> p e", p=TP)).then_inc(edges_in, 16)
                for n in WT:
                    k = WROWS.get(n, 1)
                    sp.dma_start(wraw[:, slot[n]:slot[n] + k, :],
                                 a[n].rearrange("(k o) i -> o k i", k=k)).then_inc(weights_in, 16)
                sp.dma_start(w0[:], a["L0_gnn_W"]).then_inc(vecs_in, 16)
                sp.dma_start(conv[:].rearrange("i (t o) -> i t o", t=STEPS),
                             a["L3_gnn_conv_w"].rearrange("t i o -> i t o")).then_inc(vecs_in, 16)
                sp.wait_ge(consts, 1)
                sp.dma_start(sums[:, :, N:NPAD], zpad[:]).then_inc(pads_out, 16)
                sp.wait_ge(pads_out, 16)

            @block.gpsimd
            def _(pool):
                pool.memset(zpad[:], 0.0).then_inc(consts, 1)
                pool.memset(ident[:], 0.0).then_inc(ident_zero, 1)
                pool.wait_ge(ident_zero, 1)
                pool.affine_select(out=ident[:], in_=ident[:], compare_op=ALU.not_equal, fill=1.0, base=0,
                                   pattern=[[-1, 128]], channel_multiplier=1).then_inc(consts, 1)
                pool.memset(mean[:], 1.0 / 128).then_inc(consts, 1)
                pool.memset(ones[:], 1.0).then_inc(consts, 1)
                pool.memset(ones_bf[:], 1.0).then_inc(consts, 1)
                pool.memset(epsc[:], EPS).then_inc(consts, 1)
                pool.iota(iota_m[:], pattern=[[1, MW]], base=0, channel_multiplier=0,
                          allow_small_or_imprecise_dtypes=True).then_inc(consts2, 1)
                pool.iota(iota_b[:], pattern=[[1, B]], base=0, channel_multiplier=0,
                          allow_small_or_imprecise_dtypes=True).then_inc(consts2, 1)
                pool.iota(wkey[:, :, 0], pattern=[[128, NW]], base=0, channel_multiplier=0,
                          allow_small_or_imprecise_dtypes=True).then_inc(consts2, 1)
                pool.iota(wkey[:, :, 1], pattern=[[W, NW]], base=0, channel_multiplier=0,
                          allow_small_or_imprecise_dtypes=True).then_inc(consts2, 1)
                pool.iota(jkey[:], pattern=[[B, T]], base=0, channel_multiplier=0,
                          allow_small_or_imprecise_dtypes=True).then_inc(consts2, 1)
                pool.iota(tnum[:], pattern=[[1, TQ], [TQ, TP]], base=0, channel_multiplier=0,
                          allow_small_or_imprecise_dtypes=True).then_inc(consts2, 1)
                pool.iota(first[:, 0:1], pattern=[[0, 1]], base=0, channel_multiplier=W,
                          allow_small_or_imprecise_dtypes=True).then_inc(consts2, 1)
                pool.iota(first[:, 1:2], pattern=[[0, 1]], base=0, channel_multiplier=B,
                          allow_small_or_imprecise_dtypes=True).then_inc(consts2, 1)

            @block.vector
            def _(dve):
                steps = [0]

                def step(ins):
                    steps[0] += 1
                    ins.then_inc(prep_step, 1)
                    dve.wait_ge(prep_step, steps[0])

                dve.wait_ge(edges_in, 32)
                step(dve.tensor_copy(ef[:], ei[:]))
                srcf, dstf = ef[:, 0, :], ef[:, 1, :]
                dve.tensor_scalar(src_tile, srcf, 1.0 / B, 0.5 / B - 0.5, ALU.mult, ALU.add)
                step(dve.tensor_scalar(window, dstf, 1.0 / W, 0.5 / W - 0.5, ALU.mult, ALU.add))
                dve.tensor_scalar(src_tile, src_tile, MAGIC, MAGIC, ALU.add, ALU.subtract)
                step(dve.tensor_scalar(window, window, MAGIC, MAGIC, ALU.add, ALU.subtract))
                dve.scalar_tensor_tensor(out=keys[:, 0, :], in0=src_tile, scalar=-float(B), in1=srcf,
                                         op0=ALU.mult, op1=ALU.add)
                step(dve.scalar_tensor_tensor(out=keys[:, 1, :], in0=src_tile, scalar=float(W), in1=dstf,
                                              op0=ALU.mult, op1=ALU.add))
                step(dve.scalar_tensor_tensor(out=keys[:, 0, :], in0=window, scalar=128.0, in1=keys[:, 0, :],
                                              op0=ALU.mult, op1=ALU.add))
                dst4 = dstf.rearrange("p (q e) -> p q e", q=TQ)
                dve.tensor_reduce(mm[:, 0, :], dst4, AX_X, ALU.min)
                step(dve.tensor_reduce(mm[:, 1, :], dst4, AX_X, ALU.max))
                dve.wait_ge(consts, 6)
                for k in range(2):
                    for q in range(TQ):
                        last = dve.tensor_scalar(mmb[:, k, q, :], ones[0:TP, 0:B], mm[:, k, q:q + 1], None, ALU.mult)
                step(last)
                for k in range(3):
                    dve.wait_ge(turned, k + 1)
                    dst_ap = (tab[:, :, k] if k < 2 else dstc[:]).rearrange("e (p q) -> e q p", q=TQ)
                    dve.tensor_copy(dst_ap, PS[k][0:B, 0:TQ * TP].rearrange("e (q p) -> e q p", q=TQ)).then_inc(taken, 1)
                dve.wait_ge(consts2, 8)
                dve.wait_ge(turned, 5)
                low, high = PS[3][0:B, 0:ET], PS[4][0:B, 0:ET]
                tn = tnum[:].rearrange("p q t -> p (q t)")
                for k, (width, most, parts) in enumerate(((W, KA, B), (B, KE, T))):
                    f = first[0:parts, k:k + 1]
                    e = ends[0:parts, k, :]
                    c0, c1, c2 = (cover[0:parts, i, :] for i in range(3))
                    step(dve.tensor_scalar(ends[0:parts, k, 3:4], f, float(width - 1), None, ALU.add))
                    step(dve.tensor_scalar(c0, low[0:parts], e[:, 3:4], None, ALU.is_le))
                    step(dve.scalar_tensor_tensor(out=c0, in0=high[0:parts], scalar=f, in1=c0,
                                                  op0=ALU.is_ge, op1=ALU.mult))
                    dve.scalar_tensor_tensor(out=c1, in0=tn[0:parts], scalar=1.0, in1=c0, op0=ALU.add, op1=ALU.mult)
                    step(dve.scalar_tensor_tensor(out=c2, in0=tn[0:parts], scalar=-BIG, in1=c0,
                                                  op0=ALU.add, op1=ALU.mult))
                    dve.tensor_reduce(e[:, 1:2], c1, AX_X, ALU.max)
                    step(dve.tensor_reduce(e[:, 0:1], c2, AX_X, ALU.min))
                    step(dve.tensor_scalar(e[:, 0:1], e[:, 0:1], BIG, float(ET - most), ALU.add, ALU.min))
                    step(dve.tensor_tensor(e[:, 1:2], e[:, 1:2], e[:, 0:1], ALU.subtract))
                    step(dve.tensor_scalar(e[:, 1:2], e[:, 1:2], float(most), None, ALU.is_gt))
                dve.sem_inc(taken, 1)
                dve.wait_ge(turned, 6)
                dve.tensor_copy(rows_i[0:1, 0:NW + T], PS[5][0:1, 0:NW + T])
                step(dve.tensor_reduce(flag_f[0:1, 0:1], PS[5][0:1, NW + T:2 * (NW + T)], AX_X, ALU.max))
                step(dve.tensor_copy(rows_i[0:1, flag_at:flag_at + 1], flag_f[0:1, 0:1]))
                step(dve.tensor_copy(vec[:], PS[5][:, 400:414]))
                bi, bh = vcol["L3_gnn_gru_bih"], vcol["L3_gnn_gru_bhh"]
                dve.tensor_tensor(gbias[:], vec[:, bi:bi + 2], vec[:, bh:bh + 2], ALU.add)
                dve.tensor_tensor(center[:], ident[:], mean[:], ALU.subtract)

            @block.scalar
            def _(act):
                for n in VECS:
                    k = 3 if "gru" in n else 1
                    act.dma_start(vraw[vcol[n]:vcol[n] + k, :],
                                  a[n].rearrange("(k f) -> k f", k=k)).then_inc(vecs_in, 16)
                for i, (g, k) in enumerate(wgroups):
                    act.wait_ge(wturned, i + 1)
                    act.activation(wT[:, g:g + k, :], mps[i % 2][:, 0:128 * k].rearrange("p (k o) -> p k o", k=k),
                                   ACT.Copy).then_inc(wtaken, 1)

            @block.tensor
            def _(pe):
                pe.wait_ge(consts, 6)
                pe.wait_ge(prep_step, 7)
                for k in range(3):
                    for q in range(TQ):
                        s = (keys[:, k, :] if k < 2 else ef[:, 1, :])[:, q * B:(q + 1) * B]
                        last = pe.transpose(PS[k][0:B, q * TP:(q + 1) * TP], s, ident[0:TP, 0:TP])
                    last.then_inc(turned, 1)
                for k in range(2):
                    for q in range(TQ):
                        last = pe.matmul(PS[3 + k][0:B, q * TP:(q + 1) * TP], mmb[:, k, q, :], ident[0:TP, 0:TP],
                                         start=True, stop=True)
                    last.then_inc(turned, 1)
                pe.wait_ge(weights_in, 16 * len(WT))
                for i, (g, k) in enumerate(wgroups):
                    if i >= 2:
                        pe.wait_ge(wtaken, i - 1)
                    for j in range(k):
                        last = pe.transpose(mps[i % 2][:, 128 * j:128 * (j + 1)], wraw[:, g + j, :], ident[:])
                    last.then_inc(wturned, 1)
                pe.wait_ge(vecs_in, 32 + 16 * len(VECS))
                pe.transpose(PS[5][:, 400:414], vraw[:], ident[0:14, 0:14])
                pe.wait_ge(taken, 4)
                pe.transpose(PS[5][0:1, 0:NW], ends[0:NW, 0, 0:1], ident[0:NW, 0:NW])
                pe.transpose(PS[5][0:1, NW:NW + T], ends[0:T, 1, 0:1], ident[0:T, 0:T])
                pe.transpose(PS[5][0:1, NW + T:2 * NW + T], ends[0:NW, 0, 1:2], ident[0:NW, 0:NW])
                pe.transpose(PS[5][0:1, 2 * NW + T:2 * (NW + T)], ends[0:T, 1, 1:2], ident[0:T, 0:T]).then_inc(turned, 1)
        prep.close()

        wk = ExitStack()
        moving = sb("moving", [B, KA, MW + 1], F16, wk)
        within = sb("within", [B, KA, B + 1], F16, wk)
        ka = sb("ka", [B, WPJ, KA, 2], F32, wk)
        ke = sb("ke", [B, KE], F32, wk)
        efeat = sb("efeat", [B, EQ, 5, 128], F32, wk)
        edst = sb("edst", [B, 2, 5, B], F32, wk)
        stage = sb("stage", [128, 2, B], F32, wk)
        zero = sb("zero", [B, C0 * W // 2 + 8], F32, wk)

        keys_ready, ekeys_ready = sem("keys_ready"), sem("ekeys_ready")
        moving_ready, within_ready, pair_free = sem("moving_ready"), sem("within_ready"), sem("pair_free")
        win_taken = sem("win_taken")
        efeat_in = [sem(f"efeat_in{q}") for q in range(EQ)]
        edst_ready, echunk_free = sem("edst_ready"), sem("echunk_free")
        esum_done, esum_taken, sums_out, adj_zero = sem("esum_done"), sem("esum_taken"), sem("sums_out"), sem("adj_zero")
        ORDER = [("w", 0), ("e", 0), ("w", 1), ("e", 1), ("w", 2), ("e", 2), ("w", 3), ("w", 4), ("e", 3)]
        win_before = [0, 0, 1, 2, 3]

        with nc.Block() as block:
            @block.sync
            def _(sp):
                with sp.Fori(0, T) as j:
                    t0 = sp.value_load(rows_i[0:1, bass.ds(NW + j, 1)], min_val=0, max_val=ET - KE)
                    for q in range(EQ):
                        sp.wait_ge(echunk_free, EQ * j + q + 1)
                        sp.dma_start(efeat[:, q, :, :],
                                     a["edge_attr_128"][bass.ds((t0 + 5 * q) * B, 5 * B), :]
                                     .rearrange("(i p) f -> p i f", p=B)).then_inc(efeat_in[q], 16)

            @block.vector
            def _(dve):
                with dve.Fori(0, T) as j:
                    for w in range(WPJ):
                        t0 = dve.value_load(rows_i[0:1, bass.ds(WPJ * j + w, 1)], min_val=0, max_val=ET - KA)
                        dve.tensor_tensor(ka[:, w, :, :], tab[:, bass.ds(t0, KA), :],
                                          wkey[:, bass.ds(WPJ * j + w, 1), :].to_broadcast([B, KA, 2]),
                                          ALU.subtract).then_inc(keys_ready, 1)
                    t0 = dve.value_load(rows_i[0:1, bass.ds(NW + j, 1)], min_val=0, max_val=ET - KE)
                    dve.tensor_scalar(ke[:], dstc[:, bass.ds(t0, KE)], jkey[:, bass.ds(j, 1)], None,
                                      ALU.subtract).then_inc(ekeys_ready, 1)
                    for kind, n in ORDER:
                        if kind == "w":
                            dve.wait_ge(keys_ready, WPJ * j + n + 1)
                            for i in range(KA):
                                g = KA * (WPJ * j + n) + i
                                dve.wait_ge(pair_free, g + 1)
                                dve.tensor_scalar(within[:, i, 0:B], iota_m[:, 0:B], ka[:, n, i, 0:1], None,
                                                  ALU.is_equal).then_inc(within_ready, 1)
                                dve.tensor_scalar(moving[:, i, 0:MW], iota_m[:], ka[:, n, i, 1:2], None,
                                                  ALU.is_equal).then_inc(moving_ready, 1)
                        else:
                            dve.wait_ge(ekeys_ready, j + 1)
                            dve.wait_ge(echunk_free, EQ * j + n + 3)
                            dve.tensor_tensor(edst[:, n % 2, :, :],
                                              iota_b[:].unsqueeze(1).to_broadcast([B, 5, B]),
                                              ke[:, 5 * n:5 * n + 5].unsqueeze(2).to_broadcast([B, 5, B]),
                                              ALU.is_equal).then_inc(edst_ready, 1)
                    dve.wait_ge(edst_ready, EQ * j + EQ)

            @block.gpsimd
            def _(pool):
                pool.memset(adj[:, :, N:NPAD], 0.0).then_inc(adj_zero, 1)
                pool.memset(zero[:], 0.0).then_inc(adj_zero, 1)

            @block.tensor
            def _(pe):
                pe.sem_inc(pair_free, KA)
                pe.sem_inc(echunk_free, EQ)
                with pe.Fori(0, T) as j:
                    for kind, n in ORDER:
                        if kind == "w":
                            pe.wait_ge(win_taken, WPJ * j + win_before[n] + 1)
                            for i in range(KA):
                                g = KA * (WPJ * j + n) + i
                                pe.wait_ge(within_ready, g + 1)
                                pe.wait_ge(moving_ready, g + 1)
                                b0, b1 = PS[2 * (n % 2)], PS[2 * (n % 2) + 1]
                                pe.matmul(b0[0:B, 0:C0 * W], within[:, i, 0:B], moving[:, i, 0:C0 * W],
                                          start=(i == 0), stop=(i == KA - 1))
                                last = pe.matmul(b1[0:B, 0:MW - C0 * W], within[:, i, 0:B], moving[:, i, C0 * W:MW],
                                                 start=(i == 0), stop=(i == KA - 1)).then_inc(pair_free, 1)
                        else:
                            if n == 0:
                                pe.wait_ge(esum_taken, 2 * j + 1)
                            pe.wait_ge(efeat_in[n], 16 * (j + 1))
                            pe.wait_ge(edst_ready, EQ * j + n + 1)
                            hot16 = edst[:, n % 2, :, :].bitcast(BF16).rearrange("p i (d h) -> p i d h", h=2)
                            for i in range(5):
                                first_, last_ = (n == 0 and i == 0), (n == EQ - 1 and i == 4)
                                pe.matmul(PS[4][:, 0:B], efeat[:, n, i, :], edst[:, n % 2, i, :],
                                          start=first_, stop=last_)
                                mmd = pe.matmul(PS[5][:, 0:B], ones_bf[:], hot16[:, i, :, 1], start=first_, stop=last_)
                            mmd.then_inc(echunk_free, 1)

            @block.scalar
            def _(act):
                act.sem_inc(win_taken, 1)
                act.sem_inc(esum_taken, 1)
                with act.Fori(0, T) as j:
                    for kind, n in ORDER:
                        if kind == "w":
                            act.wait_ge(pair_free, KA * (WPJ * j + n) + 2 * KA)
                            b0, b1 = PS[2 * (n % 2)], PS[2 * (n % 2) + 1]
                            at_ = (j * WPJ + n) * W
                            act.activation(adj[:, 0:C0, bass.ds(at_, W)],
                                           b0[0:B, 0:C0 * W].rearrange("p (c d) -> p c d", c=C0), ACT.Copy)
                            act.activation(adj[:, C0:T, bass.ds(at_, W)],
                                           b1[0:B, 0:MW - C0 * W].rearrange("p (c d) -> p c d", c=T - C0),
                                           ACT.Copy).then_inc(win_taken, 1)
                    act.wait_ge(echunk_free, EQ * j + 2 * EQ)
                    act.activation(stage[:, 0, :], PS[4][:, 0:B], ACT.Copy).then_inc(esum_taken, 1)
                    act.activation(stage[:, 1, :], PS[5][:, 0:B], ACT.Copy).then_inc(esum_taken, 1)
                    act.wait_ge(esum_taken, 2 * j + 3)
                    act.dma_start(sums[:, :, bass.ds(j * B, B)], stage[:]).then_inc(sums_out, 16)
                    act.wait_ge(sums_out, 16 * j + 16)
        pair_keys, pair_hot, pair_used = sem("pair_keys"), sem("pair_hot"), sem("pair_used")
        all_done, all_taken = sem("all_done"), sem("all_taken")
        efeat1_in, ekey1, ehot1, epair_used = sem("efeat1_in"), sem("ekey1"), sem("ehot1"), sem("epair_used")
        esum1_done, esum1_taken, sums1_out = sem("esum1_done"), sem("esum1_taken"), sem("sums1_out")

        def general(eng):
            flag = eng.value_load(rows_i[0:1, flag_at:flag_at + 1], min_val=0, max_val=1)
            return eng.If(flag == 1)

        with nc.Block() as block:
            @block.sync
            def _(sp):
                with general(sp):
                    with sp.Fori(0, T) as j:
                        with sp.Fori(0, ET) as t:
                            sp.wait_ge(epair_used, ET * j + t + 1)
                            sp.dma_start(efeat[:, 0, 0, :],
                                         a["edge_attr_128"][bass.ds(t * B, B), :]).then_inc(efeat1_in, 16)

            @block.vector
            def _(dve):
                with general(dve):
                    with dve.Fori(0, NW) as w:
                        with dve.Fori(0, ET) as t:
                            n = ET * w + t
                            dve.wait_ge(pair_used, n + 1)
                            dve.tensor_tensor(ka[:, 0, 0:1, :], tab[:, bass.ds(t, 1), :], wkey[:, bass.ds(w, 1), :],
                                              ALU.subtract).then_inc(pair_keys, 1)
                            dve.wait_ge(pair_keys, n + 1)
                            dve.tensor_scalar(within[:, 0, 0:B], iota_m[:, 0:B], ka[:, 0, 0, 0:1], None,
                                              ALU.is_equal).then_inc(pair_hot, 1)
                            dve.tensor_scalar(moving[:, 0, 0:MW], iota_m[:], ka[:, 0, 0, 1:2], None,
                                              ALU.is_equal).then_inc(pair_hot, 1)
                            dve.wait_ge(pair_hot, 2 * n + 2)
                    with dve.Fori(0, T) as j:
                        with dve.Fori(0, ET) as t:
                            n = ET * j + t
                            dve.wait_ge(epair_used, n + 1)
                            dve.tensor_scalar(ke[:, 0:1], dstc[:, bass.ds(t, 1)], jkey[:, bass.ds(j, 1)], None,
                                              ALU.subtract).then_inc(ekey1, 1)
                            dve.wait_ge(ekey1, n + 1)
                            dve.tensor_scalar(edst[:, 0, 0, :], iota_b[:], ke[:, 0:1], None,
                                              ALU.is_equal).then_inc(ehot1, 1)
                            dve.wait_ge(ehot1, n + 1)

            @block.tensor
            def _(pe):
                z16, zbf = zero[:].bitcast(F16), zero[:].bitcast(BF16)
                with general(pe):
                    pe.sem_inc(pair_used, 1)
                    pe.sem_inc(epair_used, 1)
                    with pe.Fori(0, NW) as w:
                        pe.wait_ge(all_taken, w + 1)
                        pe.matmul(PS[0][0:B, 0:C0 * W], z16[:, 0:B], z16[:, 0:C0 * W], start=True, stop=False)
                        pe.matmul(PS[1][0:B, 0:MW - C0 * W], z16[:, 0:B], z16[:, 0:MW - C0 * W], start=True, stop=False)
                        with pe.Fori(0, ET) as t:
                            pe.wait_ge(pair_hot, 2 * (ET * w + t) + 2)
                            pe.matmul(PS[0][0:B, 0:C0 * W], within[:, 0, 0:B], moving[:, 0, 0:C0 * W],
                                      start=False, stop=False)
                            pe.matmul(PS[1][0:B, 0:MW - C0 * W], within[:, 0, 0:B], moving[:, 0, C0 * W:MW],
                                      start=False, stop=False).then_inc(pair_used, 1)
                        pe.matmul(PS[0][0:B, 0:C0 * W], z16[:, 0:B], z16[:, 0:C0 * W], start=False, stop=True)
                        pe.matmul(PS[1][0:B, 0:MW - C0 * W], z16[:, 0:B], z16[:, 0:MW - C0 * W],
                                  start=False, stop=True).then_inc(all_done, 1)
                    with pe.Fori(0, T) as j:
                        pe.wait_ge(esum1_taken, 2 * j + 1)
                        pe.matmul(PS[4][:, 0:B], zero[:, 0:128], zero[:, 0:B], start=True, stop=False)
                        pe.matmul(PS[5][:, 0:B], zbf[:, 0:128], zbf[:, 0:B], start=True, stop=False)
                        with pe.Fori(0, ET) as t:
                            n = ET * j + t
                            pe.wait_ge(ehot1, n + 1)
                            pe.wait_ge(efeat1_in, 16 * n + 16)
                            pe.matmul(PS[4][:, 0:B], efeat[:, 0, 0, :], edst[:, 0, 0, :], start=False, stop=False)
                            hot16 = edst[:, 0, 0, :].bitcast(BF16).rearrange("p (d h) -> p d h", h=2)
                            pe.matmul(PS[5][:, 0:B], ones_bf[:], hot16[:, :, 1], start=False,
                                      stop=False).then_inc(epair_used, 1)
                        pe.matmul(PS[4][:, 0:B], zero[:, 0:128], zero[:, 0:B], start=False, stop=True)
                        pe.matmul(PS[5][:, 0:B], zbf[:, 0:128], zbf[:, 0:B], start=False, stop=True).then_inc(esum1_done, 1)

            @block.scalar
            def _(act):
                with general(act):
                    act.sem_inc(all_taken, 1)
                    act.sem_inc(esum1_taken, 1)
                    with act.Fori(0, NW) as w:
                        act.wait_ge(all_done, w + 1)
                        act.activation(adj[:, 0:C0, bass.ds(w * W, W)],
                                       PS[0][0:B, 0:C0 * W].rearrange("p (c d) -> p c d", c=C0), ACT.Copy)
                        act.activation(adj[:, C0:T, bass.ds(w * W, W)],
                                       PS[1][0:B, 0:MW - C0 * W].rearrange("p (c d) -> p c d", c=T - C0),
                                       ACT.Copy).then_inc(all_taken, 1)
                    with act.Fori(0, T) as j:
                        act.wait_ge(esum1_done, j + 1)
                        act.activation(stage[:, 0, :], PS[4][:, 0:B], ACT.Copy).then_inc(esum1_taken, 1)
                        act.activation(stage[:, 1, :], PS[5][:, 0:B], ACT.Copy).then_inc(esum1_taken, 1)
                        act.wait_ge(esum1_taken, 2 * j + 3)
                        act.dma_start(sums[:, :, bass.ds(j * B, B)], stage[:]).then_inc(sums1_out, 16)
                        act.wait_ge(sums1_out, 16 * j + 16)
        wk.close()
        build.close()
        layers(nc, ctx, sb, sem, a, out, locals())


def layers(nc, ctx, sb, sem, a, out, env):
    adj, wT, w0, conv, vec, slot, vcol = (env[k] for k in ("adj", "wT", "w0", "conv", "vec", "slot", "vcol"))
    gbias, ident, center, mean, epsc = (env[k] for k in ("gbias", "ident", "center", "mean", "epsc"))
    acc, gate, mps, sums, x1s, x3s = (env[k] for k in ("acc", "gate", "mps", "sums", "x1s", "x3s"))

    hT = sb("hT", [128, NPAD], F32)
    msg = sb("msg", [B, T, 2, 128], F16)
    sd = sb("sd", [128, 2, 2, CW], F32)
    u = sb("u", [128, CW], F32)
    sq = sb("sq", [128, CW], F32)
    rdeg = sb("rdeg", [128, CW], F32)
    v1 = sb("v1", [128, CW], F32)
    v2 = sb("v2", [128, CW], F32)
    res = sb("res", [128, CW], F32)
    x_in = msg[:].rearrange("p s h f -> p (s h f)").bitcast(F32).rearrange("p (s f) -> p s f", s=T)
    res3 = sd[:, :, 0, :]
    agg = sd[:, :, 0, :]
    gr, gz, gt, gn = u, sq, v1, v2

    def col(name, k=0):
        return vec[:, vcol[name] + k:vcol[name] + k + 1]

    def w(name, k=0):
        return wT[:, slot[name] + k, :]

    APPS = 4 + STEPS
    pad_zero = sem("pad_zero")
    x_loaded, xT_done, xT_taken = sem("x_loaded"), sem("xT_done"), sem("xT_taken")
    m_done, hi_ready, lo_ready = sem("m_done"), sem("hi_ready"), sem("lo_ready")
    acc_done, acc_free = sem("acc_done"), sem("acc_free")
    self_free = sem("self_free")
    sd_in = [sem("sd_in0"), sem("sd_in1")]
    res_in, res3_in = sem("res_in"), [sem("res3_in0"), sem("res3_in1")]
    rdeg_max, rdeg_ready = sem("rdeg_max"), sem("rdeg_ready")
    scaled, mixed, mixed2, summed = sem("scaled"), sem("mixed"), sem("mixed2"), sem("summed")
    u_ready, center_done, sq_ready, var_done = sem("u_ready"), sem("center_done"), sem("sq_ready"), sem("var_done")
    dev_ready, rdev_ready, norm_ready, act_ready = sem("dev_ready"), sem("rdev_ready"), sem("norm_ready"), sem("act_ready")
    h_ready = sem("h_ready")
    x1_out, x3_out = sem("x1_out"), [sem(f"x3_out{c}") for c in range(NC)]
    enc1_done, enc1_ready, enc2_done = sem("enc1_done"), sem("enc1_ready"), sem("enc2_done")
    agg_ready, gates_done, r_ready, z_ready = sem("agg_ready"), sem("gates_done"), sem("r_ready"), sem("z_ready")
    inner1, inner2, n_ready, diff1, diff2 = sem("inner1"), sem("inner2"), sem("n_ready"), sem("diff1"), sem("diff2")
    relu_ready, dec1_done, dec1_ready, dec2_done = sem("relu_ready"), sem("dec1_done"), sem("dec1_ready"), sem("dec2_done")
    sig_ready, outT_done, out_taken, out_stored = sem("sig_ready"), sem("outT_done"), sem("out_taken"), sem("out_stored")

    def cols(t, c):
        return t[:, bass.ds(c * CW, CW)]

    def h_count(version, c):
        return NC * (version - 1) + c + 1

    groups = [(4 * g, min(4, T - 4 * g)) for g in range(MG)]
    turned_with = [[g for g, (s0, k) in enumerate(groups) if min(NC - 1, (B * (s0 + k) - 1) // CW + 1) == c]
                   for c in range(NC)]
    def norm_at(app, c, second=0):
        return 2 * c + second if app == 0 else NC * (app + (app == 1)) + c

    PADS = NPAD - N
    with nc.Block() as block:
        @block.sync
        def _(sp):
            sp.dma_start(x_in, a["x"].rearrange("(s p) f -> p s f", p=B)).then_inc(x_loaded, 16)

            def load_sums(app, c, b, i):
                n = NC * app + c
                if not (app == 0 and isinstance(i, int) and i == 0):
                    sp.wait_ge(acc_free, n - 1)
                    sp.wait_ge(acc_done, n - 1)
                sp.dma_start(sd[:, b, :, :], sums[:, :, bass.ds(c * CW, CW)]).then_inc(sd_in[b], 16)

            def store(dst, version, c, done):
                sp.wait_ge(h_ready, h_count(version, c))
                sp.dma_start(dst[:, bass.ds(c * CW, CW)], cols(hT, c)).then_inc(done, 16)

            for b in range(2):
                load_sums(0, b, b, 0)
            with sp.Fori(1, NPAIR) as i:
                for b in range(2):
                    load_sums(0, 2 * i + b, b, i)
                    store(x1s, 1, 2 * i + b - 2, x1_out)
            for c in (NC - 2, NC - 1):
                store(x1s, 1, c, x1_out)
            with sp.Fori(0, NPAIR) as i:
                for b in range(2):
                    load_sums(1, 2 * i + b, b, i)
            sp.wait_ge(x1_out, 16 * NC)
            with sp.Fori(0, NPAIR) as i:
                for b in range(2):
                    c = 2 * i + b
                    load_sums(2, c, b, i)
                    sp.wait_ge(u_ready, 2 * NC + c)
                    sp.dma_start(res[:], cols(x1s, c)).then_inc(res_in, 16)
            with sp.Fori(0, NPAIR) as i:
                for b in range(2):
                    load_sums(3, 2 * i + b, b, i)
            for c in range(NC):
                store(x3s, 4, c, x3_out[c])
            for c in range(NC):
                sp.wait_ge(x3_out[c], 16)
            with sp.Fori(0, NPAIR) as i:
                for b in range(2):
                    c = 2 * i + b
                    sp.wait_ge(h_ready, h_count(6 + STEPS, 0) + c - 2)
                    sp.wait_ge(gates_done, NC * STEPS)
                    sp.dma_start(res3[:, b, :], cols(x3s, c)).then_inc(res3_in[b], 16)
            for g, (s0, k) in enumerate(groups):
                sp.wait_ge(out_taken, g + 1)
                sp.dma_start(out[B * s0:B * (s0 + k), :].rearrange("(s p) f -> p s f", p=B),
                             x_in[:, s0:s0 + k, :]).then_inc(out_stored, 16)
            sp.wait_ge(out_stored, 16 * MG)

        @block.tensor
        def _(pe):
            def messages(app, rhs, version):
                for g, (s0, k) in enumerate(groups):
                    if version:
                        pe.wait_ge(h_ready, h_count(version, min(NC - 1, (B * (s0 + k) - 1) // CW)))
                    elif g == 0:
                        pe.wait_ge(xT_taken, MG)
                        pe.wait_ge(pad_zero, 1)
                    if g >= 2:
                        pe.wait_ge(lo_ready, MG * app + g - 1)
                    for s in range(s0, s0 + k):
                        last = pe.matmul(mps[g % 2][0:B, 128 * (s - s0):128 * (s - s0 + 1)],
                                         hT[:, B * s:B * (s + 1)], rhs, start=True, stop=True)
                    last.then_inc(m_done, 1)

            def neighbours(app, c, b, hooks={}, tail=None):
                n = NC * app + c
                if app >= 4 and not (isinstance(n, int) and n < 4 * NC + 2):
                    pe.wait_ge(agg_ready, n - 4 * NC - 1)
                elif not (isinstance(n, int) and n < 2):
                    pe.wait_ge(acc_free, n - 1)
                for s in range(T):
                    if s in hooks:
                        hooks[s]()
                    if isinstance(c, int) and c == 0 and s % 4 == 0:
                        pe.wait_ge(lo_ready, MG * app + s // 4 + 1)
                    rhs = adj[:, s, bass.ds(c * CW, CW)]
                    pe.matmul(acc[b][:, 0:CW], msg[:, s, 0, :], rhs, start=(s == 0), stop=False)
                    last = pe.matmul(acc[b][:, 0:CW], msg[:, s, 1, :], rhs, start=False,
                                     stop=(s == T - 1 and tail is None))
                if tail:
                    last = tail()
                last.then_inc(acc_done, 1)

            def centered(k, g):
                pe.wait_ge(u_ready, k + 1)
                pe.matmul(gate[g][:, 0:CW], center[:], u[:], start=True, stop=True).then_inc(center_done, 1)

            def variance(k, g):
                pe.wait_ge(sq_ready, k + 1)
                pe.matmul(gate[g][:, 0:CW], mean[:], sq[:], start=True, stop=True).then_inc(var_done, 1)

            def pairs(body):
                for b in range(2):
                    body(b, b)
                with pe.Fori(1, NPAIR) as i:
                    for b in range(2):
                        body(2 * i + b, b)

            pe.wait_ge(x_loaded, 16)
            for g, (s0, k) in enumerate(groups):
                if g >= 2:
                    pe.wait_ge(xT_taken, g - 1)
                for s in range(s0, s0 + k):
                    last = pe.transpose(mps[g % 2][:, B * (s - s0):B * (s - s0 + 1)], x_in[:, s, :], ident[0:B, 0:B])
                last.then_inc(xT_done, 1)

            messages(0, w0[:], 0)

            def hooks0(c):
                return {4: lambda: centered(2 * c, 0), 7: lambda: variance(2 * c, 1),
                        22: lambda: centered(2 * c + 1, 2), 24: lambda: variance(2 * c + 1, 3)}

            pairs(lambda c, b: neighbours(0, c, b, {} if isinstance(c, int) and c == 0 else hooks0(c - 1)))
            for hook in hooks0(NC - 1).values():
                hook()

            for app in (1, 2):
                messages(app, w(f"L1_gnn_W1_{app - 1}"), app)

                def own(app, c, b):
                    n = NC * app + c
                    if isinstance(c, int):
                        pe.wait_ge(sd_in[b], 16 * (NPAIR * app + 1))
                    else:
                        pe.wait_ge(sd_in[b], (NC * app + c - b + 2) * 8)
                    if not (isinstance(n, int) and n == NC):
                        pe.wait_ge(self_free, n - NC)
                    for k in (2, 3):
                        pe.matmul(gate[k - 2][:, 0:CW], w(f"L1_gnn_W{k}_{app - 1}"), cols(hT, c), start=True, stop=True)
                    return pe.matmul(acc[b][:, 0:CW], w(f"L1_gnn_W1_{app - 1}"), sd[:, b, 0, :], start=False, stop=True)

                def hooks1(app, c):
                    if app == 1 or (isinstance(c, int) and c < 0):
                        return {}
                    k = norm_at(2, c)
                    return {10: lambda: centered(k, 2), 15: lambda: variance(k, 3)}

                pairs(lambda c, b: neighbours(app, c, b, hooks1(app, c - 1), lambda: own(app, c, b)))
                for hook in hooks1(app, NC - 1).values():
                    hook()

            messages(3, w("L2_gnn_W_neigh"), 3)

            def own2(c, b):
                pe.wait_ge(self_free, 2 * NC + c)
                pe.matmul(gate[0][:, 0:CW], w("L2_gnn_W_self"), cols(hT, c), start=True, stop=True)

            def hooks2(c):
                k = norm_at(3, c)
                return {8: lambda: centered(k, 2), 13: lambda: variance(k, 3)}

            def chunk2(c, b):
                hooks = {} if isinstance(c, int) and c == 0 else hooks2(c - 1)
                neighbours(3, c, b, {**hooks, 20: lambda: own2(c, b)})
            pairs(chunk2)
            for hook in hooks2(NC - 1).values():
                hook()

            def enc1(c):
                pe.wait_ge(h_ready, h_count(4, c))
                pe.matmul(gate[c % 2][:, 0:CW], w("L3_gnn_enc_w1"), cols(hT, c), start=True, stop=True).then_inc(enc1_done, 1)

            def enc2(c):
                pe.wait_ge(enc1_ready, c + 1)
                if c >= 2:
                    pe.wait_ge(h_ready, h_count(5, c - 2))
                pe.matmul(gate[2 + c % 2][:, 0:CW], w("L3_gnn_enc_w2"), (u, sq)[c % 2][:],
                          start=True, stop=True).then_inc(enc2_done, 1)
            enc1(0)
            pe.wait_ge(h_ready, h_count(4, NC - 1))
            for c in range(NC):
                if c + 1 < NC:
                    enc1(c + 1)
                enc2(c)

            def gates(k, c, b):
                if not (isinstance(k, int) and k == 0):
                    pe.wait_ge(inner2, k)
                    pe.wait_ge(z_ready, k)
                hc, ih, hh = cols(hT, c), "L3_gnn_gru_wih", "L3_gnn_gru_whh"
                pe.matmul(gate[0][:, 0:CW], w(hh, 0), hc, start=True, stop=False)
                pe.matmul(gate[1][:, 0:CW], w(hh, 1), hc, start=True, stop=False)
                pe.matmul(gate[3][:, 0:CW], w(hh, 2), hc, start=True, stop=True)
                pe.wait_ge(agg_ready, k + 1)
                pe.matmul(gate[0][:, 0:CW], w(ih, 0), agg[:, b, :], start=False, stop=True)
                pe.matmul(gate[1][:, 0:CW], w(ih, 1), agg[:, b, :], start=False, stop=True)
                pe.matmul(gate[2][:, 0:CW], w(ih, 2), agg[:, b, :], start=True, stop=True).then_inc(gates_done, 1)

            for t in range(STEPS):
                messages(4 + t, conv[:, 128 * t:128 * (t + 1)], 5 + t)

                def chunk3(c, b):
                    hooks = {} if isinstance(c, int) and c == 0 else {3: lambda: gates(NC * t + c - 1, c - 1, 1 - b)}
                    neighbours(4 + t, c, b, hooks)
                pairs(chunk3)
                gates(NC * t + NC - 1, NC - 1, 1)

            def dec1(c):
                pe.wait_ge(relu_ready, c + 1)
                pe.matmul(gate[c % 2][:, 0:CW], w("L3_gnn_dec_w1"), (v1, v2)[c % 2][:],
                          start=True, stop=True).then_inc(dec1_done, 1)

            def dec2(c):
                pe.wait_ge(dec1_ready, c + 1)
                if c >= 2:
                    pe.wait_ge(sig_ready, c - 1)
                pe.matmul(gate[2 + c % 2][:, 0:CW], w("L3_gnn_dec_w2"), (u, sq)[c % 2][:],
                          start=True, stop=True).then_inc(dec2_done, 1)
            dec1(0)
            for c in range(NC):
                if c + 1 < NC:
                    dec1(c + 1)
                dec2(c)

            def last_center(c):
                pe.wait_ge(h_ready, h_count(6 + STEPS, c))
                if c >= 2:
                    pe.wait_ge(h_ready, h_count(7 + STEPS, c - 2))
                pe.matmul(gate[c % 2][:, 0:CW], center[:], cols(hT, c), start=True, stop=True).then_inc(center_done, 1)

            def last_variance(c):
                k = 4 * NC + c
                pe.wait_ge(sq_ready, k + 1)
                if c >= 2:
                    pe.wait_ge(dev_ready, k - 1)
                pe.matmul(gate[2 + c % 2][:, 0:CW], mean[:], (u, sq)[c % 2][:], start=True, stop=True).then_inc(var_done, 1)
            last_center(0)
            for c in range(NC):
                if c + 1 < NC:
                    last_center(c + 1)
                last_variance(c)
                for g in turned_with[c]:
                    s0, k = groups[g]
                    pe.wait_ge(h_ready, h_count(7 + STEPS, min(NC - 1, (B * (s0 + k) - 1) // CW)))
                    if g >= 2:
                        pe.wait_ge(out_taken, g - 1)
                    for s in range(s0, s0 + k):
                        last = pe.transpose(mps[g % 2][0:B, 128 * (s - s0):128 * (s - s0 + 1)],
                                            hT[:, B * s:B * (s + 1)], ident[:])
                    last.then_inc(outT_done, 1)

        @block.scalar
        def _(act):
            def hi(app):
                for g, (s0, k) in enumerate(groups):
                    act.wait_ge(m_done, MG * app + g + 1)
                    act.activation(msg[:, s0:s0 + k, 0, :], mps[g % 2][0:B, 0:128 * k].rearrange("p (s f) -> p s f", s=k),
                                   ACT.Copy).then_inc(hi_ready, 1)

            def square(k, g, to=sq):
                act.wait_ge(center_done, k + 1)
                act.activation(to[:], gate[g][:, 0:CW], ACT.Square).then_inc(sq_ready, 1)

            def deviation(k, g, to=sq):
                act.wait_ge(var_done, k + 1)
                act.activation(to[:], gate[g][:, 0:CW], ACT.Sqrt, bias=epsc[:, 0:1]).then_inc(dev_ready, 1)

            def loop(body):
                with act.Fori(0, NPAIR) as i:
                    for b in range(2):
                        body(2 * i + b, b)

            for g, (s0, k) in enumerate(groups):
                act.wait_ge(xT_done, g + 1)
                act.activation(hT[:, B * s0:B * (s0 + k)], mps[g % 2][:, 0:B * k], ACT.Copy).then_inc(xT_taken, 1)

            hi(0)

            def chunk0(c, b):
                square(2 * c, 0)
                deviation(2 * c, 1)
                act.wait_ge(norm_ready, c + 1)
                act.activation(v2[:], v1[:], ACT.Gelu, bias=col("L0_gnn_beta"),
                               scale=col("L0_gnn_gamma")).then_inc(act_ready, 1)
                square(2 * c + 1, 2)
                deviation(2 * c + 1, 3)
            loop(chunk0)

            hi(1)
            hi(2)

            def norm(app):
                def chunk(c, b):
                    square(norm_at(app, c), 2)
                    deviation(norm_at(app, c), 3)
                loop(chunk)
            norm(2)
            hi(3)
            norm(3)

            def enc_in(c):
                act.wait_ge(enc1_done, c + 1)
                if c >= 2:
                    act.wait_ge(enc2_done, c - 1)
                act.activation((u, sq)[c % 2][:], gate[c % 2][:, 0:CW], ACT.Relu,
                               bias=col("L3_gnn_enc_b1")).then_inc(enc1_ready, 1)
            enc_in(0)
            act.wait_ge(h_ready, h_count(4, NC - 1))
            for c in range(NC):
                if c + 1 < NC:
                    enc_in(c + 1)
                act.wait_ge(enc2_done, c + 1)
                act.wait_ge(x3_out[c], 16)
                act.activation(cols(hT, c), gate[2 + c % 2][:, 0:CW], ACT.Identity,
                               bias=col("L3_gnn_enc_b2")).then_inc(h_ready, 1)

            def take(k, app, c, b):
                act.wait_ge(acc_done, NC * app + c + 1)
                if not (isinstance(k, int) and k < 2):
                    act.wait_ge(gates_done, k - 1)
                act.activation(agg[:, b, :], acc[b][:, 0:CW], ACT.Copy).then_inc(agg_ready, 1)

            def gated(k):
                act.wait_ge(gates_done, k + 1)
                act.wait_ge(h_ready, 5 * NC + k)
                act.activation(gr[:], gate[0][:, 0:CW], ACT.Sigmoid, bias=gbias[:, 0:1]).then_inc(r_ready, 1)
                act.activation(gz[:], gate[1][:, 0:CW], ACT.Sigmoid, bias=gbias[:, 1:2]).then_inc(z_ready, 1)
                act.wait_ge(inner2, k + 1)
                act.activation(gn[:], gt[:], ACT.Tanh, bias=col("L3_gnn_gru_bih", 2)).then_inc(n_ready, 1)

            for t in range(STEPS):
                hi(4 + t)
                take(NC * t, 4 + t, 0, 0)
                take(NC * t + 1, 4 + t, 1, 1)
                gated(NC * t)
                with act.Fori(1, NPAIR) as i:
                    for b in range(2):
                        c = 2 * i + b
                        take(NC * t + c, 4 + t, c, b)
                        gated(NC * t + c - 1)
                gated(NC * t + NC - 1)

            def dec_in(c):
                act.wait_ge(dec1_done, c + 1)
                if c >= 2:
                    act.wait_ge(dec2_done, c - 1)
                act.activation((u, sq)[c % 2][:], gate[c % 2][:, 0:CW], ACT.Relu,
                               bias=col("L3_gnn_dec_b1")).then_inc(dec1_ready, 1)
            dec_in(0)
            for c in range(NC):
                if c + 1 < NC:
                    dec_in(c + 1)
                act.wait_ge(dec2_done, c + 1)
                if c >= 2:
                    act.wait_ge(h_ready, h_count(6 + STEPS, c - 2))
                act.activation(sd[:, c % 2, 1, :], gate[2 + c % 2][:, 0:CW], ACT.Sigmoid,
                               bias=col("L3_gnn_dec_b2")).then_inc(sig_ready, 1)

            k0 = 4 * NC
            for c in range(NC):
                if c >= 2:
                    act.wait_ge(rdev_ready, k0 + c - 1)
                square(k0 + c, c % 2, (u, sq)[c % 2])
                deviation(k0 + c, 2 + c % 2, (u, sq)[c % 2])

        @block.vector
        def _(dve):
            def lo(app):
                for g, (s0, k) in enumerate(groups):
                    dve.wait_ge(hi_ready, MG * app + g + 1)
                    dve.tensor_tensor(msg[:, s0:s0 + k, 1, :], mps[g % 2][0:B, 0:128 * k].rearrange("p (s f) -> p s f", s=k),
                                      msg[:, s0:s0 + k, 0, :], ALU.subtract).then_inc(lo_ready, 1)

            def scale_by_degree(app, c, b):
                n = NC * app + c
                dve.wait_ge(sd_in[b], 8 * (n - b) + 16)
                dve.tensor_scalar(rdeg[:], sd[:, b, 1, :], 1.0, None, ALU.max).then_inc(rdeg_max, 1)
                dve.wait_ge(rdeg_max, n + 1)
                dve.reciprocal(rdeg[:], rdeg[:]).then_inc(rdeg_ready, 1)
                dve.wait_ge(rdeg_ready, n + 1)
                dve.wait_ge(acc_done, n + 1)
                dve.tensor_tensor(v1[:], acc[b][:, 0:CW], rdeg[:], ALU.mult).then_inc(scaled, 1)
                dve.wait_ge(scaled, n + 1)

            def normalised(k, g, to, ready, dev=sq):
                dve.wait_ge(dev_ready, k + 1)
                dve.reciprocal(dev[:], dev[:]).then_inc(rdev_ready, 1)
                dve.wait_ge(rdev_ready, k + 1)
                dve.tensor_tensor(to, gate[g][:, 0:CW], dev[:], ALU.mult).then_inc(ready, 1)

            def loop(body):
                with dve.Fori(0, NPAIR) as i:
                    for b in range(2):
                        body(2 * i + b, b)

            dve.memset(hT[:, N:NPAD], 0.0).then_inc(pad_zero, 1)
            lo(0)

            def chunk0(c, b):
                scale_by_degree(0, c, b)
                dve.scalar_tensor_tensor(out=u[:], in0=v1[:], scalar=col("L0_gnn_b"), in1=cols(hT, c),
                                         op0=ALU.add, op1=ALU.add).then_inc(u_ready, 1)
                dve.sem_inc(acc_free, 1)
                dve.wait_ge(u_ready, 2 * c + 1)
                normalised(2 * c, 0, v1[:], norm_ready)
                dve.wait_ge(act_ready, c + 1)
                dve.tensor_tensor(u[:], v2[:], cols(hT, c), ALU.add).then_inc(u_ready, 1)
                dve.wait_ge(u_ready, 2 * c + 2)
                normalised(2 * c + 1, 2, cols(hT, c), h_ready)
            loop(chunk0)

            def chunk1(app, c, b):
                n = NC * app + c
                k = n - NC
                if app == 2:
                    dve.wait_ge(h_ready, NC * 2 + c)
                scale_by_degree(app, c, b)
                deg = sd[:, b, 1, :]
                dve.scalar_tensor_tensor(out=v2[:], in0=deg, scalar=1.0, in1=gate[0][:, 0:CW],
                                         op0=ALU.min, op1=ALU.mult).then_inc(mixed, 1)
                dve.scalar_tensor_tensor(out=rdeg[:], in0=deg, scalar=0.0, in1=gate[1][:, 0:CW],
                                         op0=ALU.is_equal, op1=ALU.mult).then_inc(self_free, 1)
                dve.wait_ge(mixed, k + 1)
                dve.tensor_tensor(v1[:], v1[:], v2[:], ALU.add).then_inc(mixed2, 1)
                dve.wait_ge(self_free, k + 1)
                dve.wait_ge(mixed2, k + 1)
                dve.sem_inc(acc_free, 1)
                dve.tensor_tensor(v1[:], v1[:], rdeg[:], ALU.add).then_inc(summed, 1)
                dve.wait_ge(summed, k + 1)
                if app == 1:
                    dve.wait_ge(x1_out, 16 * NC)
                    dve.scalar_tensor_tensor(out=cols(hT, c), in0=v1[:], scalar=LEAK, in1=v1[:],
                                             op0=ALU.mult, op1=ALU.max).then_inc(h_ready, 1)
                    dve.wait_ge(h_ready, h_count(2, c))
                else:
                    dve.scalar_tensor_tensor(out=v2[:], in0=v1[:], scalar=LEAK, in1=v1[:],
                                             op0=ALU.mult, op1=ALU.max).then_inc(norm_ready, 1)
                    dve.wait_ge(norm_ready, NC + c + 1)
                    dve.wait_ge(res_in, 16 * (c + 1))
                    dve.tensor_tensor(u[:], v2[:], res[:], ALU.add).then_inc(u_ready, 1)
                    dve.wait_ge(u_ready, norm_at(2, c) + 1)
                    normalised(norm_at(2, c), 2, cols(hT, c), h_ready)

            lo(1)
            loop(lambda c, b: chunk1(1, c, b))
            lo(2)
            loop(lambda c, b: chunk1(2, c, b))

            def chunk2(c, b):
                dve.wait_ge(h_ready, NC * 3 + c)
                scale_by_degree(3, c, b)
                dve.scalar_tensor_tensor(out=v2[:], in0=gate[0][:, 0:CW], scalar=col("L2_gnn_b_self"), in1=v1[:],
                                         op0=ALU.add, op1=ALU.add).then_inc(self_free, 1)
                dve.wait_ge(self_free, 2 * NC + c + 1)
                dve.sem_inc(acc_free, 1)
                dve.tensor_tensor(u[:], v2[:], cols(hT, c), ALU.add).then_inc(u_ready, 1)
                dve.wait_ge(u_ready, norm_at(3, c) + 1)
                normalised(norm_at(3, c), 2, cols(hT, c), h_ready)
            lo(3)
            loop(chunk2)

            def gated(t, c):
                k = NC * t + c
                dve.wait_ge(r_ready, k + 1)
                dve.scalar_tensor_tensor(out=gt[:], in0=gate[3][:, 0:CW], scalar=col("L3_gnn_gru_bhh", 2), in1=gr[:],
                                         op0=ALU.add, op1=ALU.mult).then_inc(inner1, 1)
                dve.wait_ge(inner1, k + 1)
                dve.tensor_tensor(gt[:], gt[:], gate[2][:, 0:CW], ALU.add).then_inc(inner2, 1)
                dve.wait_ge(n_ready, k + 1)
                dve.tensor_tensor(gr[:], cols(hT, c), gn[:], ALU.subtract).then_inc(diff1, 1)
                dve.wait_ge(diff1, k + 1)
                dve.wait_ge(z_ready, k + 1)
                dve.tensor_tensor(gr[:], gr[:], gz[:], ALU.mult).then_inc(diff2, 1)
                dve.wait_ge(diff2, k + 1)
                dve.tensor_tensor(cols(hT, c), gr[:], gn[:], ALU.add).then_inc(h_ready, 1)

            for t in range(STEPS):
                lo(4 + t)
                with dve.Fori(0, NC) as c:
                    gated(t, c)

            def relu(c):
                if c >= 2:
                    dve.wait_ge(dec1_done, c - 1)
                dve.wait_ge(h_ready, h_count(5 + STEPS, c))
                dve.tensor_scalar((v1, v2)[c % 2][:], cols(hT, c), 0.0, None, ALU.max).then_inc(relu_ready, 1)
            dve.wait_ge(h_ready, h_count(5 + STEPS, NC - 1))
            relu(0)
            relu(1)
            for c in range(NC):
                dve.wait_ge(sig_ready, c + 1)
                dve.wait_ge(res3_in[c % 2], 16 * (c // 2 + 1))
                dve.wait_ge(relu_ready, c + 1)
                dve.tensor_tensor(cols(hT, c), sd[:, c % 2, 1, :], res3[:, c % 2, :], ALU.add).then_inc(h_ready, 1)
                if c + 2 < NC:
                    relu(c + 2)
            for c in range(NC):
                normalised(4 * NC + c, c % 2, cols(hT, c), h_ready, (u, sq)[c % 2])
                for g in turned_with[c]:
                    s0, k = groups[g]
                    dve.wait_ge(outT_done, g + 1)
                    dve.tensor_copy(x_in[:, s0:s0 + k, :], mps[g % 2][0:B, 0:128 * k]
                                    .rearrange("p (s f) -> p s f", s=k)).then_inc(out_taken, 1)


_INS = ["x", "src", "dst", "edge_attr_128", "L0_gnn_W", "L0_gnn_b", "L0_gnn_gamma", "L0_gnn_beta",
        "L1_gnn_W1_0", "L1_gnn_W2_0", "L1_gnn_W3_0", "L1_gnn_W1_1", "L1_gnn_W2_1", "L1_gnn_W3_1",
        "L2_gnn_W_neigh", "L2_gnn_W_self", "L2_gnn_b_self", "L3_gnn_enc_w1", "L3_gnn_enc_b1", "L3_gnn_enc_w2",
        "L3_gnn_enc_b2", "L3_gnn_conv_w", "L3_gnn_gru_wih", "L3_gnn_gru_whh", "L3_gnn_gru_bih", "L3_gnn_gru_bhh",
        "L3_gnn_dec_w1", "L3_gnn_dec_b1", "L3_gnn_dec_w2", "L3_gnn_dec_b2"]


def kernel(**inputs):
    import numpy as _np
    import concourse.bacc as _bacc
    from concourse import mybir as _mybir
    from concourse.bass_utils import run_bass_kernel_spmd as _run

    nc = _bacc.Bacc("TRN2", target_bir_lowering=False, num_devices=1)
    arrays, ins = {}, {}
    for name in _INS:
        arr = _np.ascontiguousarray(inputs[name])
        arrays[f"in_{name}_dram"] = arr
        ins[name] = nc.dram_tensor(f"in_{name}_dram", arr.shape, _mybir.dt.from_np(arr.dtype), kind="ExternalInput").ap()
    out = nc.dram_tensor("out_0_dram", (N, D), _mybir.dt.float32, kind="ExternalOutput").ap()
    gnn_kernel(nc, ins, out)
    r = _run(nc, [arrays], core_ids=[0])
    return r.results[0]["out_0_dram"]
```

```python
from contextlib import ExitStack

import concourse.bass as bass
from concourse import mybir

F32 = mybir.dt.float32
F16 = mybir.dt.float16
BF16 = mybir.dt.bfloat16
I32 = mybir.dt.int32
ALU = mybir.AluOpType
ACT = mybir.ActivationFunctionType
AX_X = mybir.AxisListType.X

N, D, E = 3125, 128, 50000
B = 125
T = N // B
ET = E // B
TQ = 4
TP = ET // TQ
W = 18
WPJ = 7
NW = WPJ * T
KA = 4
UNROLL = 5
RING = 10
KES = [5, 5, 5, 4]
EQ, KE = len(KES), sum(KES)
KOFF = [sum(KES[:q]) for q in range(EQ)]
MW = T * W
SW = 98
CW = 4 * SW
NC = 8
NPAD = NC * CW
NADJ = NW * W
MG = (T + 3) // 4
BIG = 512.0
MAGIC = 12582912.0
LEAK = (1.0 / 8.0 + 1.0 / 3.0) / 2.0
EPS = 1e-5
STEPS = 5
assert NADJ >= NPAD >= N

WT = ["L1_gnn_W1_0", "L1_gnn_W2_0", "L1_gnn_W3_0", "L1_gnn_W1_1", "L1_gnn_W2_1", "L1_gnn_W3_1",
      "L2_gnn_W_neigh", "L2_gnn_W_self", "L3_gnn_enc_w1", "L3_gnn_enc_w2",
      "L3_gnn_gru_wih", "L3_gnn_gru_whh", "L3_gnn_dec_w1", "L3_gnn_dec_w2"]
WROWS = {"L3_gnn_gru_wih": 3, "L3_gnn_gru_whh": 3}
VECS = ["L0_gnn_b", "L0_gnn_gamma", "L0_gnn_beta", "L2_gnn_b_self", "L3_gnn_enc_b1", "L3_gnn_enc_b2",
        "L3_gnn_gru_bih", "L3_gnn_gru_bhh", "L3_gnn_dec_b1", "L3_gnn_dec_b2"]
NVEC = sum(3 if "gru" in n else 1 for n in VECS)


def gnn_kernel(nc, ins, out):
    a = ins
    ctx = ExitStack()
    with ctx:
        def sb(name, shape, dt, stack=ctx):
            return stack.enter_context(nc.sbuf_tensor(name, shape, dt))

        def sem(name):
            return ctx.enter_context(nc.semaphore(name))

        adj = sb("adj", [B, T * NADJ], F16)
        adj3 = adj[:].rearrange("p (s d) -> p s d", s=T)
        nW = sum(WROWS.get(n, 1) for n in WT)
        wT = sb("wT", [128, nW, 128], F32)
        slot, at = {}, 0
        for n in WT:
            slot[n] = at
            at += WROWS.get(n, 1)
        w0 = sb("w0", [128, 128], F32)
        conv = sb("conv", [128, STEPS * 128], F32)
        vec = sb("vec", [128, NVEC], F32)
        vcol, at = {}, 0
        for n in VECS:
            vcol[n] = at
            at += 3 if "gru" in n else 1
        gbias = sb("gbias", [128, 2], F32)
        ident = sb("ident", [128, 128], F32)
        center = sb("center", [128, 128], F32)
        mean = sb("mean", [128, 1], F32)
        ones = sb("ones", [128, 128], F32)
        epsc = sb("epsc", [128, 1], F32)
        rows_i = sb("rows_i", [1, T + 1], I32)
        flag_at = T

        PS = [ctx.enter_context(nc.psum_tensor(n, [128, 512], F32))
              for n in ("acc0", "acc1", "g0", "g1", "g2", "g3", "m0", "m1")]
        acc, gate, mps = PS[0:2], PS[2:6], PS[6:8]

        sums = nc.dram_tensor("edge_sums_transposed", (128, NPAD), F32).ap()
        degs = nc.dram_tensor("degrees", (1, NPAD), F32).ap()
        tabs = nc.dram_tensor("edge_tables", (B, 3 * ET), F32).ap()
        rdegs = nc.dram_tensor("inverse_degrees", (1, NPAD), F32).ap()
        x1s = nc.dram_tensor("x1_transposed", (128, NPAD), F32).ap()
        x3s = nc.dram_tensor("x3_transposed", (128, NPAD), F32).ap()

        build = ExitStack()
        jkey = sb("jkey", [B, T], F32, build)
        ka = sb("ka", [B, 2, NW * KA], F32, build)
        ke = sb("ke", [B, (T + 1) * KE], F32, build)
        iota_m = sb("iota_m", [B, MW], F16, build)
        ones_bf = sb("ones_bf", [B, 1], BF16, build)
        zpad = sb("zpad", [128, NPAD - N], F32, build)
        used = [0]

        def scratch(parts, cols):
            lo = used[0]
            used[0] += cols
            assert 2 * used[0] <= T * NADJ
            return adj[0:parts, 2 * lo:2 * used[0]].bitcast(F32)

        ei = scratch(TP, 2 * TQ * B).bitcast(I32)
        ef = scratch(TP, 2 * TQ * B)
        srcf, dstf = ef[:, 0:TQ * B], ef[:, TQ * B:]
        src_tile, window = scratch(TP, TQ * B), scratch(TP, TQ * B)
        key = [scratch(TP, TQ * B), scratch(TP, TQ * B), dstf]
        tab = scratch(B, 3 * ET).rearrange("p (k t) -> p k t", k=3)
        wkey = scratch(B, 2 * NW).rearrange("p (k w) -> p k w", k=2)
        mm = scratch(TP, 2 * TQ)
        mmb = scratch(TP, 2 * TQ * B)
        tnum = scratch(B, TQ * TP)
        first = scratch(B, 2)
        firstj = scratch(B, 1)
        cover = [scratch(B, ET) for _ in range(3)]
        ends = scratch(B, 4 * 3)
        trow = scratch(1, NW + T)
        flags = scratch(1, NW + T)
        tile_of = scratch(TP, NW * KA)
        tile_e = scratch(TP, T * KE)
        pick = [scratch(TP, NW * KA) for _ in range(TQ)]
        pick_e = [scratch(TP, T * KE) for _ in range(TQ)]
        kofs = scratch(TP, NW * KA)
        kofs_e = scratch(TP, T * KE)
        vraw = scratch(NVEC, 128)
        flag_f = scratch(1, 1)

        weights_in, edges_in, vecs_in = sem("weights_in"), sem("edges_in"), sem("vecs_in")
        consts, ident_zero, consts2 = sem("consts"), sem("ident_zero"), sem("consts2")
        prep_step, turned, taken = sem("prep_step"), sem("turned"), sem("taken")
        wturned, wtaken, gathered, gather_taken = sem("wturned"), sem("wtaken"), sem("gathered"), sem("gather_taken")
        rows_done, rows_read, picks_ready = sem("rows_done"), sem("rows_read"), sem("picks_ready")
        pads_out = sem("pads_out")

        wgroups = [(g, min(4, nW - g)) for g in range(0, nW, 4)]
        half = NW * KA // 2
        PARTS = [(B, 0), (NW - B, B), (T, NW)]

        with nc.Block() as block:
            @block.sync
            def _(sp):
                sp.dma_start(ei[:, 0:TQ * B], a["src"].rearrange("(p e) -> p e", p=TP)).then_inc(edges_in, 16)
                sp.dma_start(ei[:, TQ * B:], a["dst"].rearrange("(p e) -> p e", p=TP)).then_inc(edges_in, 16)
                for n in WT:
                    k = WROWS.get(n, 1)
                    sp.dma_start(wT[:, slot[n]:slot[n] + k, :],
                                 a[n].rearrange("(k o) i -> o k i", k=k)).then_inc(weights_in, 16)
                sp.dma_start(w0[:], a["L0_gnn_W"]).then_inc(vecs_in, 16)
                sp.dma_start(conv[:].rearrange("i (t o) -> i t o", t=STEPS),
                             a["L3_gnn_conv_w"].rearrange("t i o -> i t o")).then_inc(vecs_in, 16)
                sp.wait_ge(consts, 1)
                sp.dma_start(sums[:, N:NPAD], zpad[:]).then_inc(pads_out, 16)
                sp.dma_start(rdegs[:, N:NPAD], zpad[0:1, :]).then_inc(pads_out, 16)
                sp.wait_ge(wtaken, 3)
                sp.dma_start(tabs, tab.rearrange("p k t -> p (k t)")).then_inc(pads_out, 16)
                sp.wait_ge(pads_out, 48)

            @block.gpsimd
            def _(pool):
                def iota(to, pattern, mult=0, base=0):
                    pool.iota(to, pattern=pattern, base=base, channel_multiplier=mult,
                              allow_small_or_imprecise_dtypes=True).then_inc(consts2, 1)

                pool.memset(zpad[:], 0.0).then_inc(consts, 1)
                pool.memset(ke[:, T * KE:], 0.0)
                pool.memset(ident[:], 0.0).then_inc(ident_zero, 1)
                pool.memset(ones[:], 1.0).then_inc(consts, 1)
                pool.wait_ge(ident_zero, 1)
                pool.affine_select(out=ident[:], in_=ident[:], compare_op=ALU.not_equal, fill=1.0, base=0,
                                   pattern=[[-1, 128]], channel_multiplier=1).then_inc(consts, 1)
                pool.memset(mean[:], 1.0 / 128).then_inc(consts, 1)
                pool.memset(ones_bf[:], 1.0).then_inc(consts, 1)
                pool.memset(epsc[:], EPS).then_inc(consts, 1)
                iota(tnum, [[1, TQ], [TQ, TP]])
                iota(first[:, 0:1], [[0, 1]], W)
                iota(first[:, 1:2], [[0, 1]], W, B * W)
                iota(firstj, [[0, 1]], B)
                iota(kofs, [[0, NW], [1, KA]], -TQ)
                iota(kofs_e, [[0, T], [1, KE]], -TQ)
                iota(wkey[:, 0, :], [[128, NW]])
                iota(wkey[:, 1, :], [[W, NW]])
                iota(jkey[:], [[B, T]])
                iota(iota_m[:], [[1, MW]])

            @block.vector
            def _(dve):
                steps = [0]

                def step(ins):
                    steps[0] += 1
                    ins.then_inc(prep_step, 1)
                    dve.wait_ge(prep_step, steps[0])

                dve.wait_ge(edges_in, 32)
                step(dve.tensor_copy(ef, ei))
                dve.tensor_scalar(src_tile, srcf, 1.0 / B, 0.5 / B - 0.5, ALU.mult, ALU.add)
                step(dve.tensor_scalar(window, dstf, 1.0 / W, 0.5 / W - 0.5, ALU.mult, ALU.add))
                dve.tensor_scalar(src_tile, src_tile, MAGIC, MAGIC, ALU.add, ALU.subtract)
                step(dve.tensor_scalar(window, window, MAGIC, MAGIC, ALU.add, ALU.subtract))
                dve.scalar_tensor_tensor(out=key[0], in0=src_tile, scalar=-float(B), in1=srcf, op0=ALU.mult, op1=ALU.add)
                step(dve.scalar_tensor_tensor(out=key[1], in0=src_tile, scalar=float(W), in1=dstf,
                                              op0=ALU.mult, op1=ALU.add))
                step(dve.scalar_tensor_tensor(out=key[0], in0=window, scalar=128.0, in1=key[0],
                                              op0=ALU.mult, op1=ALU.add))
                dst4 = dstf.rearrange("p (q e) -> p q e", q=TQ)
                dve.tensor_reduce(mm[:, 0:TQ], dst4, AX_X, ALU.min)
                step(dve.tensor_reduce(mm[:, TQ:], dst4, AX_X, ALU.max))
                dve.wait_ge(consts, 6)
                for k in range(2 * TQ):
                    last = dve.tensor_scalar(mmb[:, k * B:(k + 1) * B], ones[0:TP, 0:B], mm[:, k:k + 1], None, ALU.mult)
                step(last)
                dve.wait_ge(consts2, 4)
                dve.wait_ge(turned, 5)
                low, high = PS[3][0:B, 0:ET], PS[4][0:B, 0:ET]
                for k, (parts, _) in enumerate(PARTS):
                    width, most = (W, KA) if k < 2 else (B, KE)
                    f = (first[0:parts, k:k + 1] if k < 2 else firstj[0:parts, :])
                    e = ends[0:parts, 4 * k:4 * k + 4]
                    c0, c1, c2 = (c[0:parts, :] for c in cover)
                    step(dve.tensor_scalar(e[:, 3:4], f, float(width - 1), None, ALU.add))
                    step(dve.tensor_scalar(c0, low[0:parts], e[:, 3:4], None, ALU.is_le))
                    step(dve.scalar_tensor_tensor(out=c0, in0=high[0:parts], scalar=f, in1=c0,
                                                  op0=ALU.is_ge, op1=ALU.mult))
                    dve.scalar_tensor_tensor(out=c1, in0=tnum[0:parts], scalar=1.0, in1=c0, op0=ALU.add, op1=ALU.mult)
                    step(dve.scalar_tensor_tensor(out=c2, in0=tnum[0:parts], scalar=-BIG, in1=c0,
                                                  op0=ALU.add, op1=ALU.mult))
                    dve.tensor_reduce(e[:, 1:2], c1, AX_X, ALU.max)
                    step(dve.tensor_reduce(e[:, 0:1], c2, AX_X, ALU.min))
                    step(dve.tensor_scalar(e[:, 0:1], e[:, 0:1], BIG, float(ET - most), ALU.add, ALU.min))
                    step(dve.tensor_tensor(e[:, 1:2], e[:, 1:2], e[:, 0:1], ALU.subtract))
                    step(dve.tensor_scalar(e[:, 1:2], e[:, 1:2], float(most), None, ALU.is_gt))
                dve.wait_ge(turned, 6)
                dve.tensor_copy(vec[:], PS[5][:, 400:400 + NVEC]).then_inc(taken, 1)
                dve.wait_ge(taken, 1)
                dve.wait_ge(rows_done, 1)
                step(dve.tensor_copy(trow, PS[5][0:1, 0:NW + T]))
                dve.sem_inc(rows_read, 1)
                dve.tensor_copy(rows_i[0:1, 0:T], trow[:, NW:NW + T])
                dve.wait_ge(rows_done, 2)
                step(dve.tensor_reduce(flag_f, PS[4][0:1, 0:NW + T], AX_X, ALU.max))
                dve.tensor_copy(rows_i[0:1, flag_at:flag_at + 1], flag_f)
                dve.wait_ge(consts2, 9)
                dve.wait_ge(rows_done, 3)
                dve.tensor_tensor(tile_of.rearrange("p (w i) -> p w i", i=KA), kofs.rearrange("p (w i) -> p w i", i=KA),
                                  PS[3][0:TP, 0:NW].unsqueeze(2).to_broadcast([TP, NW, KA]), ALU.add)
                step(dve.tensor_tensor(tile_e.rearrange("p (w i) -> p w i", i=KE), kofs_e.rearrange("p (w i) -> p w i", i=KE),
                                       PS[3][0:TP, NW:NW + T].unsqueeze(2).to_broadcast([TP, T, KE]), ALU.add))
                for q in range(TQ):
                    dve.tensor_scalar(pick[q], tile_of, float(q), None, ALU.is_equal)
                    dve.tensor_scalar(pick_e[q], tile_e, float(q), None, ALU.is_equal).then_inc(picks_ready, 1)
                for k in range(2):
                    for h in range(2):
                        n = 2 * k + h
                        dve.wait_ge(gathered, n + 1)
                        dve.tensor_copy(ka[:, k, h * half:(h + 1) * half], PS[n % 2][0:B, 0:half]).then_inc(gather_taken, 1)
                dve.wait_ge(gathered, 5)
                dve.tensor_tensor(ke[:, 0:T * KE].rearrange("e (j i) -> e j i", i=KE),
                                  jkey[:].unsqueeze(2).to_broadcast([B, T, KE]),
                                  PS[2][0:B, 0:T * KE].rearrange("e (j i) -> e j i", i=KE), ALU.subtract).then_inc(gather_taken, 1)
                dve.wait_ge(gather_taken, 5)
                for k in range(2):
                    kw = ka[:, k, :].rearrange("e (w i) -> e w i", i=KA)
                    dve.tensor_tensor(kw, kw, wkey[:, k, :].unsqueeze(2).to_broadcast([B, NW, KA]), ALU.subtract)
                bi, bh = vcol["L3_gnn_gru_bih"], vcol["L3_gnn_gru_bhh"]
                dve.tensor_tensor(gbias[:], vec[:, bi:bi + 2], vec[:, bh:bh + 2], ALU.add)
                dve.tensor_scalar(center[:], ident[:], 1.0 / 128, None, ALU.subtract)

            @block.scalar
            def _(act):
                for n in VECS:
                    k = 3 if "gru" in n else 1
                    act.dma_start(vraw[vcol[n]:vcol[n] + k, :], a[n].rearrange("(k f) -> k f", k=k)).then_inc(vecs_in, 16)
                for k in range(3):
                    act.wait_ge(turned, k + 1)
                    to = tab[:, k, :].rearrange("e (p q) -> e q p", q=TQ)
                    act.activation(to, PS[k][0:B, 0:TQ * TP].rearrange("e (q p) -> e q p", q=TQ), ACT.Copy).then_inc(wtaken, 1)
                for i, (g, k) in enumerate(wgroups):
                    act.wait_ge(wturned, i + 1)
                    act.activation(wT[:, g:g + k, :], mps[i % 2][:, 0:128 * k].rearrange("p (k o) -> p k o", k=k),
                                   ACT.Copy).then_inc(wtaken, 1)

            @block.tensor
            def _(pe):
                pe.wait_ge(consts, 6)
                pe.wait_ge(prep_step, 7)
                for k in range(3):
                    for q in range(TQ):
                        last = pe.transpose(PS[k][0:B, q * TP:(q + 1) * TP], key[k][:, q * B:(q + 1) * B], ident[0:TP, 0:TP])
                    last.then_inc(turned, 1)
                for k in range(2):
                    for q in range(TQ):
                        n = TQ * k + q
                        last = pe.matmul(PS[3 + k][0:B, q * TP:(q + 1) * TP], mmb[:, n * B:(n + 1) * B],
                                         ident[0:TP, 0:TP], start=True, stop=True)
                    last.then_inc(turned, 1)
                pe.wait_ge(vecs_in, 32 + 16 * len(VECS))
                pe.transpose(PS[5][:, 400:400 + NVEC], vraw, ident[0:NVEC, 0:NVEC]).then_inc(turned, 1)
                pe.wait_ge(weights_in, 16 * len(WT))
                for i, (g, k) in enumerate(wgroups):
                    if i >= 2:
                        pe.wait_ge(wtaken, 3 + i - 1)
                    for j in range(k):
                        last = pe.transpose(mps[i % 2][:, 128 * j:128 * (j + 1)], wT[:, g + j, :], ident[:])
                    last.then_inc(wturned, 1)
                pe.wait_ge(taken, 1)
                for k, (parts, col) in enumerate(PARTS):
                    last = pe.transpose(PS[5][0:1, col:col + parts], ends[0:parts, 4 * k:4 * k + 1], ident[0:parts, 0:parts])
                last.then_inc(rows_done, 1)
                for k, (parts, col) in enumerate(PARTS):
                    last = pe.transpose(PS[4][0:1, col:col + parts], ends[0:parts, 4 * k + 1:4 * k + 2],
                                        ident[0:parts, 0:parts])
                last.then_inc(rows_done, 1)
                pe.wait_ge(rows_read, 1)
                pe.matmul(PS[3][0:TP, 0:NW + T], ones[0:1, 0:TP], trow, start=True, stop=True).then_inc(rows_done, 1)
                pe.wait_ge(picks_ready, TQ)
                pe.wait_ge(wtaken, 3)
                for k in range(2):
                    for h in range(2):
                        n = 2 * k + h
                        if n >= 2:
                            pe.wait_ge(gather_taken, n - 1)
                        for q in range(TQ):
                            last = pe.matmul(PS[n % 2][0:B, 0:half], key[k][:, q * B:(q + 1) * B],
                                             pick[q][:, h * half:(h + 1) * half], start=(q == 0), stop=(q == TQ - 1))
                        last.then_inc(gathered, 1)
                for q in range(TQ):
                    last = pe.matmul(PS[2][0:B, 0:T * KE], key[2][:, q * B:(q + 1) * B], pick_e[q],
                                     start=(q == 0), stop=(q == TQ - 1))
                last.then_inc(gathered, 1)

        wk = ExitStack()
        moving = sb("moving", [B, RING, MW], F16, wk)
        within = sb("within", [B, RING, 126], F16, wk)
        efeat = sb("efeat", [B, KE, 128], F32, wk)
        edst = sb("edst", [B, KE, B], F32, wk)
        stage = sb("stage", [128, 2, B], F32, wk)
        kg = sb("kg", [B, 3], F32, wk)

        moving_ready, within_ready, pair_free = sem("moving_ready"), sem("within_ready"), sem("pair_free")
        win_taken = sem("win_taken")
        efeat_in = [sem(f"efeat_in{q}") for q in range(EQ)]
        distance, edst_ready, echunk_free = sem("distance"), sem("edst_ready"), sem("echunk_free")
        esum_taken, sums_out, stage_free = sem("esum_taken"), sem("sums_out"), sem("stage_free")
        ORDER = [("w", 0), ("w", 1), ("e", 0), ("w", 2), ("w", 3), ("e", 1), ("w", 4), ("w", 5), ("e", 2), ("w", 6), ("e", 3)]
        AHEAD = [("e", 2), ("w", 0), ("w", 1), ("e", 3), ("w", 2), ("w", 3), ("e", 4), ("w", 4), ("w", 5), ("e", 5), ("w", 6), ("s", 0)]
        win_bank = [PS[0], PS[1], PS[2], PS[3], PS[6], PS[7], PS[3]]
        win_before = [1, 2, 3, 7, 7, 7, 11]

        with nc.Block() as block:
            @block.sync
            def _(sp):
                with sp.Fori(0, T // UNROLL) as jj:
                    for r in range(UNROLL):
                        j = UNROLL * jj + r
                        t0 = sp.value_load(rows_i[0:1, bass.ds(j, 1)], min_val=0, max_val=ET - KE)
                        for q, k in enumerate(KES):
                            sp.wait_ge(echunk_free, EQ * j + q + 1)
                            sp.dma_start(efeat[:, KOFF[q]:KOFF[q] + k, :],
                                         a["edge_attr_128"][bass.ds((t0 + KOFF[q]) * B, k * B), :]
                                         .rearrange("(i p) f -> p i f", p=B)).then_inc(efeat_in[q], 16)

            @block.vector
            def _(dve):
                with dve.Fori(0, T // UNROLL) as jj:
                    for r in range(UNROLL):
                        j = UNROLL * jj + r
                        for kind, n in ORDER:
                            if kind == "w":
                                for i in range(KA):
                                    l = KA * (WPJ * r + n) + i
                                    g = KA * (WPJ * j + n) + i
                                    dve.wait_ge(pair_free, g + 1)
                                    dve.tensor_scalar(within[:, l % RING, 0:B], iota_m[:, 0:B], ka[:, 0, bass.ds(g, 1)], None,
                                                      ALU.is_equal).then_inc(within_ready, 1)
                                    dve.tensor_scalar(moving[:, l % RING, :], iota_m[:], ka[:, 1, bass.ds(g, 1)], None,
                                                      ALU.is_equal).then_inc(moving_ready, 1)

            @block.gpsimd
            def _(pool):
                pool.sem_inc(stage_free, 1)
                with pool.Fori(0, T) as j:
                    pool.wait_ge(esum_taken, 2 * j + 3)
                    pool.dma_start(sums[:, bass.ds(j * B, B)], stage[:, 0, :]).then_inc(sums_out, 16)
                    pool.dma_start(degs[:, bass.ds(j * B, B)], stage[0:1, 1, :]).then_inc(sums_out, 16)
                    pool.wait_ge(sums_out, 32 * j + 32)
                    pool.sem_inc(stage_free, 1)

            @block.tensor
            def _(pe):
                pe.sem_inc(pair_free, RING)
                pe.sem_inc(echunk_free, EQ)
                with pe.Fori(0, T // UNROLL) as jj:
                    for r in range(UNROLL):
                        j = UNROLL * jj + r
                        for kind, n in ORDER:
                            if kind == "w":
                                pe.wait_ge(win_taken, WPJ * j + win_before[n])
                                for i in range(KA):
                                    l = KA * (WPJ * r + n) + i
                                    g = KA * (WPJ * j + n) + i
                                    pe.wait_ge(moving_ready, g + 1)
                                    pe.matmul(win_bank[n][0:B, 0:MW], within[:, l % RING, 0:B], moving[:, l % RING, :],
                                              start=(i == 0), stop=(i == KA - 1)).then_inc(pair_free, 1)
                            else:
                                if n == 0:
                                    pe.wait_ge(esum_taken, 2 * j + 1)
                                pe.wait_ge(efeat_in[n], 16 * (j + 1))
                                pe.wait_ge(edst_ready, EQ * j + n + 1)
                                hot16 = edst[:].bitcast(BF16).rearrange("p i (d h) -> p i d h", h=2)
                                for i in range(KES[n]):
                                    first_, last_ = (n == 0 and i == 0), (n == EQ - 1 and i == KES[n] - 1)
                                    pe.matmul(PS[4][:, 0:B], efeat[:, KOFF[n] + i, :], edst[:, KOFF[n] + i, :], start=first_, stop=last_)
                                    mmd = pe.matmul(PS[5][0:1, 0:B], ones_bf[:], hot16[:, KOFF[n] + i, :, 1], start=first_, stop=last_)
                                mmd.then_inc(echunk_free, 1)

            @block.scalar
            def _(act):
                act.sem_inc(win_taken, WPJ)
                act.sem_inc(esum_taken, 1)

                def edge_hot(j, n):
                    m = EQ * j + n
                    hot = edst[:, KOFF[n]:KOFF[n] + KES[n], :]
                    act.wait_ge(echunk_free, m + 1)
                    for i in range(KES[n]):
                        last = act.activation(hot[:, i, :], iota_m[:, 0:B], ACT.Square, bias=ke[:, bass.ds(KE * j + KOFF[n] + i, 1)])
                    last.then_inc(distance, 1)
                    act.wait_ge(distance, m + 1)
                    act.activation(hot, hot, ACT.Relu, scale=-1.0, bias=ones[0:B, 0:1]).then_inc(edst_ready, 1)

                edge_hot(0, 0)
                edge_hot(0, 1)
                with act.Fori(0, T // UNROLL) as jj:
                    for r in range(UNROLL):
                        j = UNROLL * jj + r
                        for kind, n in AHEAD:
                            if kind == "e":
                                edge_hot(j + n // EQ, n % EQ)
                            elif kind == "s":
                                act.wait_ge(echunk_free, EQ * j + 2 * EQ)
                                act.wait_ge(stage_free, j + 1)
                                act.activation(stage[:, 0, :], PS[4][:, 0:B], ACT.Copy).then_inc(esum_taken, 1)
                                act.activation(stage[0:1, 1, :], PS[5][0:1, 0:B], ACT.Copy).then_inc(esum_taken, 1)
                            else:
                                act.wait_ge(pair_free, KA * (WPJ * j + n + 1) + RING)
                                act.activation(adj3[:, :, bass.ds((j * WPJ + n) * W, W)],
                                               win_bank[n][0:B, 0:MW].rearrange("p (c d) -> p c d", c=T),
                                               ACT.Copy).then_inc(win_taken, 1)

        pair_keys, pair_hot, pair_used = sem("pair_keys"), sem("pair_hot"), sem("pair_used")
        all_done, all_taken = sem("all_done"), sem("all_taken")
        efeat1_in, ekey1, ehot1, epair_used = sem("efeat1_in"), sem("ekey1"), sem("ehot1"), sem("epair_used")
        esum1_done, esum1_taken, sums1_out = sem("esum1_done"), sem("esum1_taken"), sem("sums1_out")

        spare = efeat[:, 1:KE].rearrange("p i f -> p (i f)")
        tab_g = spare[:, 0:3 * ET].rearrange("p (k t) -> p k t", k=3)
        wkey_g = spare[:, 3 * ET:3 * ET + 2 * NW].rearrange("p (k w) -> p k w", k=2)
        zero = spare[:, 3 * ET + 2 * NW:3 * ET + 2 * NW + MW // 2]
        tables_in, tables_made = sem("tables_in"), sem("tables_made")

        def general(eng):
            flag = eng.value_load(rows_i[0:1, flag_at:flag_at + 1], min_val=0, max_val=1)
            return eng.If(flag == 1)

        with nc.Block() as block:
            @block.sync
            def _(sp):
                with general(sp):
                    sp.dma_start(spare[:, 0:3 * ET], tabs).then_inc(tables_in, 16)
                    with sp.Fori(0, T) as j:
                        with sp.Fori(0, ET) as t:
                            sp.wait_ge(epair_used, ET * j + t + 1)
                            sp.dma_start(efeat[:, 0, :],
                                         a["edge_attr_128"][bass.ds(t * B, B), :]).then_inc(efeat1_in, 16)

            @block.gpsimd
            def _(pool):
                with general(pool):
                    pool.memset(zero, 0.0).then_inc(tables_made, 1)
                    for k, step in enumerate((128, W)):
                        pool.iota(wkey_g[:, k, :], pattern=[[step, NW]], base=0, channel_multiplier=0,
                                  allow_small_or_imprecise_dtypes=True).then_inc(tables_made, 1)

            @block.vector
            def _(dve):
                with general(dve):
                    dve.wait_ge(tables_in, 16)
                    dve.wait_ge(tables_made, 3)
                    with dve.Fori(0, NW) as w:
                        with dve.Fori(0, ET) as t:
                            n = ET * w + t
                            dve.wait_ge(pair_used, n + 1)
                            dve.tensor_tensor(kg[:, 0:2].unsqueeze(2), tab_g[:, 0:2, bass.ds(t, 1)],
                                              wkey_g[:, :, bass.ds(w, 1)], ALU.subtract).then_inc(pair_keys, 1)
                            dve.wait_ge(pair_keys, n + 1)
                            dve.tensor_scalar(within[:, 0, 0:B], iota_m[:, 0:B], kg[:, 0:1], None,
                                              ALU.is_equal).then_inc(pair_hot, 1)
                            dve.tensor_scalar(moving[:, 0, :], iota_m[:], kg[:, 1:2], None,
                                              ALU.is_equal).then_inc(pair_hot, 1)
                            dve.wait_ge(pair_hot, 2 * n + 2)
                    with dve.Fori(0, T) as j:
                        with dve.Fori(0, ET) as t:
                            n = ET * j + t
                            dve.wait_ge(epair_used, n + 1)
                            dve.tensor_scalar(kg[:, 2:3], tab_g[:, 2, bass.ds(t, 1)], jkey[:, bass.ds(j, 1)], None,
                                              ALU.subtract).then_inc(ekey1, 1)
                            dve.wait_ge(ekey1, n + 1)
                            dve.tensor_scalar(edst[:, 0, :], iota_m[:, 0:B], kg[:, 2:3], None,
                                              ALU.is_equal).then_inc(ehot1, 1)
                            dve.wait_ge(ehot1, n + 1)

            @block.tensor
            def _(pe):
                z16, zbf = zero.bitcast(F16), zero.bitcast(BF16)
                with general(pe):
                    pe.wait_ge(tables_made, 3)
                    pe.sem_inc(pair_used, 1)
                    pe.sem_inc(epair_used, 1)
                    with pe.Fori(0, NW) as w:
                        pe.wait_ge(all_taken, w + 1)
                        pe.matmul(PS[0][0:B, 0:MW], z16[:, 0:B], z16[:, 0:MW], start=True, stop=False)
                        with pe.Fori(0, ET) as t:
                            pe.wait_ge(pair_hot, 2 * (ET * w + t) + 2)
                            pe.matmul(PS[0][0:B, 0:MW], within[:, 0, 0:B], moving[:, 0, :],
                                      start=False, stop=False).then_inc(pair_used, 1)
                        pe.matmul(PS[0][0:B, 0:MW], z16[:, 0:B], z16[:, 0:MW], start=False,
                                  stop=True).then_inc(all_done, 1)
                    with pe.Fori(0, T) as j:
                        pe.wait_ge(esum1_taken, 2 * j + 1)
                        pe.matmul(PS[4][:, 0:B], zero[:, 0:128], zero[:, 0:B], start=True, stop=False)
                        pe.matmul(PS[5][0:1, 0:B], zbf[:, 0:1], zbf[:, 0:B], start=True, stop=False)
                        with pe.Fori(0, ET) as t:
                            n = ET * j + t
                            pe.wait_ge(ehot1, n + 1)
                            pe.wait_ge(efeat1_in, 16 * n + 16)
                            pe.matmul(PS[4][:, 0:B], efeat[:, 0, :], edst[:, 0, :], start=False, stop=False)
                            hot16 = edst[:, 0, :].bitcast(BF16).rearrange("p (d h) -> p d h", h=2)
                            pe.matmul(PS[5][0:1, 0:B], ones_bf[:], hot16[:, :, 1], start=False,
                                      stop=False).then_inc(epair_used, 1)
                        pe.matmul(PS[4][:, 0:B], zero[:, 0:128], zero[:, 0:B], start=False, stop=True)
                        pe.matmul(PS[5][0:1, 0:B], zbf[:, 0:1], zbf[:, 0:B], start=False, stop=True).then_inc(esum1_done, 1)

            @block.scalar
            def _(act):
                with general(act):
                    act.sem_inc(all_taken, 1)
                    act.sem_inc(esum1_taken, 1)
                    with act.Fori(0, NW) as w:
                        act.wait_ge(all_done, w + 1)
                        act.activation(adj3[:, :, bass.ds(w * W, W)],
                                       PS[0][0:B, 0:MW].rearrange("p (c d) -> p c d", c=T),
                                       ACT.Copy).then_inc(all_taken, 1)
                    with act.Fori(0, T) as j:
                        act.wait_ge(esum1_done, j + 1)
                        act.activation(stage[:, 0, :], PS[4][:, 0:B], ACT.Copy).then_inc(esum1_taken, 1)
                        act.activation(stage[0:1, 1, :], PS[5][0:1, 0:B], ACT.Copy).then_inc(esum1_taken, 1)
                        act.wait_ge(esum1_taken, 2 * j + 3)
                        act.dma_start(sums[:, bass.ds(j * B, B)], stage[:, 0, :]).then_inc(sums1_out, 16)
                        act.dma_start(degs[:, bass.ds(j * B, B)], stage[0:1, 1, :]).then_inc(sums1_out, 16)
                        act.wait_ge(sums1_out, 32 * j + 32)
        wk.close()
        build.close()
        layers(nc, ctx, sb, sem, a, out, locals())


def layers(nc, ctx, sb, sem, a, out, env):
    adj3, wT, w0, conv, vec, slot, vcol = (env[k] for k in ("adj3", "wT", "w0", "conv", "vec", "slot", "vcol"))
    gbias, ident, center, mean, ones, epsc = (env[k] for k in ("gbias", "ident", "center", "mean", "ones", "epsc"))
    acc, gate, mps = (env[k] for k in ("acc", "gate", "mps"))
    sums, degs, rdegs, x1s, x3s = (env[k] for k in ("sums", "degs", "rdegs", "x1s", "x3s"))

    hT = sb("hT", [128, NPAD], F32)
    msg = sb("msg", [B, T, 2, 128], F16)
    x_in = msg[:].rearrange("p s h f -> p (s h f)").bitcast(F32).rearrange("p (s f) -> p s f", s=T)
    buf = [sb(f"chunk{i}", [128, CW], F32) for i in range(10)]
    small = sb("small", [SW, 2, 2, 4], F32)
    dg = buf[9][0:B, 0:3 * T].rearrange("p (k e) -> p k e", k=3)
    rd = buf[0:2]
    esum = buf[2:4]
    norm_sq, norm_dev, norm_diag = (buf[2], buf[5]), (buf[3], buf[6]), (buf[4], buf[7])
    va = buf[8:10]
    v1, v2, res = buf[8], buf[9], buf[4]
    hid, relu_h, sigm, res3 = buf[0:2], buf[4:6], buf[6:8], buf[8:10]
    agg16, h16 = ([b[:].bitcast(F16).rearrange("p (h d) -> p h d", h=2) for b in bs] for bs in (buf[0:2], buf[6:8]))
    gr, gz, gt, gn = buf[2:6]
    g0, gcols = slot["L3_gnn_gru_wih"], 6 * 128
    w32 = wT[:, g0:g0 + 6, :].rearrange("p k o -> p (k o)")
    w16 = w32.bitcast(F16).rearrange("p (h o) -> p h o", h=2)
    w_parts = [b[:].bitcast(F16)[:, 0:gcols] for b in buf[6:8]]
    assert slot["L3_gnn_gru_whh"] == g0 + 3 and gcols <= 2 * CW

    def col(name, k=0):
        return vec[:, vcol[name] + k:vcol[name] + k + 1]

    def w(name, k=0):
        return wT[:, slot[name] + k, :]

    def cols(t, c):
        return t[:, c * CW:(c + 1) * CW]

    pad_zero, x_loaded, xT_done, xT_taken = sem("pad_zero"), sem("x_loaded"), sem("xT_done"), sem("xT_taken")
    degs_in, rdeg_step, rdegs_out = sem("degs_in"), sem("rdeg_step"), sem("rdegs_out")
    w_split, own_hi, own_lo = sem("w_split"), sem("own_hi"), sem("own_lo")
    m_done, hi_ready, lo_ready = sem("m_done"), sem("hi_ready"), sem("lo_ready")
    acc_done, acc_free, own_done, self_free = sem("acc_done"), sem("acc_free"), sem("own_done"), sem("self_free")
    rd_in, e_in = [sem("rd_in0"), sem("rd_in1")], [sem("e_in0"), sem("e_in1")]
    res_in, res3_in = sem("res_in"), [sem("res3_in0"), sem("res3_in1")]
    scaled, mixed, mixed2, summed, leaked = sem("scaled"), sem("mixed"), sem("mixed2"), sem("summed"), sem("leaked")
    act_ready, u_ready = sem("act_ready"), [sem("u_ready0"), sem("u_ready1")]

    def pair(name):
        return [sem(name + "0"), sem(name + "1")]
    center_done, sq_ready, dev_ready, var_done = pair("center_done"), pair("sq_ready"), pair("dev_ready"), pair("var_done")
    std_ready, rstd_ready, diag_ready = pair("std_ready"), pair("rstd_ready"), pair("diag_ready")
    spread_done, normed = pair("spread_done"), pair("normed")
    h_ready = sem("h_ready")
    x1_out, x3_out = sem("x1_out"), [sem(f"x3_out{c}") for c in range(NC)]
    enc1_done, enc1_ready, enc2_done = sem("enc1_done"), sem("enc1_ready"), sem("enc2_done")
    agg_hi, agg_ready, gates_done, r_ready, z_ready = sem("agg_hi"), sem("agg_ready"), sem("gates_done"), sem("r_ready"), sem("z_ready")
    inner1, inner2, n_ready, diff1, diff2 = sem("inner1"), sem("inner2"), sem("n_ready"), sem("diff1"), sem("diff2")
    relu_ready, dec1_done, dec1_ready, dec2_done = sem("relu_ready"), sem("dec1_done"), sem("dec1_ready"), sem("dec2_done")
    sig_ready, outT_done, out_taken, out_stored = sem("sig_ready"), sem("outT_done"), sem("out_taken"), sem("out_stored")

    def wait_if(eng, s, n):
        if n > 0:
            eng.wait_ge(s, n)

    NORMS = {"x1": 0, "x2": NC, "x3": 2 * NC}
    WRITES = {"h1": 0, "enc": NC, "dec": (2 + STEPS) * NC}

    def await_h(eng, version, c):
        if not isinstance(version, (str, int)):
            eng.wait_ge(h_ready, version * NC + WRITES["enc"] + c + 1)
        elif version in NORMS:
            eng.wait_ge(normed[1], NORMS[version] + c + 1)
        elif version in WRITES:
            eng.wait_ge(h_ready, WRITES[version] + c + 1)
        else:
            eng.wait_ge(h_ready, version * NC + WRITES["enc"] + c + 1)

    def norm0(c):
        return 0, c

    def norm1(app, c):
        return 1, NC * (0, None, 1, 2)[app] + c

    def norm_last(c):
        return c % 2, (1 + 2 * (c % 2)) * NC + c // 2

    groups = [(4 * g, min(4, T - 4 * g)) for g in range(MG)]

    def last_chunk(g):
        return min(NC - 1, (B * sum(groups[g]) - 1) // CW)
    turned_with = [[g for g in range(MG) if last_chunk(g) == c] for c in range(NC)]

    DRAIN0 = "C c m0 V v m1 S s m2 C m3 V m4 S m5 m6".split()
    DRAIN = "m0 m1 C m2 V m3 S m4 m5 m6".split()

    with nc.Block() as block:
        @block.sync
        def _(sp):
            sp.dma_start(x_in, a["x"].rearrange("(s p) f -> p s f", p=B)).then_inc(x_loaded, 16)
            sp.dma_start(dg[:, 0, :], degs[0:1, 0:N].rearrange("o (p e) -> (o p) e", p=B)).then_inc(degs_in, 16)
            sp.wait_ge(rdeg_step, 3)
            sp.dma_start(rdegs[0:1, 0:N].rearrange("o (p e) -> (o p) e", p=B), dg[:, 0, :]).then_inc(rdegs_out, 16)
            sp.wait_ge(rdegs_out, 16)

            def load(app, c):
                n, b = NC * app + c, c % 2
                wait_if(sp, acc_free, n - 1)
                sp.dma_start(rd[b][:], rdegs[0:1, c * CW:(c + 1) * CW].to_broadcast([128, CW])).then_inc(rd_in[b], 16)
                if app in (1, 2):
                    wait_if(sp, acc_done, n - 1)
                    if app == 1 and c == 0:
                        await_h(sp, "x1", NC - 1)
                    sp.dma_start(esum[b][:], cols(sums, c)).then_inc(e_in[b], 16)
                if app == 2:
                    if c == 0:
                        sp.wait_ge(x1_out, 16 * NC)
                    wait_if(sp, u_ready[1], NC + c)
                    sp.dma_start(res[:], cols(x1s, c)).then_inc(res_in, 16)

            def store(dst, version, c, done):
                await_h(sp, version, c)
                sp.dma_start(cols(dst, c), cols(hT, c)).then_inc(done, 16)

            for c in range(NC):
                load(0, c)
                if c >= 4:
                    store(x1s, "x1", c - 4, x1_out)
            for c in range(NC - 4, NC):
                store(x1s, "x1", c, x1_out)
            for app in (1, 2, 3):
                for c in range(NC):
                    load(app, c)
            for c in range(NC):
                store(x3s, "x3", c, x3_out[c])
            for c in range(NC):
                sp.wait_ge(x3_out[c], 16)
            for c in range(NC):
                sp.wait_ge(h_ready, WRITES["dec"] + max(0, c - 1))
                sp.dma_start(res3[c % 2][:], cols(x3s, c)).then_inc(res3_in[c % 2], 16)
            for g, (s0, k) in enumerate(groups):
                sp.wait_ge(out_taken, g + 1)
                sp.dma_start(out[B * s0:B * (s0 + k), :].rearrange("(s p) f -> p s f", p=B),
                             x_in[:, s0:s0 + k, :]).then_inc(out_stored, 16)
            sp.wait_ge(out_stored, 16 * MG)

        @block.tensor
        def _(pe):
            def message(app, rhs, version, g):
                s0, k = groups[g]
                if version is not None:
                    await_h(pe, version, last_chunk(g))
                elif g == 0:
                    pe.wait_ge(xT_taken, MG)
                    pe.wait_ge(pad_zero, 1)
                if g >= 2:
                    pe.wait_ge(lo_ready, MG * app + g - 1)
                for s in range(s0, s0 + k):
                    last = pe.matmul(mps[g % 2][0:B, 128 * (s - s0):128 * (s - s0 + 1)],
                                     hT[:, B * s:B * (s + 1)], rhs, start=True, stop=True)
                last.then_inc(m_done, 1)

            def neighbours(app, c, hooks={}, tail=None):
                b = c % 2
                if isinstance(app, int):
                    wait_if(pe, acc_free, NC * app + c - 1)
                else:
                    pe.wait_ge(agg_ready, NC * (app - 4) + c + 1)
                for s in range(T):
                    for hook in hooks.get(s, []):
                        hook()
                    if c == 0 and s % 4 == 0:
                        pe.wait_ge(lo_ready, MG * app + s // 4 + 1)
                    rhs = adj3[:, s, c * CW:(c + 1) * CW]
                    pe.matmul(acc[b][:, 0:CW], msg[:, s, 0, :], rhs, start=(s == 0), stop=False)
                    last = pe.matmul(acc[b][:, 0:CW], msg[:, s, 1, :], rhs, start=False,
                                     stop=(s == T - 1 and tail is None))
                if tail:
                    last = tail()
                last.then_inc(acc_done, 1)

            def centered(norm, u):
                st, n = norm
                wait_if(pe, dev_ready[st], n)
                pe.matmul(gate[2 * st][:, 0:CW], center[:], u, start=True, stop=True).then_inc(center_done[st], 1)

            def variance(norm):
                st, n = norm
                pe.wait_ge(sq_ready[st], n + 1)
                wait_if(pe, normed[st], n)
                for i in range(4):
                    last = pe.matmul(gate[2 * st + 1][0:SW, i:i + 1], norm_sq[st][:, SW * i:SW * (i + 1)], mean[:],
                                     start=True, stop=True)
                last.then_inc(var_done[st], 1)

            def spread(norm):
                st, n = norm
                pe.wait_ge(diag_ready[st], n + 1)
                pe.matmul(gate[2 * st + 1][:, 0:CW], ones[0:SW, :], norm_diag[st][0:SW, :],
                          start=True, stop=True).then_inc(spread_done[st], 1)

            pe.wait_ge(x_loaded, 16)
            for g, (s0, k) in enumerate(groups):
                if g >= 2:
                    pe.wait_ge(xT_taken, g - 1)
                for s in range(s0, s0 + k):
                    last = pe.transpose(mps[g % 2][:, B * (s - s0):B * (s - s0 + 1)], x_in[:, s, :], ident[0:B, 0:B])
                last.then_inc(xT_done, 1)

            for g in range(MG):
                message(0, w0[:], None, g)

            def first_center(c):
                pe.wait_ge(u_ready[0], c + 1)
                centered(norm0(c), va[c % 2][:])

            def second_center(app, c):
                pe.wait_ge(u_ready[1], norm1(app, c)[1] + 1)
                centered(norm1(app, c), (cols(hT, c) if app == 0 else v1[:]))

            def hooks0(c):
                hooks = {}
                if c >= 2:
                    hooks.update({1: [lambda: second_center(0, c - 2)], 5: [lambda: variance(norm1(0, c - 2))],
                                  15: [lambda: spread(norm1(0, c - 2))]})
                if c >= 1:
                    hooks.update({4: [lambda: first_center(c - 1)], 9: [lambda: variance(norm0(c - 1))],
                                  17: [lambda: spread(norm0(c - 1))]})
                return hooks

            for c in range(NC):
                neighbours(0, c, hooks0(c))

            def drain(app, order, rhs, version):
                left = [NC - 2, NC - 1] if order is DRAIN0 else [NC - 1]
                seen = {}
                for part in order:
                    if part[0] == "m":
                        message(app, rhs, version, int(part[1]))
                        continue
                    c = NC - 1 if part.islower() else left[seen.get(part, 0)]
                    seen[part] = seen.get(part, 0) + 1
                    norm = norm0(c) if part.islower() else norm1(app - 1, c)
                    if part == "c":
                        first_center(c)
                    elif part == "C":
                        second_center(app - 1, c)
                    elif part in "Vv":
                        variance(norm)
                    else:
                        spread(norm)

            drain(1, DRAIN0, w("L1_gnn_W1_0"), "x1")

            def own(app, c):
                n, b = NC * (app - 1) + c, c % 2
                pe.wait_ge(e_in[b], 16 * (n // 2 + 1))
                wait_if(pe, self_free, n)
                if n == 0:
                    await_h(pe, "x1", NC - 1)
                for k in (2, 3):
                    last = pe.matmul(gate[k - 2][:, 0:CW], w(f"L1_gnn_W{k}_{app - 1}"), cols(hT, c), start=True, stop=True)
                return pe.matmul(acc[b][:, 0:CW], w(f"L1_gnn_W1_{app - 1}"), esum[b][:], start=False, stop=True)

            def hooks1(app, c, at):
                return {} if c == 0 else {at[0]: [lambda: second_center(app, c - 1)],
                                          at[1]: [lambda: variance(norm1(app, c - 1))],
                                          at[2]: [lambda: spread(norm1(app, c - 1))]}

            for c in range(NC):
                neighbours(1, c, {}, lambda: own(1, c))
            for g in range(MG):
                message(2, w("L1_gnn_W1_1"), "h1", g)
            for c in range(NC):
                neighbours(2, c, hooks1(2, c, (13, 17, 22)), lambda: own(2, c))
            drain(3, DRAIN, w("L2_gnn_W_neigh"), "x2")

            def own2(c):
                pe.wait_ge(self_free, 2 * NC + c)
                pe.matmul(gate[0][:, 0:CW], w("L2_gnn_W_self"), cols(hT, c), start=True, stop=True)

            for c in range(NC):
                neighbours(3, c, {**hooks1(3, c, (6, 10, 15)), 20: [lambda: own2(c)]})
            second_center(3, NC - 1)
            variance(norm1(3, NC - 1))
            spread(norm1(3, NC - 1))

            def enc1(c):
                await_h(pe, "x3", c)
                pe.matmul(gate[c % 2][:, 0:CW], w("L3_gnn_enc_w1"), cols(hT, c), start=True, stop=True).then_inc(enc1_done, 1)

            def enc2(c):
                pe.wait_ge(enc1_ready, c + 1)
                if c >= 2:
                    await_h(pe, "enc", c - 2)
                pe.matmul(gate[2 + c % 2][:, 0:CW], w("L3_gnn_enc_w2"), hid[c % 2][:],
                          start=True, stop=True).then_inc(enc2_done, 1)
            enc1(0)
            enc1(1)
            await_h(pe, "x3", NC - 1)
            for c in range(NC):
                enc2(c)
                if c + 2 < NC:
                    enc1(c + 2)

            def product16(bank, block, x, start, stop):
                for i, (hw, hx) in enumerate(((0, 0), (0, 1), (1, 0))):
                    last = pe.matmul(bank[:, 0:CW], w16[:, hw, 128 * block:128 * (block + 1)], x[:, hx, :],
                                     start=(start and i == 0), stop=(stop and i == 2))
                return last

            def gates_own(t, c):
                k = NC * t + c
                pe.wait_ge(h_ready, k + WRITES["enc"] + NC)
                pe.wait_ge(own_lo, k + 1)
                for i in range(3):
                    product16(gate[(0, 1, 3)[i]], 3 + i, h16[c % 2], True, i == 2)

            def gates(t, c):
                pe.wait_ge(agg_ready, NC * t + c + 3)
                for i in range(3):
                    last = product16(gate[i], i, agg16[c % 2], i == 2, True)
                last.then_inc(gates_done, 1)
            pe.wait_ge(w_split, 4)

            with pe.Fori(0, STEPS) as t:
                for g in range(MG):
                    message(4 + t, conv[:, bass.ds(128 * t, 128)], t, g)
                for c in range(NC):
                    neighbours(4 + t, c, {3: [lambda: gates_own(t, c - 1)], 6: [lambda: gates(t, c - 1)]} if c else {})
                gates_own(t, NC - 1)
                gates(t, NC - 1)

            def dec1(c):
                pe.wait_ge(relu_ready, c + 1)
                pe.matmul(gate[c % 2][:, 0:CW], w("L3_gnn_dec_w1"), relu_h[c % 2][:],
                          start=True, stop=True).then_inc(dec1_done, 1)

            def dec2(c):
                pe.wait_ge(dec1_ready, c + 1)
                wait_if(pe, sig_ready, c - 1)
                pe.matmul(gate[2 + c % 2][:, 0:CW], w("L3_gnn_dec_w2"), hid[c % 2][:],
                          start=True, stop=True).then_inc(dec2_done, 1)
            dec1(0)
            dec1(1)
            for c in range(NC):
                dec2(c)
                if c + 2 < NC:
                    dec1(c + 2)

            def last_center(c):
                await_h(pe, "dec", c)
                if c < 2:
                    await_h(pe, "dec", NC - 1)
                centered(norm_last(c), cols(hT, c))

            def turn(c):
                for g in turned_with[c]:
                    s0, k = groups[g]
                    for cc in (c - 1, c):
                        st, n = norm_last(cc)
                        pe.wait_ge(normed[st], n + 1)
                    if g >= 2:
                        pe.wait_ge(out_taken, g - 1)
                    for s in range(s0, s0 + k):
                        last = pe.transpose(mps[g % 2][0:B, 128 * (s - s0):128 * (s - s0 + 1)],
                                            hT[:, B * s:B * (s + 1)], ident[:])
                    last.then_inc(outT_done, 1)
            last_center(0)
            for c in range(NC):
                if c + 1 < NC:
                    last_center(c + 1)
                variance(norm_last(c))
                if c >= 1:
                    spread(norm_last(c - 1))
                if c >= 2:
                    turn(c - 2)
            spread(norm_last(NC - 1))
            turn(NC - 2)
            turn(NC - 1)

        @block.scalar
        def _(act):
            def hi(app, g):
                s0, k = groups[g]
                act.wait_ge(m_done, MG * app + g + 1)
                act.activation(msg[:, s0:s0 + k, 0, :], mps[g % 2][0:B, 0:128 * k].rearrange("p (s f) -> p s f", s=k),
                               ACT.Copy).then_inc(hi_ready, 1)

            def square(norm):
                st, n = norm
                act.wait_ge(center_done[st], n + 1)
                wait_if(act, var_done[st], n)
                act.activation(norm_sq[st][:], gate[2 * st][:, 0:CW], ACT.Square).then_inc(sq_ready[st], 1)

            def deviation(norm):
                st, n = norm
                act.wait_ge(var_done[st], n + 1)
                wait_if(act, rstd_ready[st], n)
                act.activation(small[:, st, 0, :], gate[2 * st + 1][0:SW, 0:4], ACT.Sqrt,
                               bias=epsc[0:SW, 0:1]).then_inc(std_ready[st], 1)

            def keep(norm):
                st, n = norm
                wait_if(act, normed[st], n)
                act.activation(norm_dev[st][:], gate[2 * st][:, 0:CW], ACT.Copy).then_inc(dev_ready[st], 1)

            for g, (s0, k) in enumerate(groups):
                act.wait_ge(xT_done, g + 1)
                act.activation(hT[:, B * s0:B * (s0 + k)], mps[g % 2][:, 0:B * k], ACT.Copy).then_inc(xT_taken, 1)

            for g in range(MG):
                hi(0, g)

            def gelu(c):
                act.wait_ge(normed[0], c + 1)
                act.activation(va[c % 2][:], va[c % 2][:], ACT.Gelu, bias=col("L0_gnn_beta"),
                               scale=col("L0_gnn_gamma")).then_inc(act_ready, 1)

            act.wait_ge(w_split, 4)
            for c in range(1, NC):
                norms = ([norm1(0, c - 2)] if c >= 2 else []) + [norm0(c - 1)]
                for part in (square, deviation, keep):
                    for norm in norms:
                        part(norm)
                gelu(c - 1)

            def drain(app, order):
                left = [NC - 2, NC - 1] if order is DRAIN0 else [NC - 1]
                seen = {}
                for part in order:
                    if part[0] == "m":
                        hi(app, int(part[1]))
                        continue
                    c = NC - 1 if part.islower() else left[seen.get(part, 0)]
                    seen[part] = seen.get(part, 0) + 1
                    norm = norm0(c) if part.islower() else norm1(app - 1, c)
                    if part in "Cc":
                        square(norm)
                    elif part in "Vv":
                        deviation(norm)
                        keep(norm)
                    elif part == "s":
                        gelu(c)
            drain(1, DRAIN0)
            for g in range(MG):
                hi(2, g)

            def norm_chunk(norm):
                square(norm)
                deviation(norm)
                keep(norm)
            for c in range(NC - 1):
                norm_chunk(norm1(2, c))
            drain(3, DRAIN)
            for c in range(NC):
                norm_chunk(norm1(3, c))

            def enc_in(c):
                act.wait_ge(enc1_done, c + 1)
                wait_if(act, enc2_done, c - 1)
                act.activation(hid[c % 2][:], gate[c % 2][:, 0:CW], ACT.Relu,
                               bias=col("L3_gnn_enc_b1")).then_inc(enc1_ready, 1)
            await_h(act, "x3", NC - 1)
            enc_in(0)
            for c in range(NC):
                if c + 1 < NC:
                    enc_in(c + 1)
                act.wait_ge(enc2_done, c + 1)
                act.wait_ge(x3_out[c], 16)
                act.activation(cols(hT, c), gate[2 + c % 2][:, 0:CW], ACT.Identity,
                               bias=col("L3_gnn_enc_b2")).then_inc(h_ready, 1)

            def take(t, c):
                act.wait_ge(acc_done, NC * (4 + t) + c + 1)
                act.wait_ge(h_ready, NC * t + c + WRITES["enc"] + NC - 1)
                act.activation(agg16[c % 2][:, 0, :], acc[c % 2][:, 0:CW], ACT.Copy).then_inc(agg_hi, 1)

            def split_own(t, c):
                act.wait_ge(h_ready, NC * t + c + WRITES["enc"] + NC - 1)
                act.activation(h16[c % 2][:, 0, :], cols(hT, c), ACT.Copy).then_inc(own_hi, 1)

            def gated(t, c):
                k = NC * t + c
                act.wait_ge(gates_done, k + 1)
                act.wait_ge(h_ready, k + WRITES["enc"] + NC)
                act.activation(gr[:], gate[0][:, 0:CW], ACT.Sigmoid, bias=gbias[:, 0:1]).then_inc(r_ready, 1)
                act.activation(gz[:], gate[1][:, 0:CW], ACT.Sigmoid, bias=gbias[:, 1:2]).then_inc(z_ready, 1)
                act.wait_ge(inner2, k + 1)
                act.activation(gn[:], gt[:], ACT.Tanh, bias=col("L3_gnn_gru_bih", 2)).then_inc(n_ready, 1)

            with act.Fori(0, STEPS) as t:
                for g in range(MG):
                    hi(4 + t, g)
                for c in range(NC):
                    split_own(t, c)
                    take(t, c)
                    gated(t, c)

            def dec_in(c):
                act.wait_ge(dec1_done, c + 1)
                wait_if(act, dec2_done, c - 1)
                act.activation(hid[c % 2][:], gate[c % 2][:, 0:CW], ACT.Relu,
                               bias=col("L3_gnn_dec_b1")).then_inc(dec1_ready, 1)
            dec_in(0)
            for c in range(NC):
                if c + 1 < NC:
                    dec_in(c + 1)
                act.wait_ge(dec2_done, c + 1)
                if c >= 2:
                    await_h(act, "dec", c - 2)
                act.activation(sigm[c % 2][:], gate[2 + c % 2][:, 0:CW], ACT.Sigmoid,
                               bias=col("L3_gnn_dec_b2")).then_inc(sig_ready, 1)

            await_h(act, "dec", NC - 1)
            for c in range(NC):
                norm_chunk(norm_last(c))

        @block.gpsimd
        def _(pool):
            pool.tensor_copy(w_parts[0], w32).then_inc(w_split, 1)
            pool.wait_ge(w_split, 1)
            pool.tensor_tensor(w_parts[1], w32, w_parts[0], ALU.subtract).then_inc(w_split, 1)
            pool.wait_ge(w_split, 2)
            for h in range(2):
                pool.tensor_copy(w16[:, h, :], w_parts[h]).then_inc(w_split, 1)

        @block.vector
        def _(dve):
            def lo(app, g):
                s0, k = groups[g]
                dve.wait_ge(hi_ready, MG * app + g + 1)
                dve.tensor_tensor(msg[:, s0:s0 + k, 1, :], mps[g % 2][0:B, 0:128 * k].rearrange("p (s f) -> p s f", s=k),
                                  msg[:, s0:s0 + k, 0, :], ALU.subtract).then_inc(lo_ready, 1)

            def scale_by_degree(app, c, to):
                n = NC * app + c
                dve.wait_ge(rd_in[c % 2], 16 * (n // 2 + 1))
                dve.wait_ge(acc_done, n + 1)
                dve.tensor_tensor(to, acc[c % 2][:, 0:CW], rd[c % 2][:], ALU.mult).then_inc(scaled, 1)
                dve.wait_ge(scaled, n + 1)

            def diagonal(norm):
                st, n = norm
                dve.wait_ge(std_ready[st], n + 1)
                wait_if(dve, diag_ready[st], n)
                wait_if(dve, spread_done[st], n)
                dve.reciprocal(small[:, st, 1, :], small[:, st, 0, :]).then_inc(rstd_ready[st], 1)
                dve.wait_ge(rstd_ready[st], n + 1)
                dve.tensor_tensor(norm_diag[st][0:SW, :].rearrange("p (i d) -> p i d", i=4),
                                  ident[0:SW, 0:SW].unsqueeze(1).to_broadcast([SW, 4, SW]),
                                  small[:, st, 1, :].unsqueeze(2).to_broadcast([SW, 4, SW]),
                                  ALU.mult).then_inc(diag_ready[st], 1)

            def normalised(norm, to):
                st, n = norm
                dve.wait_ge(dev_ready[st], n + 1)
                dve.wait_ge(spread_done[st], n + 1)
                dve.tensor_tensor(to, gate[2 * st + 1][:, 0:CW], norm_dev[st][:], ALU.mult).then_inc(normed[st], 1)

            dve.memset(hT[:, N:NPAD], 0.0).then_inc(pad_zero, 1)
            dve.wait_ge(degs_in, 16)
            dve.tensor_scalar(dg[:, 1, :], dg[:, 0, :], 1.0, None, ALU.max).then_inc(rdeg_step, 1)
            dve.wait_ge(rdeg_step, 1)
            dve.reciprocal(dg[:, 2, :], dg[:, 1, :]).then_inc(rdeg_step, 1)
            dve.wait_ge(rdeg_step, 2)
            dve.scalar_tensor_tensor(out=dg[:, 0, :], in0=dg[:, 0, :], scalar=0.0, in1=dg[:, 2, :],
                                     op0=ALU.is_gt, op1=ALU.mult).then_inc(rdeg_step, 1)
            for g in range(MG):
                lo(0, g)
            dve.wait_ge(w_split, 4)

            def before0(c):
                scale_by_degree(0, c, va[c % 2][:])
                dve.scalar_tensor_tensor(out=va[c % 2][:], in0=va[c % 2][:], scalar=col("L0_gnn_b"), in1=cols(hT, c),
                                         op0=ALU.add, op1=ALU.add).then_inc(u_ready[0], 1)
                dve.sem_inc(acc_free, 1)

            def residual0(c):
                dve.wait_ge(act_ready, c + 1)
                dve.tensor_tensor(cols(hT, c), va[c % 2][:], cols(hT, c), ALU.add).then_inc(u_ready[1], 1)

            for c in range(1, NC):
                before0(c - 1)
                if c >= 2:
                    diagonal(norm1(0, c - 2))
                diagonal(norm0(c - 1))
                if c >= 2:
                    normalised(norm1(0, c - 2), cols(hT, c - 2))
                normalised(norm0(c - 1), va[(c - 1) % 2][:])
                residual0(c - 1)

            def drain(app, order):
                left = [NC - 2, NC - 1] if order is DRAIN0 else [NC - 1]
                seen = {}
                for part in order:
                    if part[0] == "m":
                        lo(app, int(part[1]))
                        continue
                    c = NC - 1 if part.islower() else left[seen.get(part, 0)]
                    seen[part] = seen.get(part, 0) + 1
                    norm = norm0(c) if part.islower() else norm1(app - 1, c)
                    if part in "Vv":
                        diagonal(norm)
                    elif part == "S":
                        normalised(norm, cols(hT, c))
                    elif part == "s":
                        normalised(norm, va[c % 2][:])
                        residual0(c)
            before0(NC - 1)
            drain(1, DRAIN0)

            def chunk1(app, c):
                k = NC * (app - 1) + c
                if app == 2 and c:
                    dve.wait_ge(normed[1], norm1(2, c)[1])
                scale_by_degree(app, c, v1[:])
                r = rd[c % 2][:]
                dve.scalar_tensor_tensor(out=v2[:], in0=r, scalar=0.0, in1=gate[0][:, 0:CW],
                                         op0=ALU.is_gt, op1=ALU.mult).then_inc(mixed, 1)
                dve.scalar_tensor_tensor(out=r, in0=r, scalar=0.0, in1=gate[1][:, 0:CW],
                                         op0=ALU.is_equal, op1=ALU.mult).then_inc(self_free, 1)
                dve.wait_ge(mixed, k + 1)
                dve.tensor_tensor(v1[:], v1[:], v2[:], ALU.add).then_inc(mixed2, 1)
                dve.wait_ge(self_free, k + 1)
                dve.wait_ge(mixed2, k + 1)
                dve.tensor_tensor(v1[:], v1[:], r, ALU.add).then_inc(summed, 1)
                dve.wait_ge(summed, k + 1)
                dve.sem_inc(acc_free, 1)
                if app == 1:
                    if c == 0:
                        dve.wait_ge(x1_out, 16 * NC)
                    dve.scalar_tensor_tensor(out=cols(hT, c), in0=v1[:], scalar=LEAK, in1=v1[:],
                                             op0=ALU.mult, op1=ALU.max).then_inc(h_ready, 1)
                    dve.wait_ge(h_ready, WRITES["h1"] + c + 1)
                else:
                    dve.scalar_tensor_tensor(out=v2[:], in0=v1[:], scalar=LEAK, in1=v1[:],
                                             op0=ALU.mult, op1=ALU.max).then_inc(leaked, 1)
                    dve.wait_ge(leaked, c + 1)
                    dve.wait_ge(res_in, 16 * (c + 1))
                    dve.tensor_tensor(v1[:], v2[:], res[:], ALU.add).then_inc(u_ready[1], 1)

            for c in range(NC):
                chunk1(1, c)
            for g in range(MG):
                lo(2, g)
            for c in range(NC - 1):
                chunk1(2, c)
                diagonal(norm1(2, c))
                normalised(norm1(2, c), cols(hT, c))
            chunk1(2, NC - 1)
            drain(3, DRAIN)

            for c in range(NC):
                dve.wait_ge(normed[1], norm1(3, c)[1])
                scale_by_degree(3, c, v1[:])
                dve.scalar_tensor_tensor(out=v2[:], in0=gate[0][:, 0:CW], scalar=col("L2_gnn_b_self"), in1=v1[:],
                                         op0=ALU.add, op1=ALU.add).then_inc(self_free, 1)
                dve.wait_ge(self_free, 2 * NC + c + 1)
                dve.sem_inc(acc_free, 1)
                dve.tensor_tensor(v1[:], v2[:], cols(hT, c), ALU.add).then_inc(u_ready[1], 1)
                diagonal(norm1(3, c))
                normalised(norm1(3, c), cols(hT, c))

            def gated(t, c):
                k = NC * t + c
                dve.wait_ge(r_ready, k + 1)
                dve.scalar_tensor_tensor(out=gt[:], in0=gate[3][:, 0:CW], scalar=col("L3_gnn_gru_bhh", 2), in1=gr[:],
                                         op0=ALU.add, op1=ALU.mult).then_inc(inner1, 1)
                dve.wait_ge(inner1, k + 1)
                dve.tensor_tensor(gt[:], gt[:], gate[2][:, 0:CW], ALU.add).then_inc(inner2, 1)
                dve.wait_ge(n_ready, k + 1)
                dve.tensor_tensor(gr[:], cols(hT, c), gn[:], ALU.subtract).then_inc(diff1, 1)
                dve.wait_ge(diff1, k + 1)
                dve.wait_ge(z_ready, k + 1)
                dve.tensor_tensor(gr[:], gr[:], gz[:], ALU.mult).then_inc(diff2, 1)
                dve.wait_ge(diff2, k + 1)
                dve.tensor_tensor(cols(hT, c), gr[:], gn[:], ALU.add).then_inc(h_ready, 1)

            def low_parts(t, c):
                k = NC * t + c
                dve.wait_ge(own_hi, k + 1)
                dve.tensor_tensor(h16[c % 2][:, 1, :], cols(hT, c), h16[c % 2][:, 0, :], ALU.subtract).then_inc(own_lo, 1)
                dve.wait_ge(agg_hi, k + 1)
                dve.tensor_tensor(agg16[c % 2][:, 1, :], acc[c % 2][:, 0:CW], agg16[c % 2][:, 0, :],
                                  ALU.subtract).then_inc(agg_ready, 1)

            dve.sem_inc(agg_ready, 2)
            with dve.Fori(0, STEPS) as t:
                for g in range(MG):
                    lo(4 + t, g)
                for c in range(NC):
                    low_parts(t, c)
                    gated(t, c)

            def relu(c):
                wait_if(dve, dec1_done, c - 1)
                dve.tensor_scalar(relu_h[c % 2][:], cols(hT, c), 0.0, None, ALU.max).then_inc(relu_ready, 1)
            await_h(dve, STEPS, NC - 1)
            relu(0)
            relu(1)
            for c in range(NC):
                if c + 2 < NC:
                    relu(c + 2)
                dve.wait_ge(sig_ready, c + 1)
                dve.wait_ge(res3_in[c % 2], 16 * (c // 2 + 1))
                dve.wait_ge(relu_ready, c + 1)
                dve.tensor_tensor(cols(hT, c), sigm[c % 2][:], res3[c % 2][:], ALU.add).then_inc(h_ready, 1)

            def take_rows(c):
                for g in turned_with[c]:
                    s0, k = groups[g]
                    dve.wait_ge(outT_done, g + 1)
                    dve.tensor_copy(x_in[:, s0:s0 + k, :], mps[g % 2][0:B, 0:128 * k]
                                    .rearrange("p (s f) -> p s f", s=k)).then_inc(out_taken, 1)
            for c in range(NC):
                diagonal(norm_last(c))
                if c >= 1:
                    normalised(norm_last(c - 1), cols(hT, c - 1))
                if c >= 2:
                    take_rows(c - 2)
            normalised(norm_last(NC - 1), cols(hT, NC - 1))
            take_rows(NC - 2)
            take_rows(NC - 1)


_INS = ["x", "src", "dst", "edge_attr_128", "L0_gnn_W", "L0_gnn_b", "L0_gnn_gamma", "L0_gnn_beta",
        "L1_gnn_W1_0", "L1_gnn_W2_0", "L1_gnn_W3_0", "L1_gnn_W1_1", "L1_gnn_W2_1", "L1_gnn_W3_1",
        "L2_gnn_W_neigh", "L2_gnn_W_self", "L2_gnn_b_self", "L3_gnn_enc_w1", "L3_gnn_enc_b1", "L3_gnn_enc_w2",
        "L3_gnn_enc_b2", "L3_gnn_conv_w", "L3_gnn_gru_wih", "L3_gnn_gru_whh", "L3_gnn_gru_bih", "L3_gnn_gru_bhh",
        "L3_gnn_dec_w1", "L3_gnn_dec_b1", "L3_gnn_dec_w2", "L3_gnn_dec_b2"]


def kernel(**inputs):
    import numpy as _np
    import concourse.bacc as _bacc
    from concourse import mybir as _mybir
    from concourse.bass_utils import run_bass_kernel_spmd as _run

    nc = _bacc.Bacc("TRN2", target_bir_lowering=False, num_devices=1)
    arrays, ins = {}, {}
    for name in _INS:
        arr = _np.ascontiguousarray(inputs[name])
        arrays[f"in_{name}_dram"] = arr
        ins[name] = nc.dram_tensor(f"in_{name}_dram", arr.shape, _mybir.dt.from_np(arr.dtype), kind="ExternalInput").ap()
    out = nc.dram_tensor("out_0_dram", (N, D), _mybir.dt.float32, kind="ExternalOutput").ap()
    gnn_kernel(nc, ins, out)
    r = _run(nc, [arrays], core_ids=[0])
    return r.results[0]["out_0_dram"]
```

```python
from contextlib import ExitStack

import concourse.bass as bass
from concourse import mybir

F32 = mybir.dt.float32
F16 = mybir.dt.float16
BF16 = mybir.dt.bfloat16
I32 = mybir.dt.int32
ALU = mybir.AluOpType
ACT = mybir.ActivationFunctionType
AX_X = mybir.AxisListType.X

N, D, E = 3125, 128, 50000
B = 125
T = N // B
ET = E // B
TQ = 4
TP = ET // TQ
W = 19
UNROLL = 5
WINS = [7, 6, 7, 6, 7]
WPB = sum(WINS)
NW = WPB * (T // UNROLL)
KA = 4
WRING = 3
RING = 11
KES = [5, 5, 4, 4]
EQ, KE = len(KES), sum(KES)
KOFF = [sum(KES[:q]) for q in range(EQ)]
MW = T * W
SW = 98
CW = 4 * SW
NC = 8
NPAD = NC * CW
NADJ = max(NPAD, NW * W)
MG = (T + 3) // 4
BIG = 512.0
MAGIC = 12582912.0
LEAK = (1.0 / 8.0 + 1.0 / 3.0) / 2.0
EPS = 1e-5
STEPS = 5
assert NW * W >= N and NADJ >= NPAD >= N and KA * WPB % RING == 0 and WPB % WRING == 0 and KA * WRING >= RING

WT = ["L1_gnn_W1_0", "L1_gnn_W2_0", "L1_gnn_W3_0", "L1_gnn_W1_1", "L1_gnn_W2_1", "L1_gnn_W3_1",
      "L2_gnn_W_neigh", "L2_gnn_W_self", "L3_gnn_enc_w1", "L3_gnn_enc_w2",
      "L3_gnn_gru_wih", "L3_gnn_gru_whh", "L3_gnn_dec_w1", "L3_gnn_dec_w2"]
WROWS = {"L3_gnn_gru_wih": 3, "L3_gnn_gru_whh": 3}
VECS = ["L0_gnn_b", "L0_gnn_gamma", "L0_gnn_beta", "L2_gnn_b_self", "L3_gnn_enc_b1", "L3_gnn_enc_b2",
        "L3_gnn_gru_bih", "L3_gnn_gru_bhh", "L3_gnn_dec_b1", "L3_gnn_dec_b2"]
NVEC = sum(3 if "gru" in n else 1 for n in VECS)


def gnn_kernel(nc, ins, out):
    a = ins
    ctx = ExitStack()
    with ctx:
        def sb(name, shape, dt, stack=ctx):
            return stack.enter_context(nc.sbuf_tensor(name, shape, dt))

        def sem(name):
            return ctx.enter_context(nc.semaphore(name))

        adj = sb("adj", [B, T * NADJ], F16)
        adj3 = adj[:].rearrange("p (s d) -> p s d", s=T)
        nW = sum(WROWS.get(n, 1) for n in WT)
        wT = sb("wT", [128, nW, 128], F32)
        slot, at = {}, 0
        for n in WT:
            slot[n] = at
            at += WROWS.get(n, 1)
        w0 = sb("w0", [128, 128], F32)
        conv = sb("conv", [128, STEPS * 128], F32)
        vec = sb("vec", [128, NVEC], F32)
        vcol, at = {}, 0
        for n in VECS:
            vcol[n] = at
            at += 3 if "gru" in n else 1
        gbias = sb("gbias", [128, 2], F32)
        ident = sb("ident", [128, 128], F32)
        center = sb("center", [128, 128], F32)
        mean = sb("mean", [128, 1], F32)
        ones = sb("ones", [128, 128], F32)
        epsc = sb("epsc", [128, 1], F32)
        rows_i = sb("rows_i", [1, T + 1], I32)
        flag_at = T

        PS = [ctx.enter_context(nc.psum_tensor(n, [128, 512], F32))
              for n in ("acc0", "acc1", "g0", "g1", "g2", "g3", "m0", "m1")]
        acc, gate, mps = PS[0:2], PS[2:6], PS[6:8]

        sums = nc.dram_tensor("edge_sums_transposed", (128, NPAD), F32).ap()
        degs = nc.dram_tensor("degrees", (1, NPAD), F32).ap()
        tabs = nc.dram_tensor("edge_tables", (B, 3 * ET), F32).ap()
        rdegs = nc.dram_tensor("inverse_degrees", (1, NPAD), F32).ap()
        x1s = nc.dram_tensor("x1_transposed", (128, NPAD), F32).ap()
        x3s = nc.dram_tensor("x3_transposed", (128, NPAD), F32).ap()

        build = ExitStack()
        jkey = sb("jkey", [B, T], F32, build)
        ka = sb("ka", [B, NW * KA], F32, build)
        ka16 = sb("ka16", [B, NW * KA], F16, build)
        ke = sb("ke", [B, (T + 1) * KE], F32, build)
        iota_m = sb("iota_m", [B, MW], F16, build)
        ones_bf = sb("ones_bf", [B, 1], BF16, build)
        zpad = sb("zpad", [128, NPAD - N], F32, build)
        used = [0]

        def scratch(parts, cols):
            lo = used[0]
            used[0] += cols
            assert 2 * used[0] <= T * NADJ
            return adj[0:parts, 2 * lo:2 * used[0]].bitcast(F32)

        ei = scratch(TP, 2 * TQ * B).bitcast(I32)
        ef = scratch(TP, 2 * TQ * B)
        srcf, dstf = ef[:, 0:TQ * B], ef[:, TQ * B:]
        src_tile, window = scratch(TP, TQ * B), scratch(TP, TQ * B)
        key = [scratch(TP, TQ * B), scratch(TP, TQ * B), dstf]
        tab = scratch(B, 3 * ET).rearrange("p (k t) -> p k t", k=3)
        wkey = scratch(B, 2 * NW).rearrange("p (k w) -> p k w", k=2)
        mm = scratch(TP, 2 * TQ)
        mmb = scratch(TP, 2 * TQ * B)
        tnum = scratch(B, TQ * TP)
        first, last_dst, most, limit = (scratch(B, 2) for _ in range(4))
        gathered_keys = [scratch(B, NW * KA), ka[:]]
        cover = [scratch(B, ET) for _ in range(3)]
        ends = scratch(B, 4 * 2)
        JP = 64
        ROW = B + JP + T
        TROW = B + JP
        assert NW - B <= JP
        trow = scratch(1, ROW)
        tile_of = scratch(TP, NW * KA)
        tile_e = scratch(TP, T * KE)
        pick = [scratch(TP, NW * KA) for _ in range(TQ)]
        pick_e = [scratch(TP, T * KE) for _ in range(TQ)]
        kofs = scratch(TP, NW * KA)
        kofs_e = scratch(TP, T * KE)
        vraw = scratch(NVEC, 128)
        flag_f = scratch(1, 1)

        weights_in, edges_in, vecs_in = sem("weights_in"), sem("edges_in"), sem("vecs_in")
        consts, ident_zero, consts2 = sem("consts"), sem("ident_zero"), sem("consts2")
        prep_step, turned, taken = sem("prep_step"), sem("turned"), sem("taken")
        wturned, wtaken, gathered, gather_taken = sem("wturned"), sem("wtaken"), sem("gathered"), sem("gather_taken")
        rows_done, rows_read, picks_ready = sem("rows_done"), sem("rows_read"), sem("picks_ready")
        pads_out = sem("pads_out")

        wgroups = [(g, min(4, nW - g)) for g in range(0, nW, 4)]
        half = NW * KA // 2
        SETS = [(B, 0), (JP + T, B)]
        PLACES = [(0, 0, B, 0, W, KA), (1, 0, JP, B * W, W, KA), (1, JP, JP + T, 0, B, KE)]

        with nc.Block() as block:
            @block.sync
            def _(sp):
                sp.dma_start(ei[:, 0:TQ * B], a["src"].rearrange("(p e) -> p e", p=TP)).then_inc(edges_in, 16)
                sp.dma_start(ei[:, TQ * B:], a["dst"].rearrange("(p e) -> p e", p=TP)).then_inc(edges_in, 16)
                for n in WT:
                    k = WROWS.get(n, 1)
                    sp.dma_start(wT[:, slot[n]:slot[n] + k, :],
                                 a[n].rearrange("(k o) i -> o k i", k=k)).then_inc(weights_in, 16)
                sp.dma_start(w0[:], a["L0_gnn_W"]).then_inc(vecs_in, 16)
                sp.dma_start(conv[:].rearrange("i (t o) -> i t o", t=STEPS),
                             a["L3_gnn_conv_w"].rearrange("t i o -> i t o")).then_inc(vecs_in, 16)
                sp.wait_ge(consts, 1)
                sp.dma_start(sums[:, N:NPAD], zpad[:]).then_inc(pads_out, 16)
                sp.dma_start(rdegs[:, N:NPAD], zpad[0:1, :]).then_inc(pads_out, 16)
                sp.wait_ge(wtaken, 3)
                sp.dma_start(tabs, tab.rearrange("p k t -> p (k t)")).then_inc(pads_out, 16)
                sp.wait_ge(pads_out, 48)

            @block.gpsimd
            def _(pool):
                def iota(to, pattern, mult=0, base=0):
                    pool.iota(to, pattern=pattern, base=base, channel_multiplier=mult,
                              allow_small_or_imprecise_dtypes=True).then_inc(consts2, 1)

                pool.memset(zpad[:], 0.0).then_inc(consts, 1)
                pool.memset(ke[:, T * KE:], 0.0)
                pool.memset(ident[:], 0.0).then_inc(ident_zero, 1)
                pool.memset(ones[:], 1.0).then_inc(consts, 1)
                pool.wait_ge(ident_zero, 1)
                pool.affine_select(out=ident[:], in_=ident[:], compare_op=ALU.not_equal, fill=1.0, base=0,
                                   pattern=[[-1, 128]], channel_multiplier=1).then_inc(consts, 1)
                pool.memset(mean[:], 1.0 / 128).then_inc(consts, 1)
                pool.memset(ones_bf[:], 1.0).then_inc(consts, 1)
                pool.memset(epsc[:], EPS).then_inc(consts, 1)
                iota(tnum, [[1, TQ], [TQ, TP]])
                for n, (k, lo, hi, dst0, width, tiles) in enumerate(PLACES):
                    if lo:
                        pool.wait_ge(consts2, 1 + 4 * n)
                    iota(first[lo:hi, k:k + 1], [[0, 1]], width, dst0)
                    iota(last_dst[lo:hi, k:k + 1], [[0, 1]], width, dst0 + width - 1)
                    pool.memset(most[lo:hi, k:k + 1], float(tiles)).then_inc(consts2, 1)
                    pool.memset(limit[lo:hi, k:k + 1], float(ET - tiles)).then_inc(consts2, 1)
                pool.wait_ge(consts2, 1 + 4 * len(PLACES))
                iota(kofs, [[0, NW], [1, KA]], -TQ)
                iota(kofs_e, [[0, T], [1, KE]], -TQ)
                iota(wkey[:, 0, :], [[128, NW]])
                iota(wkey[:, 1, :], [[W, NW]])
                iota(jkey[:], [[B, T]])
                iota(iota_m[:], [[1, MW]])

            @block.vector
            def _(dve):
                steps = [0]

                def step(ins):
                    steps[0] += 1
                    ins.then_inc(prep_step, 1)
                    dve.wait_ge(prep_step, steps[0])

                dve.wait_ge(edges_in, 32)
                step(dve.tensor_copy(ef, ei))
                dst4 = dstf.rearrange("p (q e) -> p q e", q=TQ)
                dve.tensor_reduce(mm[:, 0:TQ], dst4, AX_X, ALU.min)
                step(dve.tensor_reduce(mm[:, TQ:], dst4, AX_X, ALU.max))
                dve.wait_ge(consts, 6)
                for k in range(2 * TQ):
                    last = dve.tensor_scalar(mmb[:, k * B:(k + 1) * B], ones[0:TP, 0:B], mm[:, k:k + 1], None, ALU.mult)
                step(last)
                dve.tensor_scalar(src_tile, srcf, 1.0 / B, 0.5 / B - 0.5, ALU.mult, ALU.add)
                step(dve.tensor_scalar(window, dstf, 1.0 / W, 0.5 / W - 0.5, ALU.mult, ALU.add))
                dve.tensor_scalar(src_tile, src_tile, MAGIC, MAGIC, ALU.add, ALU.subtract)
                step(dve.tensor_scalar(window, window, MAGIC, MAGIC, ALU.add, ALU.subtract))
                dve.scalar_tensor_tensor(out=key[0], in0=src_tile, scalar=-float(B), in1=srcf, op0=ALU.mult, op1=ALU.add)
                step(dve.scalar_tensor_tensor(out=key[1], in0=src_tile, scalar=float(W), in1=dstf,
                                              op0=ALU.mult, op1=ALU.add))
                step(dve.scalar_tensor_tensor(out=key[0], in0=window, scalar=128.0, in1=key[0],
                                              op0=ALU.mult, op1=ALU.add))
                dve.wait_ge(consts2, 1 + 4 * len(PLACES))
                dve.wait_ge(turned, 2)
                low, high = PS[3][0:B, 0:ET], PS[4][0:B, 0:ET]
                for k, (parts, _) in enumerate(SETS):
                    e = ends[0:parts, 4 * k:4 * k + 4]
                    c0, c1, c2 = (c[0:parts, :] for c in cover)
                    step(dve.tensor_scalar(c0, low[0:parts], last_dst[0:parts, k:k + 1], None, ALU.is_le))
                    step(dve.scalar_tensor_tensor(out=c0, in0=high[0:parts], scalar=first[0:parts, k:k + 1], in1=c0,
                                                  op0=ALU.is_ge, op1=ALU.mult))
                    dve.scalar_tensor_tensor(out=c1, in0=tnum[0:parts], scalar=1.0, in1=c0, op0=ALU.add, op1=ALU.mult)
                    step(dve.scalar_tensor_tensor(out=c2, in0=tnum[0:parts], scalar=-BIG, in1=c0,
                                                  op0=ALU.add, op1=ALU.mult))
                    dve.tensor_reduce(e[:, 1:2], c1, AX_X, ALU.max)
                    step(dve.tensor_reduce(e[:, 0:1], c2, AX_X, ALU.min))
                    step(dve.tensor_scalar(e[:, 0:1], e[:, 0:1], BIG, limit[0:parts, k:k + 1], ALU.add, ALU.min))
                    step(dve.tensor_tensor(e[:, 1:2], e[:, 1:2], e[:, 0:1], ALU.subtract))
                    step(dve.tensor_scalar(e[:, 1:2], e[:, 1:2], most[0:parts, k:k + 1], None, ALU.is_gt))
                dve.wait_ge(turned, 6)
                dve.tensor_copy(vec[:], PS[5][:, 400:400 + NVEC]).then_inc(taken, 1)
                dve.wait_ge(taken, 1)
                dve.wait_ge(rows_done, 1)
                step(dve.tensor_copy(trow, PS[5][0:1, 0:ROW]))
                dve.sem_inc(rows_read, 1)
                dve.tensor_copy(rows_i[0:1, 0:T], trow[:, TROW:ROW])
                dve.wait_ge(rows_done, 2)
                step(dve.tensor_reduce(flag_f, PS[4][0:1, 0:ROW], AX_X, ALU.max))
                dve.tensor_copy(rows_i[0:1, flag_at:flag_at + 1], flag_f)
                dve.wait_ge(consts2, 1 + 4 * len(PLACES) + 5)
                dve.wait_ge(rows_done, 3)
                dve.tensor_tensor(tile_of.rearrange("p (w i) -> p w i", i=KA), kofs.rearrange("p (w i) -> p w i", i=KA),
                                  PS[3][0:TP, 0:NW].unsqueeze(2).to_broadcast([TP, NW, KA]), ALU.add)
                step(dve.tensor_tensor(tile_e.rearrange("p (w i) -> p w i", i=KE), kofs_e.rearrange("p (w i) -> p w i", i=KE),
                                       PS[3][0:TP, TROW:ROW].unsqueeze(2).to_broadcast([TP, T, KE]), ALU.add))
                for q in range(TQ):
                    dve.tensor_scalar(pick[q], tile_of, float(q), None, ALU.is_equal)
                    dve.tensor_scalar(pick_e[q], tile_e, float(q), None, ALU.is_equal).then_inc(picks_ready, 1)
                for k in range(2):
                    for h in range(2):
                        n = 2 * k + h
                        dve.wait_ge(gathered, n + 1)
                        dve.tensor_copy(gathered_keys[k][:, h * half:(h + 1) * half], PS[n % 2][0:B, 0:half]).then_inc(gather_taken, 1)
                dve.wait_ge(gathered, 5)
                dve.tensor_tensor(ke[:, 0:T * KE].rearrange("e (j i) -> e j i", i=KE),
                                  jkey[:].unsqueeze(2).to_broadcast([B, T, KE]),
                                  PS[2][0:B, 0:T * KE].rearrange("e (j i) -> e j i", i=KE), ALU.subtract).then_inc(gather_taken, 1)
                dve.wait_ge(gather_taken, 5)
                for k in range(2):
                    kw, to = (t.rearrange("e (w i) -> e w i", i=KA) for t in (gathered_keys[k], (ka16, ka)[k][:]))
                    dve.tensor_tensor(to, kw, wkey[:, k, :].unsqueeze(2).to_broadcast([B, NW, KA]), ALU.subtract)
                bi, bh = vcol["L3_gnn_gru_bih"], vcol["L3_gnn_gru_bhh"]
                dve.tensor_tensor(gbias[:], vec[:, bi:bi + 2], vec[:, bh:bh + 2], ALU.add)
                dve.tensor_scalar(center[:], ident[:], 1.0 / 128, None, ALU.subtract)

            @block.scalar
            def _(act):
                for n in VECS:
                    k = 3 if "gru" in n else 1
                    act.dma_start(vraw[vcol[n]:vcol[n] + k, :], a[n].rearrange("(k f) -> k f", k=k)).then_inc(vecs_in, 16)
                for k in range(3):
                    act.wait_ge(turned, k + 3)
                    to = tab[:, k, :].rearrange("e (p q) -> e q p", q=TQ)
                    act.activation(to, PS[k][0:B, 0:TQ * TP].rearrange("e (q p) -> e q p", q=TQ), ACT.Copy).then_inc(wtaken, 1)
                for i, (g, k) in enumerate(wgroups):
                    act.wait_ge(wturned, i + 1)
                    act.activation(wT[:, g:g + k, :], mps[i % 2][:, 0:128 * k].rearrange("p (k o) -> p k o", k=k),
                                   ACT.Copy).then_inc(wtaken, 1)

            @block.tensor
            def _(pe):
                pe.wait_ge(consts, 6)
                pe.wait_ge(prep_step, 3)
                for k in range(2):
                    for q in range(TQ):
                        n = TQ * k + q
                        last = pe.matmul(PS[3 + k][0:B, q * TP:(q + 1) * TP], mmb[:, n * B:(n + 1) * B],
                                         ident[0:TP, 0:TP], start=True, stop=True)
                    last.then_inc(turned, 1)
                pe.wait_ge(prep_step, 7)
                for k in range(3):
                    for q in range(TQ):
                        last = pe.transpose(PS[k][0:B, q * TP:(q + 1) * TP], key[k][:, q * B:(q + 1) * B], ident[0:TP, 0:TP])
                    last.then_inc(turned, 1)
                pe.wait_ge(vecs_in, 32 + 16 * len(VECS))
                pe.transpose(PS[5][:, 400:400 + NVEC], vraw, ident[0:NVEC, 0:NVEC]).then_inc(turned, 1)
                pe.wait_ge(taken, 1)
                for k, (parts, col) in enumerate(SETS):
                    last = pe.transpose(PS[5][0:1, col:col + parts], ends[0:parts, 4 * k:4 * k + 1], ident[0:parts, 0:parts])
                last.then_inc(rows_done, 1)
                for k, (parts, col) in enumerate(SETS):
                    last = pe.transpose(PS[4][0:1, col:col + parts], ends[0:parts, 4 * k + 1:4 * k + 2],
                                        ident[0:parts, 0:parts])
                last.then_inc(rows_done, 1)
                pe.wait_ge(rows_read, 1)
                pe.matmul(PS[3][0:TP, 0:ROW], ones[0:1, 0:TP], trow, start=True, stop=True).then_inc(rows_done, 1)
                pe.wait_ge(weights_in, 16 * len(WT))
                for i, (g, k) in enumerate(wgroups):
                    if i >= 2:
                        pe.wait_ge(wtaken, 3 + i - 1)
                    for j in range(k):
                        last = pe.transpose(mps[i % 2][:, 128 * j:128 * (j + 1)], wT[:, g + j, :], ident[:])
                    last.then_inc(wturned, 1)
                pe.wait_ge(picks_ready, TQ)
                pe.wait_ge(wtaken, 3)
                for k in range(2):
                    for h in range(2):
                        n = 2 * k + h
                        if n >= 2:
                            pe.wait_ge(gather_taken, n - 1)
                        for q in range(TQ):
                            last = pe.matmul(PS[n % 2][0:B, 0:half], key[k][:, q * B:(q + 1) * B],
                                             pick[q][:, h * half:(h + 1) * half], start=(q == 0), stop=(q == TQ - 1))
                        last.then_inc(gathered, 1)
                for q in range(TQ):
                    last = pe.matmul(PS[2][0:B, 0:T * KE], key[2][:, q * B:(q + 1) * B], pick_e[q],
                                     start=(q == 0), stop=(q == TQ - 1))
                last.then_inc(gathered, 1)

        wk = ExitStack()
        moving = sb("moving", [B, RING, MW], F16, wk)
        within = sb("within", [B, WRING, KA, 126], F16, wk)
        efeat = sb("efeat", [B, KE, 128], F32, wk)
        edst = sb("edst", [B, KE, B], F32, wk)
        stage = sb("stage", [128, 2, B], F32, wk)
        kg = sb("kg", [B, 3], F32, wk)

        moving_ready, within_ready, pair_free = sem("moving_ready"), sem("within_ready"), sem("pair_free")
        win_taken = sem("win_taken")
        efeat_in = [sem(f"efeat_in{q}") for q in range(EQ)]
        distance, edst_ready, last_hot_ready = sem("distance"), sem("edst_ready"), sem("last_hot_ready")
        echunk_free = sem("echunk_free")
        esum_taken, sums_out, last_sums_out, stage_free = (
            sem("esum_taken"), sem("sums_out"), sem("last_sums_out"), sem("stage_free"))
        ORDER = [("w", 0), ("w", 1), ("e", 0), ("w", 2), ("w", 3), ("e", 1), ("w", 4), ("w", 5), ("e", 2), ("w", 6), ("e", 3)]
        AHEAD = [("e", 2), ("w", 0), ("f", 2), ("w", 1), ("e", 3), ("w", 2), ("w", 3), ("e", 4), ("w", 4), ("f", 4),
                 ("w", 5), ("e", 5), ("w", 6), ("f", 5), ("s", 0)]
        win_banks = PS[0:4] + PS[6:8]
        WB = len(win_banks)

        def win_before(w):
            return (w - WB if w >= WB else (WPB - 1 - w) // WB * WB + w - WPB) + 1

        def windows(order, r):
            return [(kind, n) for kind, n in order if kind != "w" or n < WINS[r]]

        flags_of = {}

        def load_flag(name, eng):
            flags_of[name] = eng.value_load(rows_i[0:1, flag_at:flag_at + 1], min_val=0, max_val=1)

        with nc.Block() as block:
            @block.sync
            def _(sp):
                load_flag("sp", sp)
                with sp.Fori(0, T // UNROLL) as jj:
                    for r in range(UNROLL):
                        j = UNROLL * jj + r
                        t0 = sp.value_load(rows_i[0:1, bass.ds(j, 1)], min_val=0, max_val=ET - KE)
                        for q, k in enumerate(KES):
                            sp.wait_ge(echunk_free, EQ * j + q + 1)
                            sp.dma_start(efeat[:, KOFF[q]:KOFF[q] + k, :],
                                         a["edge_attr_128"][bass.ds((t0 + KOFF[q]) * B, k * B), :]
                                         .rearrange("(i p) f -> p i f", p=B)).then_inc(efeat_in[q], 16)
                sp.wait_ge(esum_taken, 2 * T + 1)
                sp.dma_start(sums[:, (T - 1) * B:N], stage[:, 0, :]).then_inc(last_sums_out, 16)
                sp.dma_start(degs[:, (T - 1) * B:N], stage[0:1, 1, :]).then_inc(last_sums_out, 16)

            @block.vector
            def _(dve):
                load_flag("dve", dve)
                with dve.Fori(0, T // UNROLL) as jj:
                    for r in range(UNROLL):
                        j = UNROLL * jj + r
                        for kind, n in windows(ORDER, r):
                            if (kind, n) == ("e", EQ - 2):
                                hot = edst[:, KOFF[EQ - 1]:KE, :]
                                dve.wait_ge(distance, EQ * j + EQ)
                                dve.tensor_scalar(hot, hot, 0.0, None, ALU.is_equal).then_inc(last_hot_ready, 1)
                            if kind == "w":
                                w = sum(WINS[:r]) + n
                                dve.wait_ge(pair_free, KA * (WPB * jj + w + 1 - WRING) + RING)
                                dve.tensor_tensor(within[:, w % WRING, :, 0:B],
                                                  iota_m[:, 0:B].unsqueeze(1).to_broadcast([B, KA, B]),
                                                  ka16[:, bass.ds(KA * (WPB * jj + w), KA)].unsqueeze(2).to_broadcast([B, KA, B]),
                                                  ALU.is_equal).then_inc(within_ready, 1)
                                for i in range(KA):
                                    l = KA * (sum(WINS[:r]) + n) + i
                                    g = KA * WPB * jj + l
                                    dve.wait_ge(pair_free, g + 1)
                                    dve.tensor_scalar(moving[:, l % RING, :], iota_m[:], ka[:, bass.ds(g, 1)], None,
                                                      ALU.is_equal).then_inc(moving_ready, 1)

            @block.gpsimd
            def _(pool):
                load_flag("pool", pool)
                if NADJ > NW * W:
                    pool.memset(adj3[:, :, NW * W:NADJ], 0.0)

                def store(j):
                    pool.wait_ge(esum_taken, 2 * j + 3)
                    pool.dma_start(sums[:, bass.ds(j * B, B)], stage[:, 0, :]).then_inc(sums_out, 16)
                    pool.dma_start(degs[:, bass.ds(j * B, B)], stage[0:1, 1, :]).then_inc(sums_out, 16)

                pool.sem_inc(stage_free, 1)
                store(0)
                with pool.Fori(1, T - 1) as j:
                    pool.wait_ge(sums_out, 32 * j)
                    pool.sem_inc(stage_free, 1)
                    store(j)
                pool.wait_ge(sums_out, 32 * (T - 1))
                pool.sem_inc(stage_free, 1)

            @block.tensor
            def _(pe):
                load_flag("pe", pe)
                pe.sem_inc(pair_free, RING)
                pe.sem_inc(echunk_free, EQ)
                with pe.Fori(0, T // UNROLL) as jj:
                    for r in range(UNROLL):
                        j = UNROLL * jj + r
                        for kind, n in windows(ORDER, r):
                            if kind == "w":
                                w = sum(WINS[:r]) + n
                                pe.wait_ge(within_ready, WPB * jj + w + 1)
                                pe.wait_ge(win_taken, WPB * jj + win_before(w) + WB)
                                for i in range(KA):
                                    l = KA * (sum(WINS[:r]) + n) + i
                                    g = KA * WPB * jj + l
                                    pe.wait_ge(moving_ready, g + 1)
                                    pe.matmul(win_banks[w % WB][0:B, 0:MW], within[:, w % WRING, i, 0:B], moving[:, l % RING, :],
                                              start=(i == 0), stop=(i == KA - 1)).then_inc(pair_free, 1)
                            else:
                                if n == 0:
                                    pe.wait_ge(esum_taken, 2 * j + 1)
                                pe.wait_ge(efeat_in[n], 16 * (j + 1))
                                if n == EQ - 1:
                                    pe.wait_ge(last_hot_ready, j + 1)
                                else:
                                    pe.wait_ge(edst_ready, (EQ - 1) * j + n + 1)
                                hot16 = edst[:].bitcast(BF16).rearrange("p i (d h) -> p i d h", h=2)
                                for i in range(KES[n]):
                                    first_, last_ = (n == 0 and i == 0), (n == EQ - 1 and i == KES[n] - 1)
                                    pe.matmul(PS[4][:, 0:B], efeat[:, KOFF[n] + i, :], edst[:, KOFF[n] + i, :],
                                              start=first_, stop=last_)
                                    last = pe.matmul(PS[5][0:1, 0:B], ones_bf[:], hot16[:, KOFF[n] + i, :, 1],
                                                     start=first_, stop=last_)
                                last.then_inc(echunk_free, 1)

            @block.scalar
            def _(act):
                load_flag("act", act)
                act.sem_inc(win_taken, WB)
                act.sem_inc(esum_taken, 1)

                def edge_hot(j, n):
                    m = EQ * j + n
                    hot = edst[:, KOFF[n]:KOFF[n] + KES[n], :]
                    act.wait_ge(echunk_free, m + 1)
                    for i in range(KES[n]):
                        last = act.activation(hot[:, i, :], iota_m[:, 0:B], ACT.Square, bias=ke[:, bass.ds(KE * j + KOFF[n] + i, 1)])
                    last.then_inc(distance, 1)

                def finish_hot(j, n):
                    hot = edst[:, KOFF[n]:KOFF[n] + KES[n], :]
                    act.wait_ge(distance, EQ * j + n + 1)
                    act.activation(hot, hot, ACT.Relu, scale=-1.0, bias=ones[0:B, 0:1]).then_inc(edst_ready, 1)

                for n in range(2):
                    edge_hot(0, n)
                    finish_hot(0, n)
                with act.Fori(0, T // UNROLL) as jj:
                    for r in range(UNROLL):
                        j = UNROLL * jj + r
                        for kind, n in windows(AHEAD, r):
                            if kind == "e":
                                edge_hot(j + n // EQ, n % EQ)
                            elif kind == "f":
                                finish_hot(j + n // EQ, n % EQ)
                            elif kind == "s":
                                act.wait_ge(echunk_free, EQ * j + 2 * EQ)
                                act.wait_ge(stage_free, j + 1)
                                act.activation(stage[:, 0, :], PS[4][:, 0:B], ACT.Copy).then_inc(esum_taken, 1)
                                act.activation(stage[0:1, 1, :], PS[5][0:1, 0:B], ACT.Copy).then_inc(esum_taken, 1)
                            else:
                                w = sum(WINS[:r]) + n
                                act.wait_ge(pair_free, KA * (WPB * jj + w + 1) + RING)
                                act.activation(adj3[:, :, bass.ds((WPB * jj + w) * W, W)],
                                               win_banks[w % WB][0:B, 0:MW].rearrange("p (c d) -> p c d", c=T),
                                               ACT.Copy).then_inc(win_taken, 1)

        pair_keys, pair_hot, pair_used = sem("pair_keys"), sem("pair_hot"), sem("pair_used")
        all_done, all_taken = sem("all_done"), sem("all_taken")
        efeat1_in, ekey1, ehot1, epair_used = sem("efeat1_in"), sem("ekey1"), sem("ehot1"), sem("epair_used")
        esum1_done, esum1_taken, sums1_out = sem("esum1_done"), sem("esum1_taken"), sem("sums1_out")

        spare = efeat[:, 1:KE].rearrange("p i f -> p (i f)")
        tab_g = spare[:, 0:3 * ET].rearrange("p (k t) -> p k t", k=3)
        wkey_g = spare[:, 3 * ET:3 * ET + 2 * NW].rearrange("p (k w) -> p k w", k=2)
        zero = spare[:, 3 * ET + 2 * NW:3 * ET + 2 * NW + (MW + 1) // 2]
        tables_in, tables_made = sem("tables_in"), sem("tables_made")

        def general(name, eng):
            return eng.If(flags_of[name] == 1)

        with nc.Block() as block:
            @block.sync
            def _(sp):
                with general("sp", sp):
                    sp.dma_start(spare[:, 0:3 * ET], tabs).then_inc(tables_in, 16)
                    with sp.Fori(0, T) as j:
                        with sp.Fori(0, ET) as t:
                            sp.wait_ge(epair_used, ET * j + t + 1)
                            sp.dma_start(efeat[:, 0, :],
                                         a["edge_attr_128"][bass.ds(t * B, B), :]).then_inc(efeat1_in, 16)

            @block.gpsimd
            def _(pool):
                with general("pool", pool):
                    pool.memset(zero, 0.0).then_inc(tables_made, 1)
                    for k, step in enumerate((128, W)):
                        pool.iota(wkey_g[:, k, :], pattern=[[step, NW]], base=0, channel_multiplier=0,
                                  allow_small_or_imprecise_dtypes=True).then_inc(tables_made, 1)

            @block.vector
            def _(dve):
                with general("dve", dve):
                    dve.wait_ge(tables_in, 16)
                    dve.wait_ge(tables_made, 3)
                    with dve.Fori(0, NW) as w:
                        with dve.Fori(0, ET) as t:
                            n = ET * w + t
                            dve.wait_ge(pair_used, n + 1)
                            dve.tensor_tensor(kg[:, 0:2].unsqueeze(2), tab_g[:, 0:2, bass.ds(t, 1)],
                                              wkey_g[:, :, bass.ds(w, 1)], ALU.subtract).then_inc(pair_keys, 1)
                            dve.wait_ge(pair_keys, n + 1)
                            dve.tensor_scalar(within[:, 0, 0, 0:B], iota_m[:, 0:B], kg[:, 0:1], None,
                                              ALU.is_equal).then_inc(pair_hot, 1)
                            dve.tensor_scalar(moving[:, 0, :], iota_m[:], kg[:, 1:2], None,
                                              ALU.is_equal).then_inc(pair_hot, 1)
                            dve.wait_ge(pair_hot, 2 * n + 2)
                    with dve.Fori(0, T) as j:
                        with dve.Fori(0, ET) as t:
                            n = ET * j + t
                            dve.wait_ge(epair_used, n + 1)
                            dve.tensor_scalar(kg[:, 2:3], tab_g[:, 2, bass.ds(t, 1)], jkey[:, bass.ds(j, 1)], None,
                                              ALU.subtract).then_inc(ekey1, 1)
                            dve.wait_ge(ekey1, n + 1)
                            dve.tensor_scalar(edst[:, 0, :], iota_m[:, 0:B], kg[:, 2:3], None,
                                              ALU.is_equal).then_inc(ehot1, 1)
                            dve.wait_ge(ehot1, n + 1)

            @block.tensor
            def _(pe):
                z16, zbf = zero.bitcast(F16), zero.bitcast(BF16)
                with general("pe", pe):
                    pe.wait_ge(tables_made, 3)
                    pe.sem_inc(pair_used, 1)
                    pe.sem_inc(epair_used, 1)
                    with pe.Fori(0, NW) as w:
                        pe.wait_ge(all_taken, w + 1)
                        pe.matmul(PS[0][0:B, 0:MW], z16[:, 0:B], z16[:, 0:MW], start=True, stop=False)
                        with pe.Fori(0, ET) as t:
                            pe.wait_ge(pair_hot, 2 * (ET * w + t) + 2)
                            pe.matmul(PS[0][0:B, 0:MW], within[:, 0, 0, 0:B], moving[:, 0, :],
                                      start=False, stop=False).then_inc(pair_used, 1)
                        pe.matmul(PS[0][0:B, 0:MW], z16[:, 0:B], z16[:, 0:MW], start=False,
                                  stop=True).then_inc(all_done, 1)
                    with pe.Fori(0, T) as j:
                        pe.wait_ge(esum1_taken, 2 * j + 1)
                        pe.matmul(PS[4][:, 0:B], zero[:, 0:128], zero[:, 0:B], start=True, stop=False)
                        pe.matmul(PS[5][0:1, 0:B], zbf[:, 0:1], zbf[:, 0:B], start=True, stop=False)
                        with pe.Fori(0, ET) as t:
                            n = ET * j + t
                            pe.wait_ge(ehot1, n + 1)
                            pe.wait_ge(efeat1_in, 16 * n + 16)
                            pe.matmul(PS[4][:, 0:B], efeat[:, 0, :], edst[:, 0, :], start=False, stop=False)
                            hot16 = edst[:, 0, :].bitcast(BF16).rearrange("p (d h) -> p d h", h=2)
                            pe.matmul(PS[5][0:1, 0:B], ones_bf[:], hot16[:, :, 1], start=False,
                                      stop=False).then_inc(epair_used, 1)
                        pe.matmul(PS[4][:, 0:B], zero[:, 0:128], zero[:, 0:B], start=False, stop=True)
                        pe.matmul(PS[5][0:1, 0:B], zbf[:, 0:1], zbf[:, 0:B], start=False, stop=True).then_inc(esum1_done, 1)

            @block.scalar
            def _(act):
                with general("act", act):
                    act.wait_ge(last_sums_out, 32)
                    act.sem_inc(all_taken, 1)
                    act.sem_inc(esum1_taken, 1)
                    with act.Fori(0, NW) as w:
                        act.wait_ge(all_done, w + 1)
                        act.activation(adj3[:, :, bass.ds(w * W, W)],
                                       PS[0][0:B, 0:MW].rearrange("p (c d) -> p c d", c=T),
                                       ACT.Copy).then_inc(all_taken, 1)
                    with act.Fori(0, T) as j:
                        act.wait_ge(esum1_done, j + 1)
                        act.activation(stage[:, 0, :], PS[4][:, 0:B], ACT.Copy).then_inc(esum1_taken, 1)
                        act.activation(stage[0:1, 1, :], PS[5][0:1, 0:B], ACT.Copy).then_inc(esum1_taken, 1)
                        act.wait_ge(esum1_taken, 2 * j + 3)
                        act.dma_start(sums[:, bass.ds(j * B, B)], stage[:, 0, :]).then_inc(sums1_out, 16)
                        act.dma_start(degs[:, bass.ds(j * B, B)], stage[0:1, 1, :]).then_inc(sums1_out, 16)
                        act.wait_ge(sums1_out, 32 * j + 32)
        wk.close()
        build.close()
        layers(nc, ctx, sb, sem, a, out, locals())


def layers(nc, ctx, sb, sem, a, out, env):
    adj3, wT, w0, conv, vec, slot, vcol = (env[k] for k in ("adj3", "wT", "w0", "conv", "vec", "slot", "vcol"))
    gbias, ident, center, mean, ones, epsc = (env[k] for k in ("gbias", "ident", "center", "mean", "ones", "epsc"))
    acc, gate, mps = (env[k] for k in ("acc", "gate", "mps"))
    sums, degs, rdegs, x1s, x3s, last_sums_out = (env[k] for k in ("sums", "degs", "rdegs", "x1s", "x3s", "last_sums_out"))

    hT = sb("hT", [128, NPAD], F32)
    msg_all = sb("msg", [128, T, 2, 128], F16)
    msg = msg_all[0:B]
    x3_all = msg_all[:].rearrange("p s h f -> p (s h f)").bitcast(F32)[:, 0:NPAD]
    x_in = msg.rearrange("p s h f -> p (s h f)").bitcast(F32).rearrange("p (s f) -> p s f", s=T)
    buf = [sb(f"chunk{i}", [128, CW], F32) for i in range(10)]
    small = sb("small", [SW, 2, 2, 4], F32)
    dg = buf[9][0:B, 0:3 * T].rearrange("p (k e) -> p k e", k=3)
    rd = buf[0:2]
    esum = buf[2:4]
    norm_sq, norm_dev, norm_diag = (buf[2], buf[5]), (buf[3], buf[6]), (buf[4], buf[7])
    va = buf[8:10]
    v1, v2, res = buf[8], buf[9], buf[4]
    hid, sigm = buf[8:10], buf[6:8] + buf[0:2]
    agg16, h16 = ([b[:].bitcast(F16).rearrange("p (h d) -> p h d", h=2) for b in bs] for bs in (buf[0:2], buf[6:8]))
    gr, gz, gt, gn = buf[2:6]
    g0, gcols = slot["L3_gnn_gru_wih"], 6 * 128
    w32 = wT[:, g0:g0 + 6, :].rearrange("p k o -> p (k o)")
    w16 = w32.bitcast(F16).rearrange("p (h o) -> p h o", h=2)
    w_parts = [b[:].bitcast(F16)[:, 0:gcols] for b in buf[6:8]]
    assert slot["L3_gnn_gru_whh"] == g0 + 3 and gcols <= 2 * CW

    def col(name, k=0):
        return vec[:, vcol[name] + k:vcol[name] + k + 1]

    def w(name, k=0):
        return wT[:, slot[name] + k, :]

    def cols(t, c):
        return t[:, c * CW:(c + 1) * CW]

    pad_zero, x_loaded = sem("pad_zero"), [sem(f"x_loaded{g}") for g in range(MG)]
    xT_done, xT_taken = sem("xT_done"), sem("xT_taken")
    degs_in, rdeg_step, rdegs_out = sem("degs_in"), sem("rdeg_step"), sem("rdegs_out")
    w_split, own_hi, own_lo = sem("w_split"), sem("own_hi"), sem("own_lo")
    m_done, hi_ready, lo_ready = sem("m_done"), sem("hi_ready"), sem("lo_ready")
    acc_done, acc_free, self_free = sem("acc_done"), sem("acc_free"), sem("self_free")
    rd_in, e_in = [sem("rd_in0"), sem("rd_in1")], [sem("e_in0"), sem("e_in1")]
    res_in, res3_in = sem("res_in"), [sem(f"res3_in{c}") for c in range(NC)]
    scaled, mixed, mixed2, summed, leaked = sem("scaled"), sem("mixed"), sem("mixed2"), sem("summed"), sem("leaked")
    act_ready, u_ready = sem("act_ready"), [sem("u_ready0"), sem("u_ready1")]

    def pair(name):
        return [sem(name + "0"), sem(name + "1")]
    center_done, sq_ready, dev_ready, var_done = pair("center_done"), pair("sq_ready"), pair("dev_ready"), pair("var_done")
    std_ready, rstd_ready, diag_ready = pair("std_ready"), pair("rstd_ready"), pair("diag_ready")
    spread_done, normed = pair("spread_done"), pair("normed")
    h_ready = sem("h_ready")
    x1_out, x3_out = sem("x1_out"), [sem(f"x3_out{c}") for c in range(NC)]
    enc1_done, enc1_ready, enc2_done = sem("enc1_done"), sem("enc1_ready"), sem("enc2_done")
    agg_hi, agg_ready, gates_done, r_ready, z_ready = sem("agg_hi"), sem("agg_ready"), sem("gates_done"), sem("r_ready"), sem("z_ready")
    inner1, inner2, n_ready, diff1, diff2 = sem("inner1"), sem("inner2"), sem("n_ready"), sem("diff1"), sem("diff2")
    relu_ready, dec1_done, dec1_ready, dec2_done = sem("relu_ready"), sem("dec1_done"), sem("dec1_ready"), sem("dec2_done")
    sig_ready, outT_done, out_taken, out_stored = sem("sig_ready"), sem("outT_done"), sem("out_taken"), sem("out_stored")

    def wait_if(eng, s, n):
        if n > 0:
            eng.wait_ge(s, n)

    NORMS = {"x1": 0, "x2": NC, "x3": 2 * NC}
    WRITES = {"h1": 0, "enc": NC, "dec": (2 + STEPS) * NC}

    def await_h(eng, version, c):
        if not isinstance(version, (str, int)):
            eng.wait_ge(h_ready, version * NC + WRITES["enc"] + c + 1)
        elif version in NORMS:
            eng.wait_ge(normed[1], NORMS[version] + c + 1)
        elif version in WRITES:
            eng.wait_ge(h_ready, WRITES[version] + c + 1)
        else:
            eng.wait_ge(h_ready, version * NC + WRITES["enc"] + c + 1)

    def norm0(c):
        return 0, c

    def norm1(app, c):
        return 1, NC * (0, None, 1, 2)[app] + c

    def norm_last(c):
        return c % 2, (1 + 2 * (c % 2)) * NC + c // 2

    groups = [(4 * g, min(4, T - 4 * g)) for g in range(MG)]

    mbank = [(mps + acc[1:])[g % 3] for g in range(MG)]

    def last_chunk(g):
        return min(NC - 1, (B * sum(groups[g]) - 1) // CW)
    turned_with = [[g for g in range(MG) if last_chunk(g) == c] for c in range(NC)]

    EARLY = [g for g in range(MG) if last_chunk(g) < NC - 1]
    LATE = [g for g in range(MG) if last_chunk(g) == NC - 1]
    early_with = [[g for g in EARLY if last_chunk(g) + 1 == c] for c in range(NC)]
    DRAIN0 = "C c m0 V v m1 m2 S s m3 m4 C V S m5 m6".split()
    DRAIN = "m0 m1 m2 C m3 V m4 S m5 m6".split()

    with nc.Block() as block:
        @block.sync
        def _(sp):
            for g, (s0, k) in enumerate(groups):
                sp.dma_start(x_in[:, s0:s0 + k, :], a["x"][B * s0:B * (s0 + k), :]
                             .rearrange("(s p) f -> p s f", p=B)).then_inc(x_loaded[g], 16)
            sp.wait_ge(last_sums_out, 32)
            sp.dma_start(dg[:, 0, :], degs[0:1, 0:N].rearrange("o (p e) -> (o p) e", p=B)).then_inc(degs_in, 16)
            sp.wait_ge(rdeg_step, 3)
            sp.dma_start(rdegs[0:1, 0:N].rearrange("o (p e) -> (o p) e", p=B), dg[:, 0, :]).then_inc(rdegs_out, 16)
            sp.wait_ge(rdegs_out, 16)

            def load(app, c):
                n, b = NC * app + c, c % 2
                wait_if(sp, acc_free, n - 1)
                sp.dma_start(rd[b][:], rdegs[0:1, c * CW:(c + 1) * CW].to_broadcast([128, CW])).then_inc(rd_in[b], 16)
                if app in (1, 2):
                    wait_if(sp, acc_done, n - 1)
                    if app == 1 and c == 0:
                        await_h(sp, "x1", NC - 1)
                    sp.dma_start(esum[b][:], cols(sums, c)).then_inc(e_in[b], 16)
                if app == 2:
                    if c == 0:
                        sp.wait_ge(x1_out, 16 * NC)
                    wait_if(sp, u_ready[1], NC + c)
                    sp.dma_start(res[:], cols(x1s, c)).then_inc(res_in, 16)

            def store(dst, version, c, done):
                await_h(sp, version, c)
                sp.dma_start(cols(dst, c), cols(hT, c)).then_inc(done, 16)

            for c in range(NC):
                load(0, c)
                if c >= 4:
                    store(x1s, "x1", c - 4, x1_out)
            for c in range(NC - 4, NC):
                store(x1s, "x1", c, x1_out)
            for app in (1, 2, 3):
                for c in range(NC):
                    load(app, c)
            for c in range(NC):
                store(x3s, "x3", c, x3_out[c])
            for c in range(NC):
                sp.wait_ge(x3_out[c], 16)
            sp.wait_ge(acc_done, NC * (4 + STEPS))
            for c in range(NC):
                sp.dma_start(cols(x3_all, c), cols(x3s, c)).then_inc(res3_in[c], 16)
            for g, (s0, k) in enumerate(groups):
                sp.wait_ge(out_taken, g + 1)
                sp.dma_start(out[B * s0:B * (s0 + k), :].rearrange("(s p) f -> p s f", p=B),
                             x_in[:, s0:s0 + k, :]).then_inc(out_stored, 16)
            sp.wait_ge(out_stored, 16 * MG)

        @block.tensor
        def _(pe):
            def message(app, rhs, version, g):
                s0, k = groups[g]
                if version is not None:
                    await_h(pe, version, last_chunk(g))
                elif g == 0:
                    pe.wait_ge(xT_taken, MG)
                    pe.wait_ge(pad_zero, 1)
                if g >= 3:
                    pe.wait_ge(lo_ready, MG * app + g - 2)
                if g == 2 and isinstance(app, int) and app < 4:
                    wait_if(pe, acc_free, NC * app)
                for s in range(s0, s0 + k):
                    last = pe.matmul(mbank[g][0:B, 128 * (s - s0):128 * (s - s0 + 1)],
                                     hT[:, B * s:B * (s + 1)], rhs, start=True, stop=True)
                last.then_inc(m_done, 1)

            def neighbours(app, c, hooks={}, tail=None):
                b = c % 2
                if isinstance(app, int) and app < 4:
                    wait_if(pe, acc_free, NC * app + c - 1)
                else:
                    pe.wait_ge(agg_ready, NC * (app - 4) + c + 1)
                for s in range(T):
                    for hook in hooks.get(s, []):
                        hook()
                    if c == 0 and s % 4 == 0:
                        pe.wait_ge(lo_ready, MG * app + s // 4 + 1)
                    rhs = adj3[:, s, c * CW:(c + 1) * CW]
                    pe.matmul(acc[b][:, 0:CW], msg[:, s, 0, :], rhs, start=(s == 0), stop=False)
                    last = pe.matmul(acc[b][:, 0:CW], msg[:, s, 1, :], rhs, start=False,
                                     stop=(s == T - 1 and tail is None))
                if tail:
                    last = tail()
                last.then_inc(acc_done, 1)

            def centered(norm, u):
                st, n = norm
                wait_if(pe, dev_ready[st], n)
                pe.matmul(gate[2 * st][:, 0:CW], center[:], u, start=True, stop=True).then_inc(center_done[st], 1)

            def variance(norm):
                st, n = norm
                pe.wait_ge(sq_ready[st], n + 1)
                wait_if(pe, normed[st], n)
                for i in range(4):
                    last = pe.matmul(gate[2 * st + 1][0:SW, i:i + 1], norm_sq[st][:, SW * i:SW * (i + 1)], mean[:],
                                     start=True, stop=True)
                last.then_inc(var_done[st], 1)

            def spread(norm):
                st, n = norm
                pe.wait_ge(diag_ready[st], n + 1)
                pe.matmul(gate[2 * st + 1][:, 0:CW], ones[0:SW, :], norm_diag[st][0:SW, :],
                          start=True, stop=True).then_inc(spread_done[st], 1)

            for g, (s0, k) in enumerate(groups):
                pe.wait_ge(x_loaded[g], 16)
                if g >= 2:
                    pe.wait_ge(xT_taken, g - 1)
                for s in range(s0, s0 + k):
                    last = pe.transpose(mps[g % 2][:, B * (s - s0):B * (s - s0 + 1)], x_in[:, s, :], ident[0:B, 0:B])
                last.then_inc(xT_done, 1)

            for g in range(MG):
                message(0, w0[:], None, g)

            def first_center(c):
                pe.wait_ge(u_ready[0], c + 1)
                centered(norm0(c), va[c % 2][:])

            def second_center(app, c):
                pe.wait_ge(u_ready[1], norm1(app, c)[1] + 1)
                centered(norm1(app, c), (cols(hT, c) if app == 0 else v1[:]))

            def hooks0(c):
                hooks = {}
                if c >= 2:
                    hooks.update({1: [lambda: second_center(0, c - 2)], 5: [lambda: variance(norm1(0, c - 2))],
                                  15: [lambda: spread(norm1(0, c - 2))]})
                if c >= 1:
                    hooks.update({4: [lambda: first_center(c - 1)], 9: [lambda: variance(norm0(c - 1))],
                                  17: [lambda: spread(norm0(c - 1))]})
                return hooks

            for c in range(NC):
                neighbours(0, c, hooks0(c))

            def drain(app, order, rhs, version):
                left = [NC - 2, NC - 1] if order is DRAIN0 else [NC - 1]
                seen = {}
                for part in order:
                    if part[0] == "m":
                        message(app, rhs, version, int(part[1]))
                        continue
                    c = NC - 1 if part.islower() else left[seen.get(part, 0)]
                    seen[part] = seen.get(part, 0) + 1
                    norm = norm0(c) if part.islower() else norm1(app - 1, c)
                    if part == "c":
                        first_center(c)
                    elif part == "C":
                        second_center(app - 1, c)
                    elif part in "Vv":
                        variance(norm)
                    else:
                        spread(norm)

            drain(1, DRAIN0, w("L1_gnn_W1_0"), "x1")

            def own(app, c):
                n, b = NC * (app - 1) + c, c % 2
                pe.wait_ge(e_in[b], 16 * (n // 2 + 1))
                wait_if(pe, self_free, n)
                if n == 0:
                    await_h(pe, "x1", NC - 1)
                for k in (2, 3):
                    last = pe.matmul(gate[k - 2][:, 0:CW], w(f"L1_gnn_W{k}_{app - 1}"), cols(hT, c), start=True, stop=True)
                return pe.matmul(acc[b][:, 0:CW], w(f"L1_gnn_W1_{app - 1}"), esum[b][:], start=False, stop=True)

            def hooks1(app, c, at):
                return {} if c == 0 else {at[0]: [lambda: second_center(app, c - 1)],
                                          at[1]: [lambda: variance(norm1(app, c - 1))],
                                          at[2]: [lambda: spread(norm1(app, c - 1))]}

            for c in range(NC):
                neighbours(1, c, {}, lambda: own(1, c))
            for g in range(MG):
                message(2, w("L1_gnn_W1_1"), "h1", g)
            for c in range(NC):
                neighbours(2, c, hooks1(2, c, (14, 18, 24)), lambda: own(2, c))
            drain(3, DRAIN, w("L2_gnn_W_neigh"), "x2")

            def own2(c):
                pe.wait_ge(self_free, 2 * NC + c)
                pe.matmul(gate[0][:, 0:CW], w("L2_gnn_W_self"), cols(hT, c), start=True, stop=True)

            for c in range(NC):
                neighbours(3, c, {**hooks1(3, c, (7, 12, 17)), 20: [lambda: own2(c)]})
            def step_message(t, g):
                message(4 + t, conv[:, bass.ds(128 * t, 128)], t, g)

            def enc1(c):
                await_h(pe, "x3", c)
                pe.matmul(gate[c % 2][:, 0:CW], w("L3_gnn_enc_w1"), cols(hT, c), start=True, stop=True).then_inc(enc1_done, 1)

            def enc2(c):
                pe.wait_ge(enc1_ready, c + 1)
                if c >= 2:
                    await_h(pe, "enc", c - 2)
                pe.matmul(gate[2 + c % 2][:, 0:CW], w("L3_gnn_enc_w2"), hid[c % 2][:],
                          start=True, stop=True).then_inc(enc2_done, 1)
            second_center(3, NC - 1)
            pe.wait_ge(self_free, 3 * NC)
            enc1(0)
            variance(norm1(3, NC - 1))
            enc1(1)
            spread(norm1(3, NC - 1))
            await_h(pe, "x3", NC - 1)
            for c in range(NC):
                enc2(c)
                if c + 2 < NC:
                    enc1(c + 2)
                for g in early_with[c]:
                    step_message(0, g)

            def product16(bank, block, x, start, stop):
                for i, (hw, hx) in enumerate(((0, 0), (0, 1), (1, 0))):
                    last = pe.matmul(bank[:, 0:CW], w16[:, hw, 128 * block:128 * (block + 1)], x[:, hx, :],
                                     start=(start and i == 0), stop=(stop and i == 2))
                return last

            def gates_own(t, c):
                k = NC * t + c
                pe.wait_ge(h_ready, k + WRITES["enc"] + NC)
                pe.wait_ge(own_lo, k + 1)
                for i in range(3):
                    product16(gate[(0, 1, 3)[i]], 3 + i, h16[c % 2], True, i == 2)

            def gates(t, c):
                pe.wait_ge(agg_ready, NC * t + c + 3)
                for i in range(3):
                    last = product16(gate[i], i, agg16[c % 2], i == 2, True)
                last.then_inc(gates_done, 1)
            pe.wait_ge(w_split, 4)

            def step(t, last):
                for g in LATE:
                    step_message(t, g)
                for c in range(NC):
                    neighbours(4 + t, c, {3: [lambda: gates_own(t, c - 1)], 6: [lambda: gates(t, c - 1)]} if c else {})
                if last:
                    dec1(0)
                    dec1(1)
                else:
                    for g in EARLY[:2]:
                        step_message(t + 1, g)
                gates_own(t, NC - 1)
                gates(t, NC - 1)
                if not last:
                    for g in EARLY[2:]:
                        step_message(t + 1, g)

            def dec1(c):
                pe.wait_ge(relu_ready, c + 1)
                pe.matmul(mps[c % 2][:, 0:CW], w("L3_gnn_dec_w1"), cols(hT, c), start=True, stop=True).then_inc(dec1_done, 1)

            def dec2(c):
                pe.wait_ge(dec1_ready, c + 1)
                wait_if(pe, sig_ready, c - 1)
                pe.matmul(acc[c % 2][:, 0:CW], w("L3_gnn_dec_w2"), hid[c % 2][:],
                          start=True, stop=True).then_inc(dec2_done, 1)

            with pe.Fori(0, STEPS - 1) as t:
                step(t, False)
            step(STEPS - 1, True)

            def last_center(c):
                await_h(pe, "dec", c)
                centered(norm_last(c), cols(hT, c))

            for c in range(NC):
                dec2(c)
                if c + 2 < NC:
                    dec1(c + 2)
                if c >= NC - 3 and c < NC - 1:
                    last_center(c - NC + 3)

            def turn(c):
                for g in turned_with[c]:
                    s0, k = groups[g]
                    for cc in (c - 1, c):
                        st, n = norm_last(cc)
                        pe.wait_ge(normed[st], n + 1)
                    if g >= 2:
                        pe.wait_ge(out_taken, g - 1)
                    for s in range(s0, s0 + k):
                        last = pe.transpose(mps[g % 2][0:B, 128 * (s - s0):128 * (s - s0 + 1)],
                                            hT[:, B * s:B * (s + 1)], ident[:])
                    last.then_inc(outT_done, 1)
            for c in range(NC):
                if 0 < c < NC - 1:
                    last_center(c + 1)
                variance(norm_last(c))
                if c >= 1:
                    spread(norm_last(c - 1))
                if c >= 2:
                    turn(c - 2)
            spread(norm_last(NC - 1))
            turn(NC - 2)
            turn(NC - 1)

        @block.scalar
        def _(act):
            def hi(app, g):
                s0, k = groups[g]
                act.wait_ge(m_done, MG * app + g + 1)
                act.activation(msg[:, s0:s0 + k, 0, :], mbank[g][0:B, 0:128 * k].rearrange("p (s f) -> p s f", s=k),
                               ACT.Copy).then_inc(hi_ready, 1)

            def square(norm):
                st, n = norm
                act.wait_ge(center_done[st], n + 1)
                wait_if(act, var_done[st], n)
                act.activation(norm_sq[st][:], gate[2 * st][:, 0:CW], ACT.Square).then_inc(sq_ready[st], 1)

            def deviation(norm):
                st, n = norm
                act.wait_ge(var_done[st], n + 1)
                wait_if(act, rstd_ready[st], n)
                act.activation(small[:, st, 0, :], gate[2 * st + 1][0:SW, 0:4], ACT.Sqrt,
                               bias=epsc[0:SW, 0:1]).then_inc(std_ready[st], 1)

            def keep(norm):
                st, n = norm
                wait_if(act, normed[st], n)
                act.activation(norm_dev[st][:], gate[2 * st][:, 0:CW], ACT.Copy).then_inc(dev_ready[st], 1)

            for g, (s0, k) in enumerate(groups):
                act.wait_ge(xT_done, g + 1)
                act.activation(hT[:, B * s0:B * (s0 + k)], mps[g % 2][:, 0:B * k], ACT.Copy).then_inc(xT_taken, 1)

            for g in range(MG):
                hi(0, g)

            def gelu(c):
                act.wait_ge(normed[0], c + 1)
                act.activation(va[c % 2][:], va[c % 2][:], ACT.Gelu, bias=col("L0_gnn_beta"),
                               scale=col("L0_gnn_gamma")).then_inc(act_ready, 1)

            act.wait_ge(w_split, 4)
            for c in range(1, NC):
                norms = ([norm1(0, c - 2)] if c >= 2 else []) + [norm0(c - 1)]
                for part in (square, deviation, keep):
                    for norm in norms:
                        part(norm)
                gelu(c - 1)

            def drain(app, order):
                left = [NC - 2, NC - 1] if order is DRAIN0 else [NC - 1]
                seen = {}
                for part in order:
                    if part[0] == "m":
                        hi(app, int(part[1]))
                        continue
                    c = NC - 1 if part.islower() else left[seen.get(part, 0)]
                    seen[part] = seen.get(part, 0) + 1
                    norm = norm0(c) if part.islower() else norm1(app - 1, c)
                    if part in "Cc":
                        square(norm)
                    elif part in "Vv":
                        deviation(norm)
                        keep(norm)
                    elif part == "s":
                        gelu(c)
            drain(1, DRAIN0)
            for g in range(MG):
                hi(2, g)

            def norm_chunk(norm):
                square(norm)
                deviation(norm)
                keep(norm)
            for c in range(NC - 1):
                norm_chunk(norm1(2, c))
            drain(3, DRAIN)
            for c in range(NC):
                norm_chunk(norm1(3, c))

            def enc_in(c):
                act.wait_ge(enc1_done, c + 1)
                wait_if(act, enc2_done, c - 1)
                act.activation(hid[c % 2][:], gate[c % 2][:, 0:CW], ACT.Relu,
                               bias=col("L3_gnn_enc_b1")).then_inc(enc1_ready, 1)
            await_h(act, "x3", NC - 1)
            enc_in(0)
            for c in range(NC):
                if c + 1 < NC:
                    enc_in(c + 1)
                act.wait_ge(enc2_done, c + 1)
                act.wait_ge(x3_out[c], 16)
                act.activation(cols(hT, c), gate[2 + c % 2][:, 0:CW], ACT.Identity,
                               bias=col("L3_gnn_enc_b2")).then_inc(h_ready, 1)
                for g in early_with[c]:
                    hi(4, g)

            def take(t, c):
                act.wait_ge(acc_done, NC * (4 + t) + c + 1)
                act.wait_ge(h_ready, NC * t + c + WRITES["enc"] + NC - 1)
                act.activation(agg16[c % 2][:, 0, :], acc[c % 2][:, 0:CW], ACT.Copy).then_inc(agg_hi, 1)

            def split_own(t, c):
                act.wait_ge(h_ready, NC * t + c + WRITES["enc"] + NC - 1)
                act.activation(h16[c % 2][:, 0, :], cols(hT, c), ACT.Copy).then_inc(own_hi, 1)

            def gated(t, c, between=lambda: None):
                k = NC * t + c
                act.wait_ge(gates_done, k + 1)
                act.wait_ge(h_ready, k + WRITES["enc"] + NC)
                act.activation(gr[:], gate[0][:, 0:CW], ACT.Sigmoid, bias=gbias[:, 0:1]).then_inc(r_ready, 1)
                act.activation(gz[:], gate[1][:, 0:CW], ACT.Sigmoid, bias=gbias[:, 1:2]).then_inc(z_ready, 1)
                between()
                act.wait_ge(inner2, k + 1)
                act.activation(gn[:], gt[:], ACT.Tanh, bias=col("L3_gnn_gru_bih", 2)).then_inc(n_ready, 1)

            def dec_in(c):
                act.wait_ge(dec1_done, c + 1)
                wait_if(act, dec2_done, c - 1)
                act.activation(hid[c % 2][:], mps[c % 2][:, 0:CW], ACT.Relu,
                               bias=col("L3_gnn_dec_b1")).then_inc(dec1_ready, 1)

            def step(t, last):
                for g in LATE:
                    hi(4 + t, g)
                for c in range(NC - 1):
                    split_own(t, c)
                    take(t, c)
                    gated(t, c)
                split_own(t, NC - 1)
                take(t, NC - 1)
                if last:
                    dec_in(0)
                    dec_in(1)
                    gated(t, NC - 1)
                else:
                    for g in EARLY[:2]:
                        hi(5 + t, g)
                    gated(t, NC - 1, lambda: hi(5 + t, EARLY[2]))
                    for g in EARLY[3:]:
                        hi(5 + t, g)

            with act.Fori(0, STEPS - 1) as t:
                step(t, False)
            step(STEPS - 1, True)

            for c in range(NC):
                act.wait_ge(dec2_done, c + 1)
                if c >= 4:
                    await_h(act, "dec", c - 4)
                act.activation(sigm[c % 4][:], acc[c % 2][:, 0:CW], ACT.Sigmoid,
                               bias=col("L3_gnn_dec_b2")).then_inc(sig_ready, 1)
                if c + 2 < NC:
                    dec_in(c + 2)
                else:
                    square(norm_last(c - NC + 2))

            for c in range(NC):
                norm = norm_last(c)
                if c >= 2:
                    square(norm)
                deviation(norm)
                if c == 0:
                    await_h(act, "dec", NC - 1)
                keep(norm)

        @block.gpsimd
        def _(pool):
            pool.tensor_copy(w_parts[0], w32).then_inc(w_split, 1)
            pool.wait_ge(w_split, 1)
            pool.tensor_tensor(w_parts[1], w32, w_parts[0], ALU.subtract).then_inc(w_split, 1)
            pool.wait_ge(w_split, 2)
            for h in range(2):
                pool.tensor_copy(w16[:, h, :], w_parts[h]).then_inc(w_split, 1)

        @block.vector
        def _(dve):
            def lo(app, g):
                s0, k = groups[g]
                dve.wait_ge(hi_ready, MG * app + g + 1)
                dve.tensor_tensor(msg[:, s0:s0 + k, 1, :], mbank[g][0:B, 0:128 * k].rearrange("p (s f) -> p s f", s=k),
                                  msg[:, s0:s0 + k, 0, :], ALU.subtract).then_inc(lo_ready, 1)

            def scale_by_degree(app, c, to):
                n = NC * app + c
                dve.wait_ge(rd_in[c % 2], 16 * (n // 2 + 1))
                dve.wait_ge(acc_done, n + 1)
                dve.tensor_tensor(to, acc[c % 2][:, 0:CW], rd[c % 2][:], ALU.mult).then_inc(scaled, 1)
                dve.wait_ge(scaled, n + 1)

            def diagonal(norm):
                st, n = norm
                dve.wait_ge(std_ready[st], n + 1)
                wait_if(dve, diag_ready[st], n)
                wait_if(dve, spread_done[st], n)
                dve.reciprocal(small[:, st, 1, :], small[:, st, 0, :]).then_inc(rstd_ready[st], 1)
                dve.wait_ge(rstd_ready[st], n + 1)
                dve.tensor_tensor(norm_diag[st][0:SW, :].rearrange("p (i d) -> p i d", i=4),
                                  ident[0:SW, 0:SW].unsqueeze(1).to_broadcast([SW, 4, SW]),
                                  small[:, st, 1, :].unsqueeze(2).to_broadcast([SW, 4, SW]),
                                  ALU.mult).then_inc(diag_ready[st], 1)

            def normalised(norm, to):
                st, n = norm
                dve.wait_ge(dev_ready[st], n + 1)
                dve.wait_ge(spread_done[st], n + 1)
                dve.tensor_tensor(to, gate[2 * st + 1][:, 0:CW], norm_dev[st][:], ALU.mult).then_inc(normed[st], 1)

            dve.memset(hT[:, N:NPAD], 0.0).then_inc(pad_zero, 1)
            dve.wait_ge(degs_in, 16)
            dve.tensor_scalar(dg[:, 1, :], dg[:, 0, :], 1.0, None, ALU.max).then_inc(rdeg_step, 1)
            dve.wait_ge(rdeg_step, 1)
            dve.reciprocal(dg[:, 2, :], dg[:, 1, :]).then_inc(rdeg_step, 1)
            dve.wait_ge(rdeg_step, 2)
            dve.scalar_tensor_tensor(out=dg[:, 0, :], in0=dg[:, 0, :], scalar=0.0, in1=dg[:, 2, :],
                                     op0=ALU.is_gt, op1=ALU.mult).then_inc(rdeg_step, 1)
            for g in range(MG):
                lo(0, g)
            dve.wait_ge(w_split, 4)

            def before0(c):
                scale_by_degree(0, c, va[c % 2][:])
                dve.scalar_tensor_tensor(out=va[c % 2][:], in0=va[c % 2][:], scalar=col("L0_gnn_b"), in1=cols(hT, c),
                                         op0=ALU.add, op1=ALU.add).then_inc(u_ready[0], 1)
                dve.sem_inc(acc_free, 1)

            def residual0(c):
                dve.wait_ge(act_ready, c + 1)
                dve.tensor_tensor(cols(hT, c), va[c % 2][:], cols(hT, c), ALU.add).then_inc(u_ready[1], 1)

            for c in range(1, NC):
                before0(c - 1)
                if c >= 2:
                    diagonal(norm1(0, c - 2))
                diagonal(norm0(c - 1))
                if c >= 2:
                    normalised(norm1(0, c - 2), cols(hT, c - 2))
                normalised(norm0(c - 1), va[(c - 1) % 2][:])
                residual0(c - 1)

            def drain(app, order):
                left = [NC - 2, NC - 1] if order is DRAIN0 else [NC - 1]
                seen = {}
                for part in order:
                    if part[0] == "m":
                        lo(app, int(part[1]))
                        continue
                    c = NC - 1 if part.islower() else left[seen.get(part, 0)]
                    seen[part] = seen.get(part, 0) + 1
                    norm = norm0(c) if part.islower() else norm1(app - 1, c)
                    if part in "Vv":
                        diagonal(norm)
                    elif part == "S":
                        normalised(norm, cols(hT, c))
                    elif part == "s":
                        normalised(norm, va[c % 2][:])
                        residual0(c)
            before0(NC - 1)
            drain(1, DRAIN0)

            def chunk1(app, c, between=lambda g: None):
                k = NC * (app - 1) + c
                if app == 2 and c:
                    dve.wait_ge(normed[1], norm1(2, c)[1])
                scale_by_degree(app, c, v1[:])
                r = rd[c % 2][:]
                dve.scalar_tensor_tensor(out=v2[:], in0=r, scalar=0.0, in1=gate[0][:, 0:CW],
                                         op0=ALU.is_gt, op1=ALU.mult).then_inc(mixed, 1)
                dve.scalar_tensor_tensor(out=r, in0=r, scalar=0.0, in1=gate[1][:, 0:CW],
                                         op0=ALU.is_equal, op1=ALU.mult).then_inc(self_free, 1)
                between(0)
                dve.wait_ge(mixed, k + 1)
                dve.tensor_tensor(v1[:], v1[:], v2[:], ALU.add).then_inc(mixed2, 1)
                between(1)
                dve.wait_ge(self_free, k + 1)
                dve.wait_ge(mixed2, k + 1)
                dve.tensor_tensor(v1[:], v1[:], r, ALU.add).then_inc(summed, 1)
                dve.wait_ge(summed, k + 1)
                dve.sem_inc(acc_free, 1)
                if app == 1:
                    if c == 0:
                        dve.wait_ge(x1_out, 16 * NC)
                    dve.scalar_tensor_tensor(out=cols(hT, c), in0=v1[:], scalar=LEAK, in1=v1[:],
                                             op0=ALU.mult, op1=ALU.max).then_inc(h_ready, 1)
                    dve.wait_ge(h_ready, WRITES["h1"] + c + 1)
                else:
                    dve.scalar_tensor_tensor(out=v2[:], in0=v1[:], scalar=LEAK, in1=v1[:],
                                             op0=ALU.mult, op1=ALU.max).then_inc(leaked, 1)
                    dve.wait_ge(leaked, c + 1)
                    dve.wait_ge(res_in, 16 * (c + 1))
                    dve.tensor_tensor(v1[:], v2[:], res[:], ALU.add).then_inc(u_ready[1], 1)

            for c in range(NC - 1):
                chunk1(1, c)
            chunk1(1, NC - 1, lambda g: lo(2, g))
            for g in range(2, MG):
                lo(2, g)
            for c in range(NC - 1):
                chunk1(2, c)
                diagonal(norm1(2, c))
                normalised(norm1(2, c), cols(hT, c))
            chunk1(2, NC - 1, lambda g: lo(3, g))
            drain(3, DRAIN[2:])

            for c in range(NC):
                dve.wait_ge(normed[1], norm1(3, c)[1])
                scale_by_degree(3, c, v1[:])
                dve.scalar_tensor_tensor(out=v2[:], in0=gate[0][:, 0:CW], scalar=col("L2_gnn_b_self"), in1=v1[:],
                                         op0=ALU.add, op1=ALU.add).then_inc(self_free, 1)
                dve.wait_ge(self_free, 2 * NC + c + 1)
                dve.sem_inc(acc_free, 1)
                dve.tensor_tensor(v1[:], v2[:], cols(hT, c), ALU.add).then_inc(u_ready[1], 1)
                diagonal(norm1(3, c))
                normalised(norm1(3, c), cols(hT, c))

            def gated(t, c, between=lambda: None):
                k = NC * t + c
                dve.wait_ge(r_ready, k + 1)
                dve.scalar_tensor_tensor(out=gt[:], in0=gate[3][:, 0:CW], scalar=col("L3_gnn_gru_bhh", 2), in1=gr[:],
                                         op0=ALU.add, op1=ALU.mult).then_inc(inner1, 1)
                dve.wait_ge(inner1, k + 1)
                dve.tensor_tensor(gt[:], gt[:], gate[2][:, 0:CW], ALU.add).then_inc(inner2, 1)
                between()
                dve.wait_ge(n_ready, k + 1)
                dve.tensor_tensor(gr[:], cols(hT, c), gn[:], ALU.subtract).then_inc(diff1, 1)
                dve.wait_ge(diff1, k + 1)
                dve.wait_ge(z_ready, k + 1)
                dve.tensor_tensor(gr[:], gr[:], gz[:], ALU.mult).then_inc(diff2, 1)
                dve.wait_ge(diff2, k + 1)
                dve.tensor_tensor(cols(hT, c), gr[:], gn[:], ALU.add).then_inc(h_ready, 1)

            def low_parts(t, c):
                k = NC * t + c
                dve.wait_ge(own_hi, k + 1)
                dve.tensor_tensor(h16[c % 2][:, 1, :], cols(hT, c), h16[c % 2][:, 0, :], ALU.subtract).then_inc(own_lo, 1)
                dve.wait_ge(agg_hi, k + 1)
                dve.tensor_tensor(agg16[c % 2][:, 1, :], acc[c % 2][:, 0:CW], agg16[c % 2][:, 0, :],
                                  ALU.subtract).then_inc(agg_ready, 1)

            dve.sem_inc(agg_ready, 2)
            for g in EARLY:
                lo(4, g)

            def relu(c):
                await_h(dve, STEPS, c)
                dve.tensor_scalar(cols(hT, c), cols(hT, c), 0.0, None, ALU.max).then_inc(relu_ready, 1)

            def step(t, last):
                for g in LATE:
                    lo(4 + t, g)
                for c in range(NC - 1):
                    low_parts(t, c)
                    gated(t, c)
                    if last:
                        relu(c)
                low_parts(t, NC - 1)
                if last:
                    gated(t, NC - 1)
                    relu(NC - 1)
                else:
                    for g in EARLY[:2]:
                        lo(5 + t, g)
                    gated(t, NC - 1, lambda: lo(5 + t, EARLY[2]))
                    for g in EARLY[3:]:
                        lo(5 + t, g)

            with dve.Fori(0, STEPS - 1) as t:
                step(t, False)
            step(STEPS - 1, True)

            for c in range(NC):
                dve.wait_ge(sig_ready, c + 1)
                dve.wait_ge(res3_in[c], 16)
                dve.tensor_tensor(cols(hT, c), sigm[c % 4][:], cols(x3_all, c), ALU.add).then_inc(h_ready, 1)

            def take_rows(c):
                for g in turned_with[c]:
                    s0, k = groups[g]
                    dve.wait_ge(outT_done, g + 1)
                    dve.tensor_copy(x_in[:, s0:s0 + k, :], mps[g % 2][0:B, 0:128 * k]
                                    .rearrange("p (s f) -> p s f", s=k)).then_inc(out_taken, 1)
            await_h(dve, "dec", NC - 1)
            for c in range(NC):
                diagonal(norm_last(c))
                if c >= 1:
                    normalised(norm_last(c - 1), cols(hT, c - 1))
                if c >= 2:
                    take_rows(c - 2)
            normalised(norm_last(NC - 1), cols(hT, NC - 1))
            take_rows(NC - 2)
            take_rows(NC - 1)


_INS = ["x", "src", "dst", "edge_attr_128", "L0_gnn_W", "L0_gnn_b", "L0_gnn_gamma", "L0_gnn_beta",
        "L1_gnn_W1_0", "L1_gnn_W2_0", "L1_gnn_W3_0", "L1_gnn_W1_1", "L1_gnn_W2_1", "L1_gnn_W3_1",
        "L2_gnn_W_neigh", "L2_gnn_W_self", "L2_gnn_b_self", "L3_gnn_enc_w1", "L3_gnn_enc_b1", "L3_gnn_enc_w2",
        "L3_gnn_enc_b2", "L3_gnn_conv_w", "L3_gnn_gru_wih", "L3_gnn_gru_whh", "L3_gnn_gru_bih", "L3_gnn_gru_bhh",
        "L3_gnn_dec_w1", "L3_gnn_dec_b1", "L3_gnn_dec_w2", "L3_gnn_dec_b2"]


def kernel(**inputs):
    import numpy as _np
    import concourse.bacc as _bacc
    from concourse import mybir as _mybir
    from concourse.bass_utils import run_bass_kernel_spmd as _run

    nc = _bacc.Bacc("TRN2", target_bir_lowering=False, num_devices=1)
    arrays, ins = {}, {}
    for name in _INS:
        arr = _np.ascontiguousarray(inputs[name])
        arrays[f"in_{name}_dram"] = arr
        ins[name] = nc.dram_tensor(f"in_{name}_dram", arr.shape, _mybir.dt.from_np(arr.dtype), kind="ExternalInput").ap()
    out = nc.dram_tensor("out_0_dram", (N, D), _mybir.dt.float32, kind="ExternalOutput").ap()
    gnn_kernel(nc, ins, out)
    r = _run(nc, [arrays], core_ids=[0])
    return r.results[0]["out_0_dram"]
```
